# Optimizing a Trainium2 kernel written in Bass

```python
import numpy as np
import jax
import jax.numpy as jnp

def _softmax(x, axis=-1):
    return jax.nn.softmax(x, axis=axis)

def _gelu(x):
    return jax.nn.gelu(x, approximate=True)

def _silu(x):
    return jax.nn.silu(x)

def _sigmoid(x):
    return jax.nn.sigmoid(x)

def _layernorm(x, axis=-1, eps=1e-05):
    m = jnp.mean(x, axis=axis, keepdims=True)
    v = jnp.var(x, axis=axis, keepdims=True)
    return (x - m) / jnp.sqrt(v + eps)

def _scatter_add(tgt, idx, src, axis=0):
    return tgt.at[idx].add(src)

def _segment_sum(src, seg, n):
    return jax.ops.segment_sum(src, seg, n)
kernel_name = 'mk_conv_seq_d4_conv_nhwc384_r4_5c7c70'

def setup_inputs(seed: int=0):
    np.random.seed(seed)
    _w = jnp.asarray

    def _rec_inputs():
        import jax
        import jax.numpy as jnp
        _gk = jax.random.key(seed)
        x = -0.0004039 + 1 * jax.random.normal(jax.random.fold_in(_gk, 1), (8, 16, 16, 96), jnp.float32)
        return x
    x = _rec_inputs()

    def _L0_conv_setup():
        import jax, jax.numpy as jnp
        import numpy as np
        DIM = 96
        H = 16
        W = 16
        NB = 8
        BS = DIM // NB
        WF = W // 2 + 1
        EPS = 1e-05

        def _layernorm(x, g, b):
            mu = jnp.mean(x, axis=-1, keepdims=True)
            var = jnp.mean(jnp.square(x - mu), axis=-1, keepdims=True)
            return (x - mu) * jax.lax.rsqrt(var + EPS) * g + b
        key = jax.random.key(seed)
        ks = jax.random.split(key, 8)
        scale = 0.02
        x = jax.random.normal(ks[0], (8, H, W, DIM), dtype=jnp.float32)
        w1 = scale * jax.random.normal(ks[1], (H, WF, NB, BS, BS, 2), dtype=jnp.float32)
        b1 = scale * jax.random.normal(ks[2], (H, WF, NB, BS, 2), dtype=jnp.float32)
        norm1_w = jnp.ones((DIM,), jnp.float32)
        norm1_b = jnp.zeros((DIM,), jnp.float32)
        norm2_w = jnp.ones((DIM,), jnp.float32)
        norm2_b = jnp.zeros((DIM,), jnp.float32)
        lim1 = 1.0 / np.sqrt(DIM)
        lim2 = 1.0 / np.sqrt(4 * DIM)
        mlp_w1 = jax.random.uniform(ks[3], (DIM, 4 * DIM), jnp.float32, -lim1, lim1)
        mlp_b1 = jax.random.uniform(ks[4], (4 * DIM,), jnp.float32, -lim1, lim1)
        mlp_w2 = jax.random.uniform(ks[5], (4 * DIM, DIM), jnp.float32, -lim2, lim2)
        mlp_b2 = jax.random.uniform(ks[6], (DIM,), jnp.float32, -lim2, lim2)
        return {'x': x, 'w1': w1, 'b1': b1, 'norm1_w': norm1_w, 'norm1_b': norm1_b, 'norm2_w': norm2_w, 'norm2_b': norm2_b, 'mlp_w1': mlp_w1, 'mlp_b1': mlp_b1, 'mlp_w2': mlp_w2, 'mlp_b2': mlp_b2}
    _L0_conv_all = _L0_conv_setup()
    _L0_conv_in = {k: v for k, v in _L0_conv_all.items() if k in ('w1', 'b1', 'norm1_w', 'norm1_b', 'norm2_w', 'norm2_b', 'mlp_w1', 'mlp_b1', 'mlp_w2', 'mlp_b2')}
    del _L0_conv_all

    def _L1_conv_setup():
        import jax, jax.numpy as jnp
        import numpy as np
        B, HH, WW, E = (8, 16, 16, 96)
        NH, EXP = (6, 2)
        D1 = EXP * E // NH * NH
        HD = D1 // NH
        RPE = 128
        LAYERS = 3
        EPS = 1e-06

        def srms(x):
            return x * jax.lax.rsqrt(jnp.mean(x * x, axis=-1, keepdims=True) + EPS)

        def rpe_forward(pos, pw, pb, lw, lb, ow, ob):
            x = jax.nn.relu(pos @ pw + pb)
            for i in range(lw.shape[0]):
                x = jax.nn.relu(srms(x)) @ lw[i] + lb[i]
            return jax.nn.relu(srms(x)) @ ow + ob

        def tno_coeffs(n, pw, pb, lw, lb, ow, ob):
            pos = jnp.arange(1, n, dtype=jnp.float32)[:, None]
            neg = -jnp.arange(1, n, dtype=jnp.float32)[::-1][:, None]
            zero = jnp.zeros((1, 1), dtype=jnp.float32)
            t_zero = rpe_forward(zero, pw, pb, lw, lb, ow, ob)
            t_pos = rpe_forward(pos, pw, pb, lw, lb, ow, ob)
            t_neg = rpe_forward(neg, pw, pb, lw, lb, ow, ob)
            a = jnp.concatenate([t_zero, t_pos, t_zero, t_neg], axis=0)
            return a.reshape(2 * n, NH, HD).transpose(1, 0, 2)

        def tno_apply(v, a, axis):
            n = v.shape[axis]
            a = a[:, :, None, :] if axis == -3 else a[:, None, :, :]
            y = jnp.fft.rfft(v, 2 * n, axis=axis)
            af = jnp.fft.rfft(a, 2 * n, axis=axis)
            out = jnp.fft.irfft(af * y, 2 * n, axis=axis)
            return jax.lax.slice_in_dim(out, 0, n, axis=out.ndim + axis)
        key = jax.random.key(seed)
        ks = jax.random.split(key, 24)
        s = 0.02

        def rn(k, shape):
            return jax.random.normal(k, shape, dtype=jnp.float32) * s
        inp = {'x': jax.random.normal(ks[0], (B, HH, WW, E), dtype=jnp.float32), 'H': HH, 'W': WW, 'Wu': rn(ks[1], (E, D1)), 'bu': jnp.zeros((D1,), jnp.float32), 'Wv': rn(ks[2], (E, D1)), 'bv': jnp.zeros((D1,), jnp.float32), 'Wo': rn(ks[3], (D1, E)), 'bo': jnp.zeros((E,), jnp.float32)}
        for t, off in (('r1', 4), ('r2', 10)):
            inp[t + '_pw'] = rn(ks[off], (1, RPE))
            inp[t + '_pb'] = jnp.zeros((RPE,), jnp.float32)
            inp[t + '_lw'] = rn(ks[off + 1], (LAYERS, RPE, RPE))
            inp[t + '_lb'] = jnp.zeros((LAYERS, RPE), jnp.float32)
            inp[t + '_ow'] = rn(ks[off + 2], (RPE, NH * HD))
            inp[t + '_ob'] = jnp.zeros((NH * HD,), jnp.float32)
        return inp
    _L1_conv_all = _L1_conv_setup()
    _L1_conv_in = {k: v for k, v in _L1_conv_all.items() if k in ('Wu', 'bu', 'Wv', 'bv', 'Wo', 'bo', 'r1_pw', 'r1_pb', 'r1_lw', 'r1_lb', 'r1_ow', 'r1_ob', 'r2_pw', 'r2_pb', 'r2_lw', 'r2_lb', 'r2_ow', 'r2_ob')}
    del _L1_conv_all

    def _L2_conv_setup():
        import jax, jax.numpy as jnp
        import numpy as np

        def _layernorm(x, g, b, eps=1e-05):
            m = x.mean(-1, keepdims=True)
            v = jnp.mean((x - m) ** 2, axis=-1, keepdims=True)
            return (x - m) / jnp.sqrt(v + eps) * g + b

        def _gru_dir(x, wih, whh, bih, bhh, reverse):
            if reverse:
                x = jnp.flip(x, 1)
            gx = jnp.einsum('blc,gc->blg', x, wih) + bih
            h = whh.shape[1]
            h0 = jnp.zeros((x.shape[0], h), x.dtype)

            def step(hprev, gxt):
                gh = hprev @ whh.T + bhh
                r = jax.nn.sigmoid(gxt[:, :h] + gh[:, :h])
                z = jax.nn.sigmoid(gxt[:, h:2 * h] + gh[:, h:2 * h])
                n = jnp.tanh(gxt[:, 2 * h:] + r * gh[:, 2 * h:])
                hn = (1.0 - z) * n + z * hprev
                return (hn, hn)
            _, ys = jax.lax.scan(step, h0, jnp.swapaxes(gx, 0, 1))
            out = jnp.swapaxes(ys, 0, 1)
            return jnp.flip(out, 1) if reverse else out

        def _bigru(x, wih_fw, whh_fw, bih_fw, bhh_fw, wih_rv, whh_rv, bih_rv, bhh_rv):
            return jnp.concatenate([_gru_dir(x, wih_fw, whh_fw, bih_fw, bhh_fw, False), _gru_dir(x, wih_rv, whh_rv, bih_rv, bhh_rv, True)], axis=-1)
        key = jax.random.key(seed)
        ks = jax.random.split(key, 16)
        B, H, W, C = (16, 48, 48, 96)
        d_inner = 2 * C
        hid = d_inner // 2
        s = 0.05
        inp = {'x': jax.random.normal(ks[0], (B, H, W, C), jnp.float32), 'ln_g': jnp.ones((C,), jnp.float32), 'ln_b': jnp.zeros((C,), jnp.float32), 'w_in': jax.random.normal(ks[1], (2 * d_inner, C), jnp.float32) * s, 'w_out': jax.random.normal(ks[2], (C, d_inner), jnp.float32) * s}
        i = 3
        for ssm in ('f', 'b'):
            for d in ('fw', 'rv'):
                inp[f'{ssm}_wih_{d}'] = jax.random.normal(ks[i], (3 * hid, d_inner), jnp.float32) * s
                i += 1
                inp[f'{ssm}_whh_{d}'] = jax.random.normal(ks[i], (3 * hid, hid), jnp.float32) * s
                i += 1
                inp[f'{ssm}_bih_{d}'] = jnp.zeros((3 * hid,), jnp.float32)
                inp[f'{ssm}_bhh_{d}'] = jnp.zeros((3 * hid,), jnp.float32)
        return inp
    _L2_conv_all = _L2_conv_setup()
    _L2_conv_in = {k: v for k, v in _L2_conv_all.items() if k in ('ln_g', 'ln_b', 'w_in', 'w_out', 'f_wih_fw', 'f_whh_fw', 'f_bih_fw', 'f_bhh_fw', 'f_wih_rv', 'f_whh_rv', 'f_bih_rv', 'f_bhh_rv', 'b_wih_fw', 'b_whh_fw', 'b_bih_fw', 'b_bhh_fw', 'b_wih_rv', 'b_whh_rv', 'b_bih_rv', 'b_bhh_rv')}
    del _L2_conv_all

    def _L3_conv_setup():
        import jax, jax.numpy as jnp
        import numpy as np

        def _layernorm(x, g, b, eps=1e-05):
            m = x.mean(-1, keepdims=True)
            v = jnp.mean((x - m) ** 2, axis=-1, keepdims=True)
            return (x - m) / jnp.sqrt(v + eps) * g + b

        def _gru_dir(x, wih, whh, bih, bhh, reverse):
            if reverse:
                x = jnp.flip(x, 1)
            gx = jnp.einsum('blc,gc->blg', x, wih) + bih
            h = whh.shape[1]
            h0 = jnp.zeros((x.shape[0], h), x.dtype)

            def step(hprev, gxt):
                gh = hprev @ whh.T + bhh
                r = jax.nn.sigmoid(gxt[:, :h] + gh[:, :h])
                z = jax.nn.sigmoid(gxt[:, h:2 * h] + gh[:, h:2 * h])
                n = jnp.tanh(gxt[:, 2 * h:] + r * gh[:, 2 * h:])
                hn = (1.0 - z) * n + z * hprev
                return (hn, hn)
            _, ys = jax.lax.scan(step, h0, jnp.swapaxes(gx, 0, 1))
            out = jnp.swapaxes(ys, 0, 1)
            return jnp.flip(out, 1) if reverse else out

        def _bigru(x, wih_fw, whh_fw, bih_fw, bhh_fw, wih_rv, whh_rv, bih_rv, bhh_rv):
            return jnp.concatenate([_gru_dir(x, wih_fw, whh_fw, bih_fw, bhh_fw, False), _gru_dir(x, wih_rv, whh_rv, bih_rv, bhh_rv, True)], axis=-1)
        key = jax.random.key(seed)
        ks = jax.random.split(key, 16)
        B, H, W, C = (16, 48, 48, 96)
        d_inner = 2 * C
        hid = d_inner // 2
        s = 0.05
        inp = {'x': jax.random.normal(ks[0], (B, H, W, C), jnp.float32), 'ln_g': jnp.ones((C,), jnp.float32), 'ln_b': jnp.zeros((C,), jnp.float32), 'w_in': jax.random.normal(ks[1], (2 * d_inner, C), jnp.float32) * s, 'w_out': jax.random.normal(ks[2], (C, d_inner), jnp.float32) * s}
        i = 3
        for ssm in ('f', 'b'):
            for d in ('fw', 'rv'):
                inp[f'{ssm}_wih_{d}'] = jax.random.normal(ks[i], (3 * hid, d_inner), jnp.float32) * s
                i += 1
                inp[f'{ssm}_whh_{d}'] = jax.random.normal(ks[i], (3 * hid, hid), jnp.float32) * s
                i += 1
                inp[f'{ssm}_bih_{d}'] = jnp.zeros((3 * hid,), jnp.float32)
                inp[f'{ssm}_bhh_{d}'] = jnp.zeros((3 * hid,), jnp.float32)
        return inp
    _L3_conv_all = _L3_conv_setup()
    _L3_conv_in = {k: v for k, v in _L3_conv_all.items() if k in ('ln_g', 'ln_b', 'w_in', 'w_out', 'f_wih_fw', 'f_whh_fw', 'f_bih_fw', 'f_bhh_fw', 'f_wih_rv', 'f_whh_rv', 'f_bih_rv', 'f_bhh_rv', 'b_wih_fw', 'b_whh_fw', 'b_bih_fw', 'b_bhh_fw', 'b_wih_rv', 'b_whh_rv', 'b_bih_rv', 'b_bhh_rv')}
    del _L3_conv_all
    return {'x': x, 'L0_conv_w1': _L0_conv_in['w1'], 'L0_conv_b1': _L0_conv_in['b1'], 'L0_conv_norm1_w': _L0_conv_in['norm1_w'], 'L0_conv_norm1_b': _L0_conv_in['norm1_b'], 'L0_conv_norm2_w': _L0_conv_in['norm2_w'], 'L0_conv_norm2_b': _L0_conv_in['norm2_b'], 'L0_conv_mlp_w1': _L0_conv_in['mlp_w1'], 'L0_conv_mlp_b1': _L0_conv_in['mlp_b1'], 'L0_conv_mlp_w2': _L0_conv_in['mlp_w2'], 'L0_conv_mlp_b2': _L0_conv_in['mlp_b2'], 'L1_conv_Wu': _L1_conv_in['Wu'], 'L1_conv_bu': _L1_conv_in['bu'], 'L1_conv_Wv': _L1_conv_in['Wv'], 'L1_conv_bv': _L1_conv_in['bv'], 'L1_conv_Wo': _L1_conv_in['Wo'], 'L1_conv_bo': _L1_conv_in['bo'], 'L1_conv_r1_pw': _L1_conv_in['r1_pw'], 'L1_conv_r1_pb': _L1_conv_in['r1_pb'], 'L1_conv_r1_lw': _L1_conv_in['r1_lw'], 'L1_conv_r1_lb': _L1_conv_in['r1_lb'], 'L1_conv_r1_ow': _L1_conv_in['r1_ow'], 'L1_conv_r1_ob': _L1_conv_in['r1_ob'], 'L1_conv_r2_pw': _L1_conv_in['r2_pw'], 'L1_conv_r2_pb': _L1_conv_in['r2_pb'], 'L1_conv_r2_lw': _L1_conv_in['r2_lw'], 'L1_conv_r2_lb': _L1_conv_in['r2_lb'], 'L1_conv_r2_ow': _L1_conv_in['r2_ow'], 'L1_conv_r2_ob': _L1_conv_in['r2_ob'], 'L2_conv_ln_g': _L2_conv_in['ln_g'], 'L2_conv_ln_b': _L2_conv_in['ln_b'], 'L2_conv_w_in': _L2_conv_in['w_in'], 'L2_conv_w_out': _L2_conv_in['w_out'], 'L2_conv_f_wih_fw': _L2_conv_in['f_wih_fw'], 'L2_conv_f_whh_fw': _L2_conv_in['f_whh_fw'], 'L2_conv_f_bih_fw': _L2_conv_in['f_bih_fw'], 'L2_conv_f_bhh_fw': _L2_conv_in['f_bhh_fw'], 'L2_conv_f_wih_rv': _L2_conv_in['f_wih_rv'], 'L2_conv_f_whh_rv': _L2_conv_in['f_whh_rv'], 'L2_conv_f_bih_rv': _L2_conv_in['f_bih_rv'], 'L2_conv_f_bhh_rv': _L2_conv_in['f_bhh_rv'], 'L2_conv_b_wih_fw': _L2_conv_in['b_wih_fw'], 'L2_conv_b_whh_fw': _L2_conv_in['b_whh_fw'], 'L2_conv_b_bih_fw': _L2_conv_in['b_bih_fw'], 'L2_conv_b_bhh_fw': _L2_conv_in['b_bhh_fw'], 'L2_conv_b_wih_rv': _L2_conv_in['b_wih_rv'], 'L2_conv_b_whh_rv': _L2_conv_in['b_whh_rv'], 'L2_conv_b_bih_rv': _L2_conv_in['b_bih_rv'], 'L2_conv_b_bhh_rv': _L2_conv_in['b_bhh_rv'], 'L3_conv_ln_g': _L3_conv_in['ln_g'], 'L3_conv_ln_b': _L3_conv_in['ln_b'], 'L3_conv_w_in': _L3_conv_in['w_in'], 'L3_conv_w_out': _L3_conv_in['w_out'], 'L3_conv_f_wih_fw': _L3_conv_in['f_wih_fw'], 'L3_conv_f_whh_fw': _L3_conv_in['f_whh_fw'], 'L3_conv_f_bih_fw': _L3_conv_in['f_bih_fw'], 'L3_conv_f_bhh_fw': _L3_conv_in['f_bhh_fw'], 'L3_conv_f_wih_rv': _L3_conv_in['f_wih_rv'], 'L3_conv_f_whh_rv': _L3_conv_in['f_whh_rv'], 'L3_conv_f_bih_rv': _L3_conv_in['f_bih_rv'], 'L3_conv_f_bhh_rv': _L3_conv_in['f_bhh_rv'], 'L3_conv_b_wih_fw': _L3_conv_in['b_wih_fw'], 'L3_conv_b_whh_fw': _L3_conv_in['b_whh_fw'], 'L3_conv_b_bih_fw': _L3_conv_in['b_bih_fw'], 'L3_conv_b_bhh_fw': _L3_conv_in['b_bhh_fw'], 'L3_conv_b_wih_rv': _L3_conv_in['b_wih_rv'], 'L3_conv_b_whh_rv': _L3_conv_in['b_whh_rv'], 'L3_conv_b_bih_rv': _L3_conv_in['b_bih_rv'], 'L3_conv_b_bhh_rv': _L3_conv_in['b_bhh_rv']}

def reference(x, L0_conv_w1, L0_conv_b1, L0_conv_norm1_w, L0_conv_norm1_b, L0_conv_norm2_w, L0_conv_norm2_b, L0_conv_mlp_w1, L0_conv_mlp_b1, L0_conv_mlp_w2, L0_conv_mlp_b2, L1_conv_Wu, L1_conv_bu, L1_conv_Wv, L1_conv_bv, L1_conv_Wo, L1_conv_bo, L1_conv_r1_pw, L1_conv_r1_pb, L1_conv_r1_lw, L1_conv_r1_lb, L1_conv_r1_ow, L1_conv_r1_ob, L1_conv_r2_pw, L1_conv_r2_pb, L1_conv_r2_lw, L1_conv_r2_lb, L1_conv_r2_ow, L1_conv_r2_ob, L2_conv_ln_g, L2_conv_ln_b, L2_conv_w_in, L2_conv_w_out, L2_conv_f_wih_fw, L2_conv_f_whh_fw, L2_conv_f_bih_fw, L2_conv_f_bhh_fw, L2_conv_f_wih_rv, L2_conv_f_whh_rv, L2_conv_f_bih_rv, L2_conv_f_bhh_rv, L2_conv_b_wih_fw, L2_conv_b_whh_fw, L2_conv_b_bih_fw, L2_conv_b_bhh_fw, L2_conv_b_wih_rv, L2_conv_b_whh_rv, L2_conv_b_bih_rv, L2_conv_b_bhh_rv, L3_conv_ln_g, L3_conv_ln_b, L3_conv_w_in, L3_conv_w_out, L3_conv_f_wih_fw, L3_conv_f_whh_fw, L3_conv_f_bih_fw, L3_conv_f_bhh_fw, L3_conv_f_wih_rv, L3_conv_f_whh_rv, L3_conv_f_bih_rv, L3_conv_f_bhh_rv, L3_conv_b_wih_fw, L3_conv_b_whh_fw, L3_conv_b_bih_fw, L3_conv_b_bhh_fw, L3_conv_b_wih_rv, L3_conv_b_whh_rv, L3_conv_b_bih_rv, L3_conv_b_bhh_rv):
    import jax
    import jax.numpy as jnp

    def _L0_conv_ref(x, w1, b1, norm1_w, norm1_b, norm2_w, norm2_b, mlp_w1, mlp_b1, mlp_w2, mlp_b2):
        import jax, jax.numpy as jnp
        import numpy as np
        DIM = 96
        H = 16
        W = 16
        NB = 8
        BS = DIM // NB
        WF = W // 2 + 1
        EPS = 1e-05

        def _layernorm(x, g, b):
            mu = jnp.mean(x, axis=-1, keepdims=True)
            var = jnp.mean(jnp.square(x - mu), axis=-1, keepdims=True)
            return (x - mu) * jax.lax.rsqrt(var + EPS) * g + b
        B, h, w, C = x.shape
        residual = x
        xn = _layernorm(x, norm1_w, norm1_b)
        xf = jnp.fft.rfft2(xn.astype(jnp.float32), axes=(1, 2), norm='ortho')
        xf = xf.reshape(B, h, w // 2 + 1, NB, BS)
        w1c = jax.lax.complex(w1[..., 0], w1[..., 1])
        b1c = jax.lax.complex(b1[..., 0], b1[..., 1])
        o1 = jnp.einsum('bhwni,hwnio->bhwno', xf, w1c) + b1c
        o1 = jax.lax.complex(jax.nn.relu(o1.real), jax.nn.relu(o1.imag))
        o1 = o1.reshape(B, h, w // 2 + 1, C)
        xs = jnp.fft.irfft2(o1, s=(h, w), axes=(1, 2), norm='ortho')
        xm = _layernorm(xs, norm2_w, norm2_b)
        hdn = jax.nn.gelu(xm @ mlp_w1 + mlp_b1, approximate=False)
        mlp_out = hdn @ mlp_w2 + mlp_b2
        return xs + residual + mlp_out

    def _L1_conv_ref(x, H, W, Wu, bu, Wv, bv, Wo, bo, r1_pw, r1_pb, r1_lw, r1_lb, r1_ow, r1_ob, r2_pw, r2_pb, r2_lw, r2_lb, r2_ow, r2_ob):
        import jax, jax.numpy as jnp
        import numpy as np
        B, HH, WW, E = (8, 16, 16, 96)
        NH, EXP = (6, 2)
        D1 = EXP * E // NH * NH
        HD = D1 // NH
        RPE = 128
        LAYERS = 3
        EPS = 1e-06

        def srms(x):
            return x * jax.lax.rsqrt(jnp.mean(x * x, axis=-1, keepdims=True) + EPS)

        def rpe_forward(pos, pw, pb, lw, lb, ow, ob):
            x = jax.nn.relu(pos @ pw + pb)
            for i in range(lw.shape[0]):
                x = jax.nn.relu(srms(x)) @ lw[i] + lb[i]
            return jax.nn.relu(srms(x)) @ ow + ob

        def tno_coeffs(n, pw, pb, lw, lb, ow, ob):
            pos = jnp.arange(1, n, dtype=jnp.float32)[:, None]
            neg = -jnp.arange(1, n, dtype=jnp.float32)[::-1][:, None]
            zero = jnp.zeros((1, 1), dtype=jnp.float32)
            t_zero = rpe_forward(zero, pw, pb, lw, lb, ow, ob)
            t_pos = rpe_forward(pos, pw, pb, lw, lb, ow, ob)
            t_neg = rpe_forward(neg, pw, pb, lw, lb, ow, ob)
            a = jnp.concatenate([t_zero, t_pos, t_zero, t_neg], axis=0)
            return a.reshape(2 * n, NH, HD).transpose(1, 0, 2)

        def tno_apply(v, a, axis):
            n = v.shape[axis]
            a = a[:, :, None, :] if axis == -3 else a[:, None, :, :]
            y = jnp.fft.rfft(v, 2 * n, axis=axis)
            af = jnp.fft.rfft(a, 2 * n, axis=axis)
            out = jnp.fft.irfft(af * y, 2 * n, axis=axis)
            return jax.lax.slice_in_dim(out, 0, n, axis=out.ndim + axis)
        b = x.shape[0]
        xn = srms(x)
        u = jax.nn.silu(xn @ Wu + bu)
        v = jax.nn.silu(xn @ Wv + bv)
        v = v.reshape(b, H, W, NH, HD).transpose(0, 3, 1, 2, 4)
        a_h = tno_coeffs(H, r2_pw, r2_pb, r2_lw, r2_lb, r2_ow, r2_ob)
        a_w = tno_coeffs(W, r1_pw, r1_pb, r1_lw, r1_lb, r1_ow, r1_ob)
        out = tno_apply(v, a_h, -3) + tno_apply(v, a_w, -2)
        out = out.transpose(0, 2, 3, 1, 4).reshape(b, H, W, NH * HD)
        out = u * out
        return out @ Wo + bo + x

    def _L2_conv_ref(x, ln_g, ln_b, w_in, w_out, f_wih_fw, f_whh_fw, f_bih_fw, f_bhh_fw, f_wih_rv, f_whh_rv, f_bih_rv, f_bhh_rv, b_wih_fw, b_whh_fw, b_bih_fw, b_bhh_fw, b_wih_rv, b_whh_rv, b_bih_rv, b_bhh_rv):
        import jax, jax.numpy as jnp
        import numpy as np

        def _layernorm(x, g, b, eps=1e-05):
            m = x.mean(-1, keepdims=True)
            v = jnp.mean((x - m) ** 2, axis=-1, keepdims=True)
            return (x - m) / jnp.sqrt(v + eps) * g + b

        def _gru_dir(x, wih, whh, bih, bhh, reverse):
            if reverse:
                x = jnp.flip(x, 1)
            gx = jnp.einsum('blc,gc->blg', x, wih) + bih
            h = whh.shape[1]
            h0 = jnp.zeros((x.shape[0], h), x.dtype)

            def step(hprev, gxt):
                gh = hprev @ whh.T + bhh
                r = jax.nn.sigmoid(gxt[:, :h] + gh[:, :h])
                z = jax.nn.sigmoid(gxt[:, h:2 * h] + gh[:, h:2 * h])
                n = jnp.tanh(gxt[:, 2 * h:] + r * gh[:, 2 * h:])
                hn = (1.0 - z) * n + z * hprev
                return (hn, hn)
            _, ys = jax.lax.scan(step, h0, jnp.swapaxes(gx, 0, 1))
            out = jnp.swapaxes(ys, 0, 1)
            return jnp.flip(out, 1) if reverse else out

        def _bigru(x, wih_fw, whh_fw, bih_fw, bhh_fw, wih_rv, whh_rv, bih_rv, bhh_rv):
            return jnp.concatenate([_gru_dir(x, wih_fw, whh_fw, bih_fw, bhh_fw, False), _gru_dir(x, wih_rv, whh_rv, bih_rv, bhh_rv, True)], axis=-1)
        B, H, W, C = x.shape
        xn = _layernorm(x, ln_g, ln_b)
        xz = jnp.einsum('bhwc,dc->bhwd', xn, w_in).reshape(B, H * W, -1)
        x_inner, z = jnp.split(xz, 2, axis=-1)
        fwd = _bigru(x_inner, f_wih_fw, f_whh_fw, f_bih_fw, f_bhh_fw, f_wih_rv, f_whh_rv, f_bih_rv, f_bhh_rv)
        bwd = jnp.flip(_bigru(jnp.flip(x_inner, 1), b_wih_fw, b_whh_fw, b_bih_fw, b_bhh_fw, b_wih_rv, b_whh_rv, b_bih_rv, b_bhh_rv), 1)
        y = jax.nn.silu(fwd + bwd) * jax.nn.silu(z)
        y = jnp.einsum('bld,cd->blc', y, w_out).reshape(B, H, W, C)
        return x + y

    def _L3_conv_ref(x, ln_g, ln_b, w_in, w_out, f_wih_fw, f_whh_fw, f_bih_fw, f_bhh_fw, f_wih_rv, f_whh_rv, f_bih_rv, f_bhh_rv, b_wih_fw, b_whh_fw, b_bih_fw, b_bhh_fw, b_wih_rv, b_whh_rv, b_bih_rv, b_bhh_rv):
        import jax, jax.numpy as jnp
        import numpy as np

        def _layernorm(x, g, b, eps=1e-05):
            m = x.mean(-1, keepdims=True)
            v = jnp.mean((x - m) ** 2, axis=-1, keepdims=True)
            return (x - m) / jnp.sqrt(v + eps) * g + b

        def _gru_dir(x, wih, whh, bih, bhh, reverse):
            if reverse:
                x = jnp.flip(x, 1)
            gx = jnp.einsum('blc,gc->blg', x, wih) + bih
            h = whh.shape[1]
            h0 = jnp.zeros((x.shape[0], h), x.dtype)

            def step(hprev, gxt):
                gh = hprev @ whh.T + bhh
                r = jax.nn.sigmoid(gxt[:, :h] + gh[:, :h])
                z = jax.nn.sigmoid(gxt[:, h:2 * h] + gh[:, h:2 * h])
                n = jnp.tanh(gxt[:, 2 * h:] + r * gh[:, 2 * h:])
                hn = (1.0 - z) * n + z * hprev
                return (hn, hn)
            _, ys = jax.lax.scan(step, h0, jnp.swapaxes(gx, 0, 1))
            out = jnp.swapaxes(ys, 0, 1)
            return jnp.flip(out, 1) if reverse else out

        def _bigru(x, wih_fw, whh_fw, bih_fw, bhh_fw, wih_rv, whh_rv, bih_rv, bhh_rv):
            return jnp.concatenate([_gru_dir(x, wih_fw, whh_fw, bih_fw, bhh_fw, False), _gru_dir(x, wih_rv, whh_rv, bih_rv, bhh_rv, True)], axis=-1)
        B, H, W, C = x.shape
        xn = _layernorm(x, ln_g, ln_b)
        xz = jnp.einsum('bhwc,dc->bhwd', xn, w_in).reshape(B, H * W, -1)
        x_inner, z = jnp.split(xz, 2, axis=-1)
        fwd = _bigru(x_inner, f_wih_fw, f_whh_fw, f_bih_fw, f_bhh_fw, f_wih_rv, f_whh_rv, f_bih_rv, f_bhh_rv)
        bwd = jnp.flip(_bigru(jnp.flip(x_inner, 1), b_wih_fw, b_whh_fw, b_bih_fw, b_bhh_fw, b_wih_rv, b_whh_rv, b_bih_rv, b_bhh_rv), 1)
        y = jax.nn.silu(fwd + bwd) * jax.nn.silu(z)
        y = jnp.einsum('bld,cd->blc', y, w_out).reshape(B, H, W, C)
        return x + y

    def _gn(v, G=32, eps=1e-05):
        B_, H_, W_, C_ = v.shape
        g = v.reshape(B_, H_, W_, G, C_ // G)
        m = jnp.mean(g, axis=(1, 2, 4), keepdims=True)
        s = jnp.var(g, axis=(1, 2, 4), keepdims=True)
        return ((g - m) / jnp.sqrt(s + eps)).reshape(v.shape)

    def _ln_c(v, eps=1e-06):
        m = jnp.mean(v, axis=-1, keepdims=True)
        s = jnp.var(v, axis=-1, keepdims=True)
        return (v - m) / jnp.sqrt(s + eps)

    def _ln_t(v, eps=1e-05):
        m = jnp.mean(v, axis=-1, keepdims=True)
        s = jnp.var(v, axis=-1, keepdims=True)
        return (v - m) / jnp.sqrt(s + eps)

    def _to_tokens(v):
        B_, H_, W_, C_ = v.shape
        return v.reshape(B_, H_ * W_, C_)

    def _from_tokens(t, like):
        return t.reshape(like.shape)
    x = _L0_conv_ref(x, L0_conv_w1, L0_conv_b1, L0_conv_norm1_w, L0_conv_norm1_b, L0_conv_norm2_w, L0_conv_norm2_b, L0_conv_mlp_w1, L0_conv_mlp_b1, L0_conv_mlp_w2, L0_conv_mlp_b2)
    x = _L1_conv_ref(x, 16, 16, L1_conv_Wu, L1_conv_bu, L1_conv_Wv, L1_conv_bv, L1_conv_Wo, L1_conv_bo, L1_conv_r1_pw, L1_conv_r1_pb, L1_conv_r1_lw, L1_conv_r1_lb, L1_conv_r1_ow, L1_conv_r1_ob, L1_conv_r2_pw, L1_conv_r2_pb, L1_conv_r2_lw, L1_conv_r2_lb, L1_conv_r2_ow, L1_conv_r2_ob)
    x = _L2_conv_ref(x, L2_conv_ln_g, L2_conv_ln_b, L2_conv_w_in, L2_conv_w_out, L2_conv_f_wih_fw, L2_conv_f_whh_fw, L2_conv_f_bih_fw, L2_conv_f_bhh_fw, L2_conv_f_wih_rv, L2_conv_f_whh_rv, L2_conv_f_bih_rv, L2_conv_f_bhh_rv, L2_conv_b_wih_fw, L2_conv_b_whh_fw, L2_conv_b_bih_fw, L2_conv_b_bhh_fw, L2_conv_b_wih_rv, L2_conv_b_whh_rv, L2_conv_b_bih_rv, L2_conv_b_bhh_rv)
    x = _L3_conv_ref(x, L3_conv_ln_g, L3_conv_ln_b, L3_conv_w_in, L3_conv_w_out, L3_conv_f_wih_fw, L3_conv_f_whh_fw, L3_conv_f_bih_fw, L3_conv_f_bhh_fw, L3_conv_f_wih_rv, L3_conv_f_whh_rv, L3_conv_f_bih_rv, L3_conv_f_bhh_rv, L3_conv_b_wih_fw, L3_conv_b_whh_fw, L3_conv_b_bih_fw, L3_conv_b_bhh_fw, L3_conv_b_wih_rv, L3_conv_b_whh_rv, L3_conv_b_bih_rv, L3_conv_b_bhh_rv)
    return x

_drawn_inputs = setup_inputs


def setup_inputs(seed=0):
    import zlib

    import numpy as np

    out = dict(_drawn_inputs(seed))
    spreads = {'L0_conv_norm1_w': (1.0, 0.2),
     'L0_conv_norm1_b': (0.0, 0.512),
     'L0_conv_norm2_w': (1.0, 0.2),
     'L0_conv_norm2_b': (0.0, 0.392),
     'L1_conv_bu': (0.0, 0.8),
     'L1_conv_bv': (0.0, 0.8),
     'L1_conv_bo': (0.0, 0.8),
     'L1_conv_r1_pb': (0.0, 0.8),
     'L1_conv_r1_lb': (0.0, 0.8),
     'L1_conv_r1_ob': (0.0, 0.8),
     'L1_conv_r2_pb': (0.0, 0.8),
     'L1_conv_r2_lb': (0.0, 0.8),
     'L1_conv_r2_ob': (0.0, 0.8),
     'L2_conv_ln_g': (1.0, 0.6),
     'L2_conv_ln_b': (0.0, 2.0),
     'L2_conv_f_bih_fw': (0.0, 2.0),
     'L2_conv_f_bhh_fw': (0.0, 2.0),
     'L2_conv_f_bih_rv': (0.0, 2.0),
     'L2_conv_f_bhh_rv': (0.0, 2.0),
     'L2_conv_b_bih_fw': (0.0, 2.0),
     'L2_conv_b_bhh_fw': (0.0, 2.0),
     'L2_conv_b_bih_rv': (0.0, 2.0),
     'L2_conv_b_bhh_rv': (0.0, 2.0),
     'L3_conv_ln_g': (1.0, 0.6),
     'L3_conv_ln_b': (0.0, 2.0),
     'L3_conv_f_bih_fw': (0.0, 2.0),
     'L3_conv_f_bhh_fw': (0.0, 2.0),
     'L3_conv_f_bih_rv': (0.0, 2.0),
     'L3_conv_f_bhh_rv': (0.0, 2.0),
     'L3_conv_b_bih_fw': (0.0, 2.0),
     'L3_conv_b_bhh_fw': (0.0, 2.0),
     'L3_conv_b_bih_rv': (0.0, 2.0),
     'L3_conv_b_bhh_rv': (0.0, 2.0)}
    factors = {'L0_conv_mlp_b1': 2.935,
     'L1_conv_Wu': 8.0,
     'L1_conv_Wv': 8.0,
     'L1_conv_Wo': 8.0,
     'L1_conv_r1_pw': 8.0,
     'L1_conv_r1_lw': 8.0,
     'L1_conv_r1_ow': 8.0,
     'L1_conv_r2_pw': 8.0,
     'L1_conv_r2_lw': 8.0,
     'L1_conv_r2_ow': 8.0,
     'L2_conv_f_wih_fw': 30.696,
     'L2_conv_f_whh_fw': 64.0,
     'L2_conv_f_wih_rv': 29.752,
     'L2_conv_f_whh_rv': 64.0,
     'L2_conv_b_wih_fw': 30.68,
     'L2_conv_b_whh_fw': 64.0,
     'L2_conv_b_wih_rv': 28.552,
     'L2_conv_b_whh_rv': 64.0,
     'L3_conv_f_wih_fw': 32.64,
     'L3_conv_f_whh_fw': 64.0,
     'L3_conv_f_wih_rv': 32.552,
     'L3_conv_f_whh_rv': 64.0,
     'L3_conv_b_wih_fw': 33.2,
     'L3_conv_b_whh_fw': 64.0,
     'L3_conv_b_wih_rv': 31.256,
     'L3_conv_b_whh_rv': 64.0,
     'L2_conv_w_in': 8.0,
     'L2_conv_w_out': 8.0,
     'L3_conv_w_in': 8.0,
     'L3_conv_w_out': 8.0}
    for name, (base, spread) in spreads.items():
        noise = np.random.default_rng([zlib.crc32(name.encode()), seed]).standard_normal(out[name].shape)
        drawn = base * np.exp(spread * noise) if base else spread * noise
        out[name] = jnp.asarray(drawn.astype(out[name].dtype))
    for name, factor in factors.items():
        out[name] = (out[name] * factor).astype(out[name].dtype)
    return out
```

```python
from contextlib import ExitStack

import numpy as np

import concourse.bass as bass
from concourse import mybir

F32 = mybir.dt.float32
F16 = mybir.dt.float16
ALU = mybir.AluOpType
ACT = mybir.ActivationFunctionType

P = 128
BATCH, SIDE, C = 8, 16, 96
SEQ = SIDE * SIDE
TOKENS = BATCH * SEQ
TILES = TOKENS // P
HALVES = SEQ // P
BANK = 512

KW = SIDE // 2 + 1
FREQS = SIDE * KW
BLOCKS = 8
BLOCK = C // BLOCKS
QUARTERS = 4
FQ = FREQS // QUARTERS
COMPLEX = 2 * BLOCK
HIDDEN = 4 * C

CHUNKS = 2
D1 = CHUNKS * C
LAGS = 2 * SIDE - 1
RPE = 128
DEPTH = 3

GRUS = ("f_%s_fw", "b_%s_rv", "f_%s_rv", "b_%s_fw")
GATES = 3
STEPS = 16
CHUNK_COUNT = SEQ // STEPS
RING = 2 * STEPS
GROUPS = 2
PER = 2 * BATCH
F16_MAX = 65504.0


def flat(ap):
    return ap.rearrange("p a b -> p (a b)")


def split_tokens(ap):
    return ap.rearrange("p (b t) -> p b t", b=BATCH)


class Norm:

    def __init__(self, nc, ctx, name, stream, out, eps, centred=True):
        sb = lambda n, shape: ctx.enter_context(nc.sbuf_tensor(f"{name}_{n}", shape, F32))
        sem = lambda n: ctx.enter_context(nc.semaphore(f"{name}_{n}"))
        self.stream, self.out, self.eps, self.centred = stream, out, eps, centred
        self.stats = sb("stats", [P, TILES, 6])
        self.moments = sb("moments", [P, TILES, 2])
        self.power = sb("power", [P, TILES])
        self.exponent = sb("exponent", [P, TILES])
        self.guess = sb("guess", [P, TILES])
        self.work = sb("work", [P, TILES])
        self.rstd = sb("rstd", [P, TILES])
        self.chained = sem("chained")
        self.power_ready = sem("power_ready")
        self.guess_ready = sem("guess_ready")
        self.rows_ready = sem("rows_ready")


def norm_vector(e, n):
    count = 0

    def link(ins):
        nonlocal count
        count += 1
        ins.then_inc(n.chained, 1)
        e.wait_ge(n.chained, count)

    e.memset(n.exponent[:], -0.5).then_inc(n.power_ready, 1)
    for i in range(TILES):
        last = e.bn_stats(n.stats[:, i, :], n.stream[:, i, :])
    link(last)
    for i in range(TILES):
        last = e.bn_aggr(n.moments[:, i, :], n.stats[:, i, :])
    link(last)
    if n.centred:
        e.tensor_scalar(n.power[:], n.moments[:, :, 1], n.eps, None, ALU.add).then_inc(n.power_ready, 1)
    else:
        link(e.tensor_tensor(n.work[:], n.moments[:, :, 0], n.moments[:, :, 0], ALU.mult))
        e.scalar_tensor_tensor(out=n.power[:], in0=n.moments[:, :, 1], scalar=n.eps, in1=n.work[:],
                               op0=ALU.add, op1=ALU.add).then_inc(n.power_ready, 1)
    e.wait_ge(n.power_ready, 2)
    e.wait_ge(n.guess_ready, 1)
    link(e.tensor_tensor(n.work[:], n.guess[:], n.guess[:], ALU.mult))
    link(e.tensor_tensor(n.work[:], n.work[:], n.power[:], ALU.mult))
    link(e.tensor_scalar(n.work[:], n.work[:], -0.5, 1.5, ALU.mult, ALU.add))
    link(e.tensor_tensor(n.rstd[:], n.work[:], n.guess[:], ALU.mult))
    for i in range(TILES):
        row = n.stream[:, i, :]
        if n.centred:
            ins = e.tensor_scalar(n.out[:, i, :], row, n.moments[:, i, 0:1], n.rstd[:, i:i + 1],
                                  ALU.subtract, ALU.mult)
        else:
            ins = e.tensor_scalar(n.out[:, i, :], row, n.rstd[:, i:i + 1], None, ALU.mult)
        ins.then_inc(n.rows_ready, 1)


def norm_gpsimd(e, n):
    e.wait_ge(n.power_ready, 2)
    e.tensor_tensor(n.guess[:], n.power[:], n.exponent[:], ALU.pow).then_inc(n.guess_ready, 1)


def transposes(e, n, ident, banks, turned):
    for i in range(TILES):
        e.wait_ge(n.rows_ready, i + 1)
        e.transpose(banks[i // 4][0:C, (i % 4) * P:(i % 4 + 1) * P], n.out[:, i, :], ident[:]).then_inc(turned, 1)


def fourier(nc, d, stream, ident, loaded_x, x_bytes):
    with ExitStack() as ctx:
        sb = lambda n, shape, dt=F32: ctx.enter_context(nc.sbuf_tensor("l0_" + n, shape, dt))
        sem = lambda n: ctx.enter_context(nc.semaphore("l0_" + n))
        w_raw = sb("w_raw", [C, FREQS * COMPLEX])
        w_for = [sb("w_for_re", [C, FREQS, 32]), sb("w_for_im", [C, FREQS, 32])]
        bias = sb("bias", [P, FQ * BLOCKS])
        dft = sb("dft", [P, HALVES, 2 * FREQS])
        idft = sb("idft", [FQ, QUARTERS * 2 * HALVES, P])
        mask = sb("mask", [C, BLOCKS])
        affine = sb("affine", [C, 2])
        rows = sb("rows", [P, TILES, C])
        spectrum = sb("spectrum", [C, 2 * FREQS, BATCH])
        spread = sb("spread", [C, 2 * FREQS, BLOCKS, BATCH])
        mixed = sb("mixed", [P, BLOCKS * BATCH, FQ])
        by_freq = spread[0:FQ].rearrange("p f n b -> p (f n b)")[:, 0:BATCH * BLOCKS * QUARTERS * COMPLEX]\
            .rearrange("p (b n m) -> p b n m", b=BATCH, n=BLOCKS)
        shift0 = sb("shift0", [C, 1])
        loaded = sem("loaded")
        w_loaded = sem("w_loaded")
        chained = sem("chained")
        w_ready = sem("w_ready")
        w_steps = sem("w_steps")
        transformed = sem("transformed")
        evacuated = sem("evacuated")
        shifted = sem("shifted")
        spread_ready = sem("spread_ready")
        products = sem("products")
        biased = sem("biased")
        relu_done = sem("relu_done")
        turned = sem("turned")
        turn_saved_v = sem("turn_saved_v")
        turn_saved_s = sem("turn_saved_s")
        inverted = sem("inverted")
        stream_s = sem("stream_s")
        xs_ready = sem("xs_ready")
        norm = Norm(nc, ctx, "l0n", stream, rows, 1e-5)
        spatial = sb("spatial", [P, TILES, C])
        residual = sb("residual", [P, TILES, C])

        banks = [ctx.enter_context(nc.psum_tensor(f"l0_bank{i}", [P, BANK], F32)) for i in range(8)]
        PRODUCT_BANKS = -(-FQ // 8)
        with nc.Block() as block:

            @block.sync
            def _(e):
                e.dma_start(dft[:], d["dft"]).then_inc(loaded, 16)
                e.dma_start(mask[:], d["mask"]).then_inc(loaded, 16)
                e.dma_start(affine[:], d["L0_norm1"]).then_inc(loaded, 16)
                e.dma_start(w_raw[:], d["L0_w1"]).then_inc(w_loaded, 16)
                e.dma_start(bias[:], d["L0_b1"]).then_inc(w_loaded, 16)
                e.dma_start(idft[:], d["idft"]).then_inc(w_loaded, 16)

            @block.gpsimd
            def _(e):
                for w in w_for:
                    e.memset(w[:, :, COMPLEX:32], 0.0).then_inc(w_ready, 1)
                norm_gpsimd(e, norm)

            @block.vector
            def _(e):
                e.wait_ge(loaded_x, x_bytes)
                norm_vector(e, norm)
                e.wait_ge(loaded, 48)
                e.tensor_scalar(shift0[:], affine[:, 1:2], float(SIDE), None, ALU.mult).then_inc(chained, 1)
                e.wait_ge(evacuated, BATCH)
                e.wait_ge(chained, 1)
                e.tensor_scalar(spectrum[:, 0, :], spectrum[:, 0, :], shift0[:], None, ALU.add).then_inc(shifted, 1)
                e.wait_ge(shifted, 1)
                for n in range(0, BLOCKS, 2):
                    e.tensor_scalar(spread[:, :, n, :], spectrum[:], mask[:, n:n + 1], None, ALU.mult)\
                        .then_inc(spread_ready, 1)
                bias_v = bias[:].rearrange("p (f n) -> p f n", n=BLOCKS)
                for k in range(PRODUCT_BANKS):
                    f0, f1 = 8 * k, min(FQ, 8 * k + 8)
                    e.wait_ge(products, k + 1)
                    for f in range(f0, f1):
                        ins = e.tensor_tensor(
                            mixed[:, :, f].rearrange("p (n b) -> p n b", b=BATCH),
                            banks[k][:, (f - f0) * 64:(f - f0 + 1) * 64].rearrange("p (n b) -> p n b", b=BATCH),
                            bias_v[:, f, :].unsqueeze(2).to_broadcast([P, BLOCKS, BATCH]), ALU.add)
                    ins.then_inc(biased, 1)
                for m in range(0, 16, 2):
                    e.wait_ge(turned, m + 1)
                    n, b0 = m // 2, 4 * (m % 2)
                    src = banks[m % 8][0:FQ, :].rearrange("p (b j m) -> p b j m", b=4, j=QUARTERS)[:, :, :, 0:COMPLEX]
                    dst = by_freq[:, b0:b0 + 4, n, :].rearrange("p b (j m) -> p b j m", j=QUARTERS)
                    e.tensor_copy(dst, src).then_inc(turn_saved_v, 1)
                for g in range(4):
                    half, pair = g // 2, g % 2
                    e.wait_ge(inverted, g + 1)
                    src = banks[g][:, 0:4 * C].rearrange("p (b c) -> p b c", b=4)
                    dst = spatial[:].rearrange("p (b s) c -> p s b c", s=HALVES)[:, half, 4 * pair:4 * pair + 4, :]
                    e.tensor_copy(dst, src).then_inc(xs_ready, 1)
                e.wait_ge(xs_ready, 4)
                e.tensor_tensor(residual[:], spatial[:], stream[:], ALU.add).then_inc(stream_s, 1)
                e.wait_ge(stream_s, 1)

            @block.scalar
            def _(e):
                e.wait_ge(w_loaded, 48)
                raw = w_raw[:].rearrange("p (f o r) -> p f o r", o=BLOCK, r=2)
                pair = [w[:, :, 0:COMPLEX].rearrange("p f (o r) -> p f o r", r=2) for w in w_for]
                e.activation(w_for[0][:, :, 0:COMPLEX], w_raw[:].rearrange("p (f m) -> p f m", m=COMPLEX),
                             ACT.Copy).then_inc(w_ready, 1)
                e.activation(pair[1][:, :, :, 1], raw[:, :, :, 0], ACT.Copy).then_inc(w_ready, 1)
                e.activation(pair[1][:, :, :, 0], raw[:, :, :, 1], ACT.Copy, scale=-1.0).then_inc(w_ready, 1)
                e.wait_ge(loaded, 48)
                for b in range(BATCH):
                    e.wait_ge(transformed, b + 1)
                    e.activation(spectrum[:, :, b], banks[b][0:C, 0:2 * FREQS], ACT.Copy, scale=affine[:, 0:1])\
                        .then_inc(evacuated, 1)
                e.wait_ge(shifted, 1)
                for n in range(1, BLOCKS, 2):
                    e.activation(spread[:, :, n, :], spectrum[:], ACT.Copy, scale=mask[:, n:n + 1])\
                        .then_inc(spread_ready, 1)
                e.wait_ge(biased, PRODUCT_BANKS)
                for n in range(BLOCKS):
                    part = mixed[:, n * BATCH:(n + 1) * BATCH, :]
                    e.activation(part, part, ACT.Relu).then_inc(relu_done, 1)
                for m in range(1, 16, 2):
                    e.wait_ge(turned, m + 1)
                    n, b0 = m // 2, 4 * (m % 2)
                    src = banks[m % 8][0:FQ, :].rearrange("p (b j m) -> p b j m", b=4, j=QUARTERS)[:, :, :, 0:COMPLEX]
                    dst = by_freq[:, b0:b0 + 4, n, :].rearrange("p b (j m) -> p b j m", j=QUARTERS)
                    e.activation(dst, src, ACT.Copy).then_inc(turn_saved_s, 1)

            @block.tensor
            def _(e):
                e.wait_ge(loaded, 48)
                for b in range(BATCH):
                    for half in range(HALVES):
                        tile = HALVES * b + half
                        e.wait_ge(norm.rows_ready, tile + 1)
                        last = e.matmul(banks[b][0:C, 0:2 * FREQS], rows[:, tile, :], dft[:, half, :],
                                        start=(half == 0), stop=(half == HALVES - 1))
                    last.then_inc(transformed, 1)
                e.wait_ge(w_ready, 5)
                e.wait_ge(spread_ready, BLOCKS)
                for f in range(FQ):
                    k, f8 = divmod(f, 8)
                    for part in range(2):
                        for j in range(QUARTERS):
                            freq = j * FQ + f
                            last = e.matmul(banks[k][32 * j:32 * j + 32, f8 * 64:(f8 + 1) * 64],
                                            w_for[part][:, freq, :], flat(spread[:, 2 * freq + part, :, :]),
                                            start=(part == 0), stop=(part == 1), skip_group_check=True)
                    if f8 == 7 or f == FQ - 1:
                        last.then_inc(products, 1)
                for m in range(16):
                    n, b0 = m // 2, 4 * (m % 2)
                    e.wait_ge(relu_done, n + 1)
                    if m >= 8:
                        e.wait_ge(turn_saved_v if m % 2 == 0 else turn_saved_s, (m - 8) // 2 + 1)
                    for b in range(4):
                        last = e.transpose(banks[m % 8][0:FQ, b * P:(b + 1) * P], mixed[:, n * BATCH + b0 + b, :], ident[:])
                    last.then_inc(turned, 1)
                e.wait_ge(turn_saved_v, 8)
                e.wait_ge(turn_saved_s, 8)
                for g in range(4):
                    half, pair = g // 2, g % 2
                    out = banks[g][:, 0:4 * C].rearrange("p (b n o) -> p b n o", b=4, n=BLOCKS)
                    for k in range(2 * QUARTERS):
                        j, part = divmod(k, 2)
                        rhs = by_freq[:, 4 * pair:4 * pair + 4, :, j * COMPLEX + part:(j + 1) * COMPLEX:2]
                        last = e.matmul(out, idft[:, k * HALVES + half, :], rhs, start=(k == 0), stop=(k == 2 * QUARTERS - 1))
                    last.then_inc(inverted, 1)

        mlp(nc, d, stream, spatial, residual, rows, banks, ident)


def mlp(nc, d, stream, spatial, residual, rows, banks, ident):
    with ExitStack() as ctx:
        sb = lambda n, shape, dt=F32: ctx.enter_context(nc.sbuf_tensor("mlp_" + n, shape, dt))
        sem = lambda n: ctx.enter_context(nc.semaphore("mlp_" + n))
        KH = HIDDEN // P
        NB = TOKENS // BANK
        w1, w2 = sb("w1", [C, HIDDEN]), sb("w2", [P, KH, C])
        b1, b2, affine = sb("b1", [P, KH]), sb("b2", [P, C]), sb("affine", [C, 2])
        xT = sb("xT", [C, TOKENS])
        hidden = sb("hidden", [P, 2, KH, BANK])
        loaded, turned, scaled = sem("loaded"), sem("turned"), sem("scaled")
        up, activated, down, added, base = sem("up"), sem("activated"), sem("down"), sem("added"), sem("base")
        norm = Norm(nc, ctx, "mlpn", spatial, rows, 1e-5)
        with nc.Block() as block:

            @block.sync
            def _(e):
                for dst, name in ((w1, "L0_mlp_w1"), (w2, "L0_mlp_w2"), (b1, "L0_mlp_b1"), (b2, "L0_mlp_b2"), (affine, "L0_norm2")):
                    e.dma_start(dst[:], d[name]).then_inc(loaded, 16)

            @block.gpsimd
            def _(e):
                norm_gpsimd(e, norm)
                e.wait_ge(loaded, 80)
                e.tensor_tensor(residual[:], residual[:], b2[:].unsqueeze(1).to_broadcast([P, TILES, C]), ALU.add)\
                    .then_inc(base, 1)

            @block.vector
            def _(e):
                norm_vector(e, norm)
                e.wait_ge(base, 1)
                for k in range(NB):
                    e.wait_ge(down, k + 1)
                    e.tensor_tensor(stream[:, 4 * k:4 * k + 4, :], residual[:, 4 * k:4 * k + 4, :],
                                    banks[6 + k % 2][:, 0:4 * C].rearrange("p (t c) -> p t c", c=C), ALU.add)\
                        .then_inc(added, 1)

            @block.scalar
            def _(e):
                e.wait_ge(loaded, 80)
                for k in range(NB):
                    e.wait_ge(turned, 4 * k + 4)
                    e.activation(xT[:, k * BANK:(k + 1) * BANK], banks[k][0:C, :], ACT.Identity,
                                 scale=affine[:, 0:1], bias=affine[:, 1:2]).then_inc(scaled, 1)
                for k in range(NB):
                    if k >= 2:
                        e.wait_ge(down, k - 1)
                    for m in range(KH):
                        e.wait_ge(up, k * KH + m + 1)
                        e.activation(hidden[:, k % 2, m, :], banks[(k * KH + m) % 6][:], ACT.Gelu,
                                     bias=b1[:, m:m + 1]).then_inc(activated, 1)

            @block.tensor
            def _(e):
                transposes(e, norm, ident, banks, turned)
                e.wait_ge(scaled, NB)
                for k in range(NB + 1):
                    if k < NB:
                        for m in range(KH):
                            n = k * KH + m
                            if n >= 6:
                                e.wait_ge(activated, n - 5)
                            e.matmul(banks[n % 6][:], w1[:, m * P:(m + 1) * P], xT[:, k * BANK:(k + 1) * BANK],
                                     start=True, stop=True).then_inc(up, 1)
                    if k >= 1:
                        q = k - 1
                        e.wait_ge(activated, KH * k)
                        if q >= 2:
                            e.wait_ge(added, q - 1)
                        for t in range(4):
                            for m in range(KH):
                                last = e.matmul(banks[6 + q % 2][:, t * C:(t + 1) * C],
                                                hidden[:, q % 2, m, t * P:(t + 1) * P], w2[:, m, :],
                                                start=(m == 0), stop=(m == KH - 1))
                        last.then_inc(down, 1)


def coefficients(nc, d, coef, ones):
    with ExitStack() as ctx:
        sb = lambda n, shape, dt=F32: ctx.enter_context(nc.sbuf_tensor("rpe_" + n, shape, dt))
        sem = lambda n: ctx.enter_context(nc.semaphore("rpe_" + n))
        pos = sb("pos", [RPE, LAGS])
        small = sb("small", [RPE, 2, 2 + DEPTH])
        lw = sb("lw", [RPE, 2, DEPTH * RPE])
        ow = sb("ow", [RPE, 2, D1])
        ob = sb("ob", [C, 2, CHUNKS])
        x = sb("x", [RPE, 2, LAGS])
        sq = sb("sq", [RPE, 2, LAGS])
        ms = sb("ms", [RPE, 2, LAGS])
        guess = sb("guess", [RPE, 2, LAGS])
        tmp = sb("tmp", [RPE, 2, LAGS])
        y = sb("y", [RPE, 2, LAGS])
        exponent = sb("exponent", [RPE, 2, LAGS])
        mean_bank = ctx.enter_context(nc.psum_tensor("rpe_mean", [RPE, 2, LAGS], F32))
        out_bank = ctx.enter_context(nc.psum_tensor("rpe_out", [RPE, 2, 2, LAGS], F32))
        loaded, x_ready, sq_ready = sem("loaded"), sem("x_ready"), sem("sq_ready")
        mean_ready, ms_ready, guessed, y_ready = sem("mean_ready"), sem("ms_ready"), sem("guessed"), sem("y_ready")
        product, chained = sem("product"), sem("chained")
        with nc.Block() as block:

            @block.sync
            def _(e):
                for dst, name in ((pos, "pos"), (small, "rpe_small"), (lw, "rpe_lw"), (ow, "rpe_ow"), (ob, "rpe_ob")):
                    e.dma_start(dst[:], d[name]).then_inc(loaded, 16)

            @block.scalar
            def _(e):
                e.wait_ge(loaded, 80)
                for a in range(2):
                    e.activation(x[:, a, :], pos[:], ACT.Relu, scale=small[:, a, 0:1], bias=small[:, a, 1:2])\
                        .then_inc(x_ready, 1)
                for i in range(DEPTH + 1):
                    if i:
                        for a in range(2):
                            e.wait_ge(product, 2 * i)
                            e.activation(x[:, a, :], out_bank[:, a, 0, :], ACT.Identity,
                                         bias=small[:, a, 1 + i:2 + i]).then_inc(x_ready, 1)
                    e.wait_ge(x_ready, 2 * i + 2)
                    e.activation(sq[:], x[:], ACT.Square).then_inc(sq_ready, 1)
                e.wait_ge(product, 2 * DEPTH + 4)
                for a in range(2):
                    for m in range(CHUNKS):
                        e.activation(coef[:, m, a, :], out_bank[0:C, a, m, :], ACT.Identity, bias=ob[:, a, m:m + 1])

            @block.tensor
            def _(e):
                for i in range(DEPTH + 1):
                    e.wait_ge(sq_ready, i + 1)
                    e.matmul(flat(mean_bank[:]), ones[:], flat(sq[:]), start=True, stop=True).then_inc(mean_ready, 1)
                    e.wait_ge(y_ready, i + 1)
                    for a in range(2):
                        if i < DEPTH:
                            e.matmul(out_bank[:, a, 0, :], lw[:, a, i * RPE:(i + 1) * RPE], y[:, a, :],
                                     start=True, stop=True).then_inc(product, 1)
                        else:
                            for m in range(CHUNKS):
                                e.matmul(out_bank[0:C, a, m, :], ow[:, a, m * C:(m + 1) * C], y[:, a, :],
                                         start=True, stop=True).then_inc(product, 1)

            @block.gpsimd
            def _(e):
                for i in range(DEPTH + 1):
                    e.wait_ge(ms_ready, i + 2)
                    e.tensor_tensor(guess[:], ms[:], exponent[:], ALU.pow).then_inc(guessed, 1)

            @block.vector
            def _(e):
                count = 0

                def link(ins):
                    nonlocal count
                    count += 1
                    ins.then_inc(chained, 1)
                    e.wait_ge(chained, count)

                e.memset(exponent[:], -0.5).then_inc(ms_ready, 1)
                for i in range(DEPTH + 1):
                    e.wait_ge(mean_ready, i + 1)
                    e.tensor_scalar(ms[:], mean_bank[:], 1e-6, None, ALU.add).then_inc(ms_ready, 1)
                    e.wait_ge(guessed, i + 1)
                    link(e.tensor_tensor(tmp[:], guess[:], guess[:], ALU.mult))
                    link(e.tensor_tensor(tmp[:], tmp[:], ms[:], ALU.mult))
                    link(e.tensor_scalar(tmp[:], tmp[:], -0.5, 1.5, ALU.mult, ALU.add))
                    link(e.tensor_tensor(tmp[:], tmp[:], guess[:], ALU.mult))
                    e.wait_ge(x_ready, 2 * i + 2)
                    e.scalar_tensor_tensor(out=flat(y[:]), in0=flat(x[:]), scalar=0.0, in1=flat(tmp[:]),
                                           op0=ALU.max, op1=ALU.mult).then_inc(y_ready, 1)


PE_LAGS = [(axis, lag) for axis, lags in ((0, range(-6, 6)), (1, range(-6, 6))) for lag in lags]
PE_LAGS.sort(key=lambda al: al != (0, 0))
DVE_LAGS = [(axis, lag) for axis in range(2) for lag in sorted(range(1 - SIDE, SIDE), key=abs) if (axis, lag) not in PE_LAGS]


def shifted(v, axis, lag):
    n = SIDE - abs(lag)
    to, of = (slice(lag, SIDE), slice(0, n)) if lag >= 0 else (slice(0, n), slice(-lag, SIDE))
    return to, of


def toeplitz(nc, d, stream, ident, coef):
    with ExitStack() as ctx:
        sb = lambda n, shape, dt=F32: ctx.enter_context(nc.sbuf_tensor("l1_" + n, shape, dt))
        sem = lambda n: ctx.enter_context(nc.semaphore("l1_" + n))
        NB = TOKENS // BANK
        NDIAG = 4
        rows = sb("rows", [P, TILES, C])
        xT = sb("xT", [C, TOKENS])
        w_uv, b_uv = sb("w_uv", [C, 2, D1]), sb("b_uv", [C, 2, CHUNKS])
        w_o, b_o = sb("w_o", [C, CHUNKS, C]), sb("b_o", [P, C])
        u, v = sb("u", [C, CHUNKS, TOKENS]), sb("v", [C, CHUNKS, TOKENS])
        acc = sb("acc", [C, CHUNKS, TOKENS])
        diag = sb("diag", [C, NDIAG, C])
        base = sb("base", [P, TILES, C])
        loaded, turned, copied = sem("loaded"), sem("turned"), sem("copied")
        uv_done, v_ready, u_ready = sem("uv_done"), sem("v_ready"), sem("u_ready")
        diag_ready, diag_used, conv_done = sem("diag_ready"), sem("diag_used"), sem("conv_done")
        acc_step, summed, gated, projected, added, based = (sem("acc_step"), sem("summed"), sem("gated"),
                                                            sem("projected"), sem("added"), sem("based"))
        norm = Norm(nc, ctx, "l1n", stream, rows, 1e-6, centred=False)
        banks = [ctx.enter_context(nc.psum_tensor(f"l1_bank{i}", [P, BANK], F32)) for i in range(8)]

        def bank_of(uv, m, k):
            return 4 + (4 * (2 * uv + m) + k) % 4

        with nc.Block() as block:

            @block.sync
            def _(e):
                for dst, name in ((w_uv, "L1_w_uv"), (b_uv, "L1_b_uv"), (w_o, "L1_w_o"), (b_o, "L1_b_o")):
                    e.dma_start(dst[:], d[name]).then_inc(loaded, 16)

            @block.gpsimd
            def _(e):
                norm_gpsimd(e, norm)
                e.wait_ge(loaded, 64)
                e.tensor_tensor(base[:], stream[:], b_o[:].unsqueeze(1).to_broadcast([P, TILES, C]), ALU.add)\
                    .then_inc(based, 1)
                for m in range(CHUNKS):
                    for i, (axis, lag) in enumerate(PE_LAGS):
                        n = m * len(PE_LAGS) + i
                        if n >= NDIAG:
                            e.wait_ge(diag_used, n - NDIAG + 1)
                        at = lag + SIDE - 1
                        e.tensor_scalar(diag[:, n % NDIAG, :], ident[0:C, 0:C], coef[:, m, axis, at:at + 1], None,
                                        ALU.mult).then_inc(diag_ready, 1)

            @block.vector
            def _(e):
                norm_vector(e, norm)
                steps = 0
                for m in range(CHUNKS):
                    e.wait_ge(v_ready, NB * (m + 1))
                    for i, (axis, lag) in enumerate(DVE_LAGS):
                        at = lag + SIDE - 1
                        a = coef[:, m, axis, at:at + 1]
                        if i == 0:
                            assert lag in (6, -7)
                            e.memset(acc[:, m, :], 0.0).then_inc(acc_step, 1)
                            steps += 1
                        to, of = shifted(v, axis, lag)
                        if axis == 0:
                            row = lambda s, t: t[:, m, :].rearrange("p (b r) -> p b r", b=BATCH)[:, :, s.start * SIDE:s.stop * SIDE]
                        else:
                            row = lambda s, t: t[:, m, :].rearrange("p (b r) -> p b r", r=SIDE)[:, :, s]
                        e.wait_ge(acc_step, steps)
                        e.scalar_tensor_tensor(out=row(to, acc), in0=row(of, v), scalar=a, in1=row(to, acc),
                                               op0=ALU.mult, op1=ALU.add).then_inc(acc_step, 1)
                        steps += 1
                    e.wait_ge(acc_step, steps)
                    for k in range(NB):
                        cols = slice(k * BANK, (k + 1) * BANK)
                        e.wait_ge(conv_done, m + 1)
                        e.tensor_tensor(acc[:, m, cols], acc[:, m, cols], banks[4 * m + k][0:C, :], ALU.add)\
                            .then_inc(summed, 1)
                    e.wait_ge(summed, NB * (m + 1))
                    e.wait_ge(u_ready, NB * (m + 1))
                    e.tensor_tensor(v[:, m, :], acc[:, m, :], u[:, m, :], ALU.mult).then_inc(gated, 1)
                e.wait_ge(based, 1)
                for k in range(NB):
                    e.wait_ge(projected, k + 1)
                    e.tensor_tensor(stream[:, 4 * k:4 * k + 4, :], base[:, 4 * k:4 * k + 4, :],
                                    banks[k][:, 0:4 * C].rearrange("p (t c) -> p t c", c=C), ALU.add)\
                        .then_inc(added, 1)

            @block.scalar
            def _(e):
                for k in range(NB):
                    e.wait_ge(turned, 4 * k + 4)
                    e.activation(xT[:, k * BANK:(k + 1) * BANK], banks[k][0:C, :], ACT.Copy).then_inc(copied, 1)
                e.wait_ge(loaded, 64)
                n = 0
                for uv in (1, 0):
                    for m in range(CHUNKS):
                        for k in range(NB):
                            n += 1
                            e.wait_ge(uv_done, n)
                            out = (u if uv == 0 else v)[:, m, k * BANK:(k + 1) * BANK]
                            e.activation(out, banks[4 + (n - 1) % 4][0:C, :], ACT.Silu, bias=b_uv[:, uv, m:m + 1])\
                                .then_inc(u_ready if uv == 0 else v_ready, 1)

            @block.tensor
            def _(e):
                transposes(e, norm, ident, banks, turned)
                e.wait_ge(loaded, 64)
                e.wait_ge(copied, NB)
                n = 0
                for uv in (1, 0):
                    for m in range(CHUNKS):
                        for k in range(NB):
                            if n >= 4:
                                done = n - 3
                                e.wait_ge(v_ready, min(done, CHUNKS * NB))
                                if done > CHUNKS * NB:
                                    e.wait_ge(u_ready, done - CHUNKS * NB)
                            e.matmul(banks[4 + n % 4][0:C, :], w_uv[:, uv, m * C:(m + 1) * C],
                                     xT[:, k * BANK:(k + 1) * BANK], start=True, stop=True).then_inc(uv_done, 1)
                            n += 1
                e.wait_ge(v_ready, CHUNKS * NB)
                e.wait_ge(u_ready, CHUNKS * NB)
                for m in range(CHUNKS):
                    for i, (axis, lag) in enumerate(PE_LAGS):
                        e.wait_ge(diag_ready, m * len(PE_LAGS) + i + 1)
                        to, of = shifted(v, axis, lag)
                        for k in range(NB):
                            src = v[:, m, k * BANK:(k + 1) * BANK]
                            dst = banks[4 * m + k][0:C, :]
                            if axis == 0:
                                row = lambda s, t: t.rearrange("p (b r) -> p b r", b=2)[:, :, s.start * SIDE:s.stop * SIDE]
                            else:
                                row = lambda s, t: t.rearrange("p (b r) -> p b r", r=SIDE)[:, :, s]
                            last = e.matmul(row(to, dst), diag[:, (m * len(PE_LAGS) + i) % NDIAG, :], row(of, src),
                                            start=(i == 0), stop=(i == len(PE_LAGS) - 1))
                        last.then_inc(diag_used, 1)
                    e.wait_ge(diag_used, (m + 1) * len(PE_LAGS))
                    e.sem_inc(conv_done, 1)
                e.wait_ge(gated, CHUNKS)
                for k in range(NB):
                    for t in range(4):
                        tile = 4 * k + t
                        for m in range(CHUNKS):
                            last = e.matmul(banks[k][:, t * C:(t + 1) * C], v[:, m, tile * P:(tile + 1) * P], w_o[:, m, :],
                                            start=(m == 0), stop=(m == CHUNKS - 1))
                    last.then_inc(projected, 1)


class GruWeights:

    def __init__(self, nc, ctx):
        sb = lambda n, shape, dt: ctx.enter_context(nc.sbuf_tensor("gru_" + n, shape, dt))
        n = len(GRUS) * GATES
        self.hidden_raw = sb("hidden_raw", [C, n, P], F32)
        self.input_raw = sb("input_raw", [C + 2, CHUNKS, n, P], F32)
        self.bias_raw = sb("bias_raw", [C + 2, len(GRUS), P], F32)
        self.hidden = sb("hidden", [C, 2, n, P], F16)
        self.input = sb("input", [C + 2, 2, CHUNKS, n, P], F16)
        self.bias = sb("bias", [C + 2, 2, len(GRUS), P], F16)
        self.loaded = ctx.enter_context(nc.semaphore("gru_loaded"))
        self.raw_free = ctx.enter_context(nc.semaphore("gru_raw_free"))

    def pairs(self):
        return ((self.hidden_raw[:], self.hidden), (self.input_raw[:], self.input), (self.bias_raw[:], self.bias))

    def load(self, e, d, layer):
        for dst, name in ((self.hidden_raw, "whh"), (self.input_raw, "wih"), (self.bias_raw, "bhn")):
            e.dma_start(dst[:], d[f"{layer}_{name}"]).then_inc(self.loaded, 16)


def gru_layer(nc, d, layer, nth, stream, ident, weights, out_dram=None):
    with ExitStack() as outer:
        sbo = lambda n, shape, dt=F32: outer.enter_context(nc.sbuf_tensor(f"{layer}_{n}", shape, dt))
        gate = sbo("gate", [C, CHUNKS, TOKENS])
        history = sbo("history", [C, SEQ, GROUPS, PER])
        w_out = sbo("w_out", [C, CHUNKS, C])
        w_loaded = outer.enter_context(nc.semaphore(f"{layer}_w_loaded"))
        with ExitStack() as ctx:
            sb = lambda n, shape, dt=F32: ctx.enter_context(nc.sbuf_tensor(f"{layer}_{n}", shape, dt))
            forward = sb("forward", [C + 2, 2, CHUNKS, SEQ + STEPS, BATCH], F16)
            backward = sb("backward", [C + 2, 2, CHUNKS, SEQ + STEPS, BATCH], F16)
            gru_input(nc, d, layer, nth, stream, ident, weights, forward, backward, gate, w_out, w_loaded)
            gru_steps(nc, layer, weights, forward, backward, history)
        gru_output(nc, layer, stream, gate, history, w_out, w_loaded, out_dram)


def gru_input(nc, d, layer, nth, stream, ident, weights, forward, backward, gate, w_out, w_loaded):
    with ExitStack() as ctx:
        sb = lambda n, shape, dt=F32: ctx.enter_context(nc.sbuf_tensor(f"{layer}i_{n}", shape, dt))
        sem = lambda n: ctx.enter_context(nc.semaphore(f"{layer}i_{n}"))
        NB = TOKENS // BANK
        TB = BANK // BATCH
        rows = sb("rows", [P, TILES, C])
        xT = sb("xT", [C, SEQ, BATCH])
        w_in = sb("w_in", [C, 2 * D1])
        affine = sb("affine", [C, 2])
        loaded, turned, scaled, projected = sem("loaded"), sem("turned"), sem("scaled"), sem("projected")
        hi_ready, lo_ready, gate_ready, filled, split, reversed_ = (sem("hi_ready"), sem("lo_ready"), sem("gate_ready"),
                                                                    sem("filled"), sem("split"), sem("reversed"))
        norm = Norm(nc, ctx, f"{layer}n", stream, rows, 1e-5)
        banks = [ctx.enter_context(nc.psum_tensor(f"{layer}i_bank{i}", [P, BANK], F32)) for i in range(8)]
        order = [(m, k) for m in range(CHUNKS) for k in range(NB)] + [(CHUNKS + m, k) for m in range(CHUNKS) for k in range(NB)]
        INNER = CHUNKS * NB
        with nc.Block() as block:

            @block.sync
            def _(e):
                e.dma_start(w_in[:], d[f"{layer}_w_in"]).then_inc(loaded, 16)
                e.dma_start(affine[:], d[f"{layer}_ln"]).then_inc(loaded, 16)
                e.dma_start(w_out[:], d[f"{layer}_w_out"]).then_inc(w_loaded, 16)

            @block.gpsimd
            def _(e):
                e.memset(forward[:], 0.0).then_inc(filled, 1)
                e.memset(backward[:], 0.0).then_inc(filled, 1)
                e.wait_ge(filled, 2)
                for x in (forward, backward):
                    e.memset(x[C:C + 2, 0, 1, :, :], 1.0).then_inc(filled, 1)
                e.wait_ge(filled, 4)
                norm_gpsimd(e, norm)
                e.wait_ge(weights.loaded, 48 * nth)
                for i, (raw, parts) in enumerate(weights.pairs()):
                    e.tensor_scalar(parts[:, 0], raw, F16_MAX, -F16_MAX, ALU.min, ALU.max).then_inc(split, 1)
                    e.wait_ge(split, 2 * i + 1)
                    e.tensor_tensor(parts[:, 1], raw, parts[:, 0], ALU.subtract).then_inc(split, 1)
                e.wait_ge(split, 6)
                e.sem_inc(weights.raw_free, 1)

            @block.vector
            def _(e):
                norm_vector(e, norm)
                for i, (m, k) in enumerate(order[:INNER]):
                    cols = slice(k * TB, (k + 1) * TB)
                    e.wait_ge(hi_ready, i + 1)
                    e.tensor_tensor(forward[0:C, 1, m, cols, :], banks[4 + i % 4][0:C, :].rearrange("p (t b) -> p t b", b=BATCH),
                                    forward[0:C, 0, m, cols, :], ALU.subtract).then_inc(lo_ready, 1)
                e.wait_ge(lo_ready, INNER)
                for part in range(2):
                    for m in range(CHUNKS):
                        e.tensor_copy(backward[0:C, part, m, 0:SEQ, :], forward[0:C, part, m, SEQ - 1::-1, :]).then_inc(reversed_, 1)

            @block.scalar
            def _(e):
                e.wait_ge(loaded, 32)
                e.wait_ge(filled, 4)
                for k in range(NB):
                    e.wait_ge(turned, 4 * k + 4)
                    e.activation(xT[:].rearrange("p t b -> p b t")[:, 2 * k:2 * k + 2, :],
                                 banks[k][0:C, :].rearrange("p (b t) -> p b t", b=2), ACT.Identity,
                                 scale=affine[:, 0:1], bias=affine[:, 1:2]).then_inc(scaled, 1)
                for i, (m, k) in enumerate(order):
                    e.wait_ge(projected, i + 1)
                    src = banks[4 + i % 4][0:C, :]
                    if m < CHUNKS:
                        e.activation(forward[0:C, 0, m, k * TB:(k + 1) * TB, :], src.rearrange("p (t b) -> p t b", b=BATCH),
                                     ACT.Copy).then_inc(hi_ready, 1)
                    else:
                        e.activation(gate[:, m - CHUNKS, k * BANK:(k + 1) * BANK], src, ACT.Silu).then_inc(gate_ready, 1)

            @block.tensor
            def _(e):
                transposes(e, norm, ident, banks, turned)
                e.wait_ge(loaded, 32)
                e.wait_ge(scaled, NB)
                x_all = flat(xT[:])
                for i, (m, k) in enumerate(order):
                    if i >= 4:
                        done = i - 3
                        e.wait_ge(lo_ready, min(done, INNER))
                        if done > INNER:
                            e.wait_ge(gate_ready, done - INNER)
                    e.matmul(banks[4 + i % 4][0:C, :], w_in[:, m * C:(m + 1) * C], x_all[:, k * BANK:(k + 1) * BANK],
                             start=True, stop=True).then_inc(projected, 1)


def gru_steps(nc, layer, weights, forward, backward, history):
    with ExitStack() as ctx:
        sb = lambda n, shape, dt=F32: ctx.enter_context(nc.sbuf_tensor(f"{layer}s_{n}", shape, dt))
        sem = lambda n: ctx.enter_context(nc.semaphore(f"{layer}s_{n}"))
        pairs = lambda n, shape, dt=F32: [sb(f"{n}{g}", shape, dt) for g in range(GROUPS)]
        each = lambda n: [sem(f"{n}{g}") for g in range(GROUPS)]
        ones = sb("ones", [C + 2, STEPS * BATCH], F16)
        reset = pairs("reset", [C, 2, PER, 2])
        cand = pairs("cand", [C, 2, PER, 2])
        update = pairs("update", [C, 2, PER, 3])
        WIDE = 3 * PER
        terms = pairs("terms", [C, RING, WIDE + 2])
        h_hi = pairs("h_hi", [C, 2, PER, 3], F16)
        h_lo = pairs("h_lo", [C, 2, PER], F16)
        rz = [[ctx.enter_context(nc.psum_tensor(f"{layer}s_rz{g}{p}", [P, STEPS, 2, PER], F32)) for p in range(2)] for g in range(GROUPS)]
        nn = [[ctx.enter_context(nc.psum_tensor(f"{layer}s_nn{g}{p}", [P, STEPS, PER, 2], F32)) for p in range(2)] for g in range(GROUPS)]
        prepared = sem("prepared")
        gates_summed, reset_ready = each("gates_summed"), each("reset_ready")
        cand_ready, tanh_ready = each("cand_ready"), each("tanh_ready")
        hi_ready, state_ready, lo_ready = each("hi_ready"), each("state_ready"), each("lo_ready")
        chunk_done, chunk_saved, ring_free = sem("chunk_done"), sem("chunk_saved"), sem("ring_free")
        PREPARED = 2 + 5 * GROUPS + 2 * GROUPS
        TURNS = SEQ // RING
        ring_of = lambda g, q: terms[g][:, q % RING, :]

        with nc.Block() as block:

            @block.vector
            def _(e):
                done = 0

                def prepare(ins):
                    nonlocal done
                    done += 1
                    ins.then_inc(prepared, 1)
                    e.wait_ge(prepared, done)

                prepare(e.memset(ones[:], 0.0))
                prepare(e.memset(ones[C:C + 2, :], 1.0))
                for g in range(GROUPS):
                    for buffer in (reset[g], update[g], terms[g], h_hi[g], h_lo[g]):
                        prepare(e.memset(buffer[:], 0.0))
                for g in range(GROUPS):
                    for x in range(2):
                        prepare(e.memset(update[g][:, x, :, 1], -1.0))
                for s in (state_ready[1], hi_ready[0], hi_ready[1], lo_ready[0]):
                    e.sem_inc(s, 1)

                def candidate(g, q):
                    p, s = divmod(q, STEPS)
                    x = q % 2
                    e.wait_ge(reset_ready[g], q + 1)
                    e.tensor_tensor_scan(flat(cand[g][:, x]), flat(reset[g][:, x]), flat(nn[g][p][0:C, s]), 0.0,
                                         ALU.mult, ALU.add).then_inc(cand_ready[g], 1)

                def new_state(g, q):
                    x = q % 2
                    e.wait_ge(tanh_ready[g], q + 1)
                    e.tensor_tensor_scan(flat(h_hi[g][:, x]), flat(update[g][:, x]), ring_of(g, q)[:, 1:1 + WIDE], 0.0,
                                         ALU.mult, ALU.add).then_inc(hi_ready[g], 1)
                    e.tensor_tensor_scan(ring_of(g, q + 1)[:, 0:WIDE], flat(update[g][:, x]), ring_of(g, q)[:, 1:1 + WIDE], 0.0,
                                         ALU.mult, ALU.add).then_inc(state_ready[g], 1)

                def rest(g, q, count):
                    e.wait_ge(state_ready[g], count)
                    e.tensor_tensor(h_lo[g][:, q % 2], ring_of(g, q + 1)[:, 2:2 + WIDE:3], h_hi[g][:, q % 2, :, 2],
                                    ALU.subtract).then_inc(lo_ready[g], 1)

                with e.Fori(0, TURNS):
                    for q in range(RING):
                        if q % STEPS == 0:
                            e.wait_ge(ring_free, q // STEPS + 1)
                        candidate(0, q)
                        rest(1, q - 1, q + 1)
                        if q % STEPS == 0:
                            e.sem_inc(chunk_done, 1)
                        new_state(0, q)
                        rest(0, q, q + 1)
                        candidate(1, q)
                        new_state(1, q)
                    for s in (*reset_ready, *tanh_ready, *state_ready):
                        e.sem_inc(s, -RING)
                    e.sem_inc(ring_free, -2)
                rest(1, -1, 1)
                e.sem_inc(chunk_done, 1)

            @block.scalar
            def _(e):
                e.wait_ge(prepared, PREPARED)
                with e.Fori(0, TURNS):
                    for q in range(RING):
                        p, s = divmod(q, STEPS)
                        x = q % 2
                        for g in range(GROUPS):
                            e.wait_ge(gates_summed[g], q + 1)
                            e.activation(reset[g][:, x, :, 1], rz[g][p][0:C, s, 0], ACT.Sigmoid).then_inc(reset_ready[g], 1)
                            e.activation(update[g][:, x, :, 2], rz[g][p][0:C, s, 1], ACT.Sigmoid)
                            e.wait_ge(cand_ready[g], q + 1)
                            places = ring_of(g, q)[:, 1:1 + WIDE].rearrange("p (a b) -> p a b", b=3)[:, :, 0::2]
                            e.activation(places, cand[g][:, x, :, 1:2].to_broadcast([C, PER, 2]), ACT.Tanh)\
                                .then_inc(tanh_ready[g], 1)
                    for s in (*gates_summed, *cand_ready):
                        e.sem_inc(s, -RING)

            @block.gpsimd
            def _(e):
                e.sem_inc(ring_free, 2)
                with e.Fori(0, TURNS) as turn:
                    for p in range(2):
                        chunk = turn * 2 + p
                        first = chunk * STEPS
                        e.wait_ge(chunk_done, chunk + 2)
                        for g in range(GROUPS):
                            e.tensor_copy(history[:, bass.ds(first, STEPS - 1), g, :],
                                          terms[g][:, p * STEPS + 1:(p + 1) * STEPS, 2:2 + WIDE:3])
                            last = e.tensor_copy(history[:, bass.ds(first + STEPS - 1, 1), g, :],
                                                 terms[g][:, (p + 1) * STEPS % RING, None, 2:2 + WIDE:3])
                        last.then_inc(chunk_saved, 1)
                        e.wait_ge(chunk_saved, chunk + 1)
                        e.sem_inc(ring_free, 1)

            @block.tensor
            def _(e):
                def inputs(p, chunk):
                    out = []
                    cols = bass.ds(chunk * (STEPS * BATCH), STEPS * BATCH)
                    for gru in range(len(GRUS)):
                        g, j = divmod(gru, 2)
                        source = forward if gru < 2 else backward
                        mine = slice(j * BATCH, (j + 1) * BATCH)

                        def share(dst, gate, first):
                            for m in range(CHUNKS):
                                rows = C + 2 if m else C
                                for wp, xp in ((0, 0), (1, 0), (0, 1)):
                                    lhsT = weights.input[0:rows, wp, m, GATES * gru + gate, :]
                                    rhs = source[0:rows, xp, m].rearrange("p t b -> p (t b)")[:, cols]
                                    start = first and m == 0 and (wp, xp) == (0, 0)
                                    out.append((dst, lhsT, rhs, start))

                        share(rz[g][p][:, :, 0, mine], 0, j == 0)
                        share(rz[g][p][:, :, 1, mine], 1, False)
                        for wp in range(2):
                            out.append((nn[g][p][:, :, mine, 0], weights.bias[:, wp, gru, :], ones[:], j == 0 and wp == 0))
                        share(nn[g][p][:, :, mine, 1], 2, False)
                    return out

                def run(product):
                    dst, lhsT, rhs, start = product
                    return e.matmul(dst, lhsT, rhs, start=start, stop=False, skip_group_check=True)

                e.wait_ge(prepared, PREPARED)
                for product in inputs(0, 0):
                    run(product)
                with e.Fori(0, TURNS) as turn:
                    for q in range(RING):
                        p, s = divmod(q, STEPS)
                        x = (q + 1) % 2
                        if s == 0:
                            ahead = inputs(1 - p, turn * 2 + (p + 1))
                            step_share = len(ahead) / (STEPS * GROUPS)
                            sent = 0
                        for g in range(GROUPS):
                            def add(gate, wp, xp, j):
                                mine = slice(j * BATCH, (j + 1) * BATCH)
                                rhs = h_lo[g][:, x, mine] if xp else h_hi[g][:, x, mine, 2]
                                dst = nn[g][p][:, s, mine, 0] if gate == 2 else rz[g][p][:, s, gate, mine]
                                return e.matmul(dst, weights.hidden[:, wp, GATES * (2 * g + j) + gate, :], rhs,
                                                start=False, stop=False, skip_group_check=True)

                            e.wait_ge(hi_ready[g], q + 1)
                            for gate in range(GATES):
                                for j in range(2):
                                    add(gate, 0, 0, j)
                                    add(gate, 1, 0, j)
                            e.wait_ge(lo_ready[g], q + 1)
                            for gate in (2, 0, 1):
                                for j in range(2):
                                    last = add(gate, 0, 1, j)
                            last.then_inc(gates_summed[g], 1)
                            due = round((2 * s + g + 1) * step_share)
                            for product in ahead[sent:due]:
                                run(product)
                            sent = due
                    for s in (*hi_ready, *lo_ready):
                        e.sem_inc(s, -RING)


def gru_output(nc, layer, stream, gate, history, w_out, w_loaded, out_dram):
    with ExitStack() as ctx:
        sb = lambda n, shape, dt=F32: ctx.enter_context(nc.sbuf_tensor(f"{layer}o_{n}", shape, dt))
        sem = lambda n: ctx.enter_context(nc.semaphore(f"{layer}o_{n}"))
        NB = TOKENS // BANK
        y = sb("y", [C, CHUNKS, SEQ, BATCH])
        s_tok = sb("s_tok", [C, CHUNKS, BATCH, SEQ])
        summed, silu_done, gated, projected, added, stored = (sem("summed"), sem("silu_done"), sem("gated"),
                                                             sem("projected"), sem("added"), sem("stored"))
        banks = [ctx.enter_context(nc.psum_tensor(f"{layer}o_bank{i}", [P, BANK], F32)) for i in range(NB)]
        hist = history[:].rearrange("p t g (j b) -> p t g j b", b=BATCH)
        mates = [((0, 0), (1, 1)), ((0, 1), (1, 0))]
        with nc.Block() as block:

            @block.vector
            def _(e):
                for m in range(CHUNKS):
                    (g0, j0), (g1, j1) = mates[m]
                    e.tensor_tensor(y[:, m], hist[:, :, g0, j0, :], hist[:, SEQ - 1::-1, g1, j1, :], ALU.add).then_inc(summed, 1)
                for m in range(CHUNKS):
                    for h in range(2):
                        t = slice(h * P, (h + 1) * P)
                        e.wait_ge(silu_done, 2 * m + h + 1)
                        e.tensor_tensor(s_tok[:, m].rearrange("p b t -> p t b")[:, t, :], y[:, m, t, :],
                                        gate[:, m, h * P * BATCH:(h + 1) * P * BATCH].rearrange("p (t b) -> p t b", b=BATCH),
                                        ALU.mult).then_inc(gated, 1)
                for k in range(NB):
                    e.wait_ge(projected, k + 1)
                    e.tensor_tensor(stream[:, 4 * k:4 * k + 4, :], stream[:, 4 * k:4 * k + 4, :],
                                    banks[k][:, 0:4 * C].rearrange("p (t c) -> p t c", c=C), ALU.add).then_inc(added, 1)

            @block.scalar
            def _(e):
                for m in range(CHUNKS):
                    e.wait_ge(summed, m + 1)
                    for h in range(2):
                        part = y[:, m, h * P:(h + 1) * P, :]
                        e.activation(part, part, ACT.Silu).then_inc(silu_done, 1)

            @block.tensor
            def _(e):
                e.wait_ge(w_loaded, 16)
                e.wait_ge(gated, 2 * CHUNKS)
                for k in range(NB):
                    for t in range(4):
                        b, half = divmod(4 * k + t, HALVES)
                        for m in range(CHUNKS):
                            last = e.matmul(banks[k][:, t * C:(t + 1) * C], s_tok[:, m, b, half * P:(half + 1) * P], w_out[:, m, :],
                                            start=(m == 0), stop=(m == CHUNKS - 1))
                    last.then_inc(projected, 1)

            if out_dram is not None:
                @block.sync
                def _(e):
                    for k in range(NB):
                        e.wait_ge(added, k + 1)
                        e.dma_start(out_dram[:, 4 * k:4 * k + 4, :], stream[:, 4 * k:4 * k + 4, :]).then_inc(stored, 16)
                    e.wait_ge(stored, 16 * NB)


def build(nc, d, out):
    with ExitStack() as ctx:
        stream = ctx.enter_context(nc.sbuf_tensor("stream", [P, TILES, C], F32))
        ident = ctx.enter_context(nc.sbuf_tensor("ident", [P, P], F32))
        coef = ctx.enter_context(nc.sbuf_tensor("coef", [C, CHUNKS, 2, LAGS], F32))
        loaded_x = ctx.enter_context(nc.semaphore("loaded_x"))
        with ExitStack() as first:
            ones = first.enter_context(nc.sbuf_tensor("ones", [P, P], F32))
            with nc.Block() as block:

                @block.sync
                def _(e):
                    e.dma_start(ones[:], d["mean"]).then_inc(loaded_x, 16)
                    e.dma_start(ident[:], d["ident"]).then_inc(loaded_x, 16)
                    e.dma_start(stream[:], d["x"].rearrange("(t p) c -> p t c", p=P)).then_inc(loaded_x, 16)

                @block.tensor
                def _(e):
                    e.wait_ge(loaded_x, 48)

            coefficients(nc, d, coef, ones)
        fourier(nc, d, stream, ident, loaded_x, 48)
        weights = GruWeights(nc, ctx)
        with nc.Block() as block:

            @block.sync
            def _(e):
                weights.load(e, d, "L2")

        toeplitz(nc, d, stream, ident, coef)
        gru_layer(nc, d, "L2", 1, stream, ident, weights)
        with nc.Block() as block:

            @block.sync
            def _(e):
                e.wait_ge(weights.raw_free, 1)
                weights.load(e, d, "L3")

        gru_layer(nc, d, "L3", 2, stream, ident, weights, out.rearrange("(t p) c -> p t c", p=P))


def constants():
    h, w = np.divmod(np.arange(SEQ), SIDE)
    kh, kw = np.divmod(np.arange(FREQS), KW)
    turns = ((np.outer(h, kh) + np.outer(w, kw)) % SIDE) * (2 * np.pi / SIDE)
    dft = np.stack([np.cos(turns), -np.sin(turns)], axis=2) / SIDE
    dft = dft.reshape(HALVES, P, 2 * FREQS).transpose(1, 0, 2)
    twice = np.where((kw == 0) | (kw == SIDE // 2), 1.0, 2.0)
    idft = np.stack([np.cos(turns) * twice, -np.sin(turns) * twice], axis=2) / SIDE
    idft = idft.reshape(HALVES, P, QUARTERS, FQ, 2).transpose(3, 2, 4, 0, 1)
    mask = np.kron(np.eye(BLOCKS), np.ones((BLOCK, 1)))
    pos = np.broadcast_to(np.arange(1 - SIDE, SIDE), (RPE, LAGS))
    return {
        "dft": dft, "idft": idft.reshape(FQ, QUARTERS * 2 * HALVES, P), "mask": mask, "pos": pos,
        "ident": np.eye(P), "mean": np.full((P, P), 1.0 / RPE),
    }


def layouts(i):
    f = lambda n: np.asarray(i[n])
    by_part = lambda v: v.reshape(-1, C).T
    d = {"x": f("x").reshape(TOKENS, C)}
    d["L0_w1"] = f("L0_conv_w1").transpose(2, 3, 0, 1, 4, 5).reshape(C, FREQS * COMPLEX)
    b1 = f("L0_conv_b1").reshape(QUARTERS, FQ, BLOCKS, COMPLEX).transpose(0, 3, 1, 2)
    bias = np.zeros((QUARTERS, 32, FQ, BLOCKS), b1.dtype)
    bias[:, :COMPLEX] = b1
    d["L0_b1"] = bias.reshape(P, FQ * BLOCKS)
    d["L0_norm1"] = np.stack([f("L0_conv_norm1_w"), f("L0_conv_norm1_b")], axis=1)
    d["L0_norm2"] = np.stack([f("L0_conv_norm2_w"), f("L0_conv_norm2_b")], axis=1)
    d["L0_mlp_w1"] = f("L0_conv_mlp_w1")
    d["L0_mlp_b1"] = f("L0_conv_mlp_b1").reshape(-1, P).T
    d["L0_mlp_w2"] = f("L0_conv_mlp_w2").reshape(-1, P, C).transpose(1, 0, 2)
    d["L0_mlp_b2"] = np.broadcast_to(f("L0_conv_mlp_b2"), (P, C))
    d["L1_w_uv"] = np.stack([f("L1_conv_Wu"), f("L1_conv_Wv")], axis=1)
    d["L1_b_uv"] = np.stack([by_part(f("L1_conv_bu")), by_part(f("L1_conv_bv"))], axis=1)
    d["L1_w_o"] = f("L1_conv_Wo").reshape(CHUNKS, C, C).transpose(1, 0, 2)
    d["L1_b_o"] = np.broadcast_to(f("L1_conv_bo"), (P, C))
    nets = ("r2", "r1")
    g = lambda r, n: f(f"L1_conv_{r}_{n}")
    d["rpe_small"] = np.stack([np.concatenate([g(r, "pw"), g(r, "pb")[None], g(r, "lb")]).T for r in nets], axis=1)
    d["rpe_lw"] = np.stack([g(r, "lw").transpose(1, 0, 2).reshape(RPE, -1) for r in nets], axis=1)
    d["rpe_ow"] = np.stack([g(r, "ow") for r in nets], axis=1)
    d["rpe_ob"] = np.stack([by_part(g(r, "ob")) for r in nets], axis=1)
    for layer in ("L2", "L3"):
        w = lambda gru, n: f(f"{layer}_conv_" + gru % n)
        n = len(GRUS)
        whh = np.zeros((C, n, GATES, P), np.float32)
        wih = np.zeros((C + 2, CHUNKS, n, GATES, P), np.float32)
        bhn = np.zeros((C + 2, n, P), np.float32)
        for k, gru in enumerate(GRUS):
            whh[:, k, :, :C] = w(gru, "whh").reshape(GATES, C, C).transpose(2, 0, 1)
            wih[:C, :, k, :, :C] = w(gru, "wih").reshape(GATES, C, CHUNKS, C).transpose(3, 2, 0, 1)
            wih[C, 1, k, :, :C] = w(gru, "bih").reshape(GATES, C)
            wih[C + 1, 1, k, :2, :C] = w(gru, "bhh").reshape(GATES, C)[:2]
            bhn[C + 1, k, :C] = w(gru, "bhh").reshape(GATES, C)[2]
        d[f"{layer}_whh"], d[f"{layer}_wih"], d[f"{layer}_bhn"] = whh.reshape(C, n * GATES, P), wih.reshape(C + 2, CHUNKS, n * GATES, P), bhn
        d[f"{layer}_w_in"] = f(f"{layer}_conv_w_in").T
        d[f"{layer}_w_out"] = f(f"{layer}_conv_w_out").reshape(C, CHUNKS, C).transpose(2, 1, 0)
        d[f"{layer}_ln"] = np.stack([f(f"{layer}_conv_ln_g"), f(f"{layer}_conv_ln_b")], axis=1)
    return d


def kernel(**inputs):
    import concourse.bacc as bacc
    from concourse.bass_utils import run_bass_kernel_spmd

    nc = bacc.Bacc("TRN2", target_bir_lowering=False, num_devices=1)
    arrays = {n: np.ascontiguousarray(a) for n, a in layouts(inputs).items()}
    arrays |= {n: np.ascontiguousarray(a, np.float32) for n, a in constants().items()}
    dram = {n: nc.dram_tensor(f"in_{n}", list(a.shape), F32, kind="ExternalInput").ap() for n, a in arrays.items()}
    out = nc.dram_tensor("out", [TOKENS, C], F32, kind="ExternalOutput").ap()
    build(nc, dram, out)
    r = run_bass_kernel_spmd(nc, [{f"in_{n}": a for n, a in arrays.items()}], core_ids=[0])
    return r.results[0]["out"].reshape(BATCH, SIDE, SIDE, C)
```

```python
from contextlib import ExitStack

import numpy as np

import concourse.bass as bass
from concourse import mybir

F32 = mybir.dt.float32
F16 = mybir.dt.float16
ALU = mybir.AluOpType
ACT = mybir.ActivationFunctionType

P = 128
BATCH, SIDE, C = 8, 16, 96
SEQ = SIDE * SIDE
TOKENS = BATCH * SEQ
TILES = TOKENS // P
HALVES = SEQ // P
BANK = 512

KW = SIDE // 2 + 1
FREQS = SIDE * KW
BLOCKS = 8
BLOCK = C // BLOCKS
QUARTERS = 4
FQ = FREQS // QUARTERS
COMPLEX = 2 * BLOCK
HIDDEN = 4 * C

CHUNKS = 2
D1 = CHUNKS * C
LAGS = 2 * SIDE - 1
RPE = 128
DEPTH = 3

GRUS = ("f_%s_fw", "b_%s_rv", "f_%s_rv", "b_%s_fw")
GATES = 3
STEPS = 16
CHUNK_COUNT = SEQ // STEPS
RING = 2 * STEPS
GROUPS = 2
AFTER_0 = 0.6
PER = 2 * BATCH


def flat(ap):
    return ap.rearrange("p a b -> p (a b)")


def split_tokens(ap):
    return ap.rearrange("p (b t) -> p b t", b=BATCH)


class Norm:

    def __init__(self, nc, ctx, name, stream, out, eps, centred=True):
        sb = lambda n, shape: ctx.enter_context(nc.sbuf_tensor(f"{name}_{n}", shape, F32))
        sem = lambda n: ctx.enter_context(nc.semaphore(f"{name}_{n}"))
        self.stream, self.out, self.eps, self.centred = stream, out, eps, centred
        self.stats = sb("stats", [P, TILES, 6])
        self.moments = sb("moments", [P, TILES, 2])
        self.power = sb("power", [P, TILES])
        self.exponent = sb("exponent", [P, TILES])
        self.guess = sb("guess", [P, TILES])
        self.work = sb("work", [P, TILES])
        self.rstd = sb("rstd", [P, TILES])
        self.chained = sem("chained")
        self.power_ready = sem("power_ready")
        self.guess_ready = sem("guess_ready")
        self.rows_ready = sem("rows_ready")


def norm_vector(e, n):
    count = 0

    def link(ins):
        nonlocal count
        count += 1
        ins.then_inc(n.chained, 1)
        e.wait_ge(n.chained, count)

    e.memset(n.exponent[:], -0.5).then_inc(n.power_ready, 1)
    for i in range(TILES):
        last = e.bn_stats(n.stats[:, i, :], n.stream[:, i, :])
    link(last)
    for i in range(TILES):
        last = e.bn_aggr(n.moments[:, i, :], n.stats[:, i, :])
    link(last)
    if n.centred:
        e.tensor_scalar(n.power[:], n.moments[:, :, 1], n.eps, None, ALU.add).then_inc(n.power_ready, 1)
    else:
        link(e.tensor_tensor(n.work[:], n.moments[:, :, 0], n.moments[:, :, 0], ALU.mult))
        e.scalar_tensor_tensor(out=n.power[:], in0=n.moments[:, :, 1], scalar=n.eps, in1=n.work[:],
                               op0=ALU.add, op1=ALU.add).then_inc(n.power_ready, 1)
    e.wait_ge(n.power_ready, 2)
    e.wait_ge(n.guess_ready, 1)
    link(e.tensor_tensor(n.work[:], n.guess[:], n.guess[:], ALU.mult))
    link(e.tensor_tensor(n.work[:], n.work[:], n.power[:], ALU.mult))
    link(e.tensor_scalar(n.work[:], n.work[:], -0.5, 1.5, ALU.mult, ALU.add))
    link(e.tensor_tensor(n.rstd[:], n.work[:], n.guess[:], ALU.mult))
    for i in range(TILES):
        row = n.stream[:, i, :]
        if n.centred:
            ins = e.tensor_scalar(n.out[:, i, :], row, n.moments[:, i, 0:1], n.rstd[:, i:i + 1],
                                  ALU.subtract, ALU.mult)
        else:
            ins = e.tensor_scalar(n.out[:, i, :], row, n.rstd[:, i:i + 1], None, ALU.mult)
        ins.then_inc(n.rows_ready, 1)


def norm_gpsimd(e, n):
    e.wait_ge(n.power_ready, 2)
    e.tensor_tensor(n.guess[:], n.power[:], n.exponent[:], ALU.pow).then_inc(n.guess_ready, 1)


def transposes(e, n, ident, banks, turned):
    for i in range(TILES):
        e.wait_ge(n.rows_ready, i + 1)
        e.transpose(banks[i // 4][0:C, (i % 4) * P:(i % 4 + 1) * P], n.out[:, i, :], ident[:]).then_inc(turned, 1)


def fourier(nc, d, stream, ident, loaded_x, x_bytes):
    with ExitStack() as ctx:
        sb = lambda n, shape, dt=F32: ctx.enter_context(nc.sbuf_tensor("l0_" + n, shape, dt))
        sem = lambda n: ctx.enter_context(nc.semaphore("l0_" + n))
        w_raw = sb("w_raw", [C, FREQS * COMPLEX])
        w_for = [sb("w_for_re", [C, FREQS, 32]), sb("w_for_im", [C, FREQS, 32])]
        bias = sb("bias", [P, FQ * BLOCKS])
        dft = sb("dft", [P, HALVES, 2 * FREQS])
        idft = sb("idft", [FQ, QUARTERS * 2 * HALVES, P])
        mask = sb("mask", [C, BLOCKS])
        affine = sb("affine", [C, 2])
        rows = sb("rows", [P, TILES, C])
        spectrum = sb("spectrum", [C, 2 * FREQS, BATCH])
        spread = sb("spread", [C, 2 * FREQS, BLOCKS, BATCH])
        mixed = sb("mixed", [P, BLOCKS * BATCH, FQ])
        by_freq = spread[0:FQ].rearrange("p f n b -> p (f n b)")[:, 0:BATCH * BLOCKS * QUARTERS * COMPLEX]\
            .rearrange("p (b n m) -> p b n m", b=BATCH, n=BLOCKS)
        shift0 = sb("shift0", [C, 1])
        loaded = sem("loaded")
        w_loaded = sem("w_loaded")
        chained = sem("chained")
        w_ready = sem("w_ready")
        w_steps = sem("w_steps")
        transformed = sem("transformed")
        evacuated = sem("evacuated")
        shifted = sem("shifted")
        spread_ready = sem("spread_ready")
        products = sem("products")
        biased = sem("biased")
        relu_done = sem("relu_done")
        turned = sem("turned")
        turn_saved_v = sem("turn_saved_v")
        turn_saved_s = sem("turn_saved_s")
        inverted = sem("inverted")
        stream_s = sem("stream_s")
        xs_ready = sem("xs_ready")
        norm = Norm(nc, ctx, "l0n", stream, rows, 1e-5)
        spatial = sb("spatial", [P, TILES, C])
        residual = sb("residual", [P, TILES, C])

        banks = [ctx.enter_context(nc.psum_tensor(f"l0_bank{i}", [P, BANK], F32)) for i in range(8)]
        PRODUCT_BANKS = -(-FQ // 8)
        with nc.Block() as block:

            @block.sync
            def _(e):
                e.dma_start(dft[:], d["dft"]).then_inc(loaded, 16)
                e.dma_start(mask[:], d["mask"]).then_inc(loaded, 16)
                e.dma_start(affine[:], d["L0_norm1"]).then_inc(loaded, 16)
                e.dma_start(w_raw[:], d["L0_w1"]).then_inc(w_loaded, 16)
                e.dma_start(bias[:], d["L0_b1"]).then_inc(w_loaded, 16)
                e.dma_start(idft[:], d["idft"]).then_inc(w_loaded, 16)

            @block.gpsimd
            def _(e):
                for w in w_for:
                    e.memset(w[:, :, COMPLEX:32], 0.0).then_inc(w_ready, 1)
                norm_gpsimd(e, norm)

            @block.vector
            def _(e):
                e.wait_ge(loaded_x, x_bytes)
                norm_vector(e, norm)
                e.wait_ge(loaded, 48)
                e.tensor_scalar(shift0[:], affine[:, 1:2], float(SIDE), None, ALU.mult).then_inc(chained, 1)
                e.wait_ge(evacuated, BATCH)
                e.wait_ge(chained, 1)
                e.tensor_scalar(spectrum[:, 0, :], spectrum[:, 0, :], shift0[:], None, ALU.add).then_inc(shifted, 1)
                e.wait_ge(shifted, 1)
                for n in range(0, BLOCKS, 2):
                    e.tensor_scalar(spread[:, :, n, :], spectrum[:], mask[:, n:n + 1], None, ALU.mult)\
                        .then_inc(spread_ready, 1)
                bias_v = bias[:].rearrange("p (f n) -> p f n", n=BLOCKS)
                for k in range(PRODUCT_BANKS):
                    f0, f1 = 8 * k, min(FQ, 8 * k + 8)
                    e.wait_ge(products, k + 1)
                    for f in range(f0, f1):
                        ins = e.tensor_tensor(
                            mixed[:, :, f].rearrange("p (n b) -> p n b", b=BATCH),
                            banks[k][:, (f - f0) * 64:(f - f0 + 1) * 64].rearrange("p (n b) -> p n b", b=BATCH),
                            bias_v[:, f, :].unsqueeze(2).to_broadcast([P, BLOCKS, BATCH]), ALU.add)
                    ins.then_inc(biased, 1)
                for m in range(0, 16, 2):
                    e.wait_ge(turned, m + 1)
                    n, b0 = m // 2, 4 * (m % 2)
                    src = banks[m % 8][0:FQ, :].rearrange("p (b j m) -> p b j m", b=4, j=QUARTERS)[:, :, :, 0:COMPLEX]
                    dst = by_freq[:, b0:b0 + 4, n, :].rearrange("p b (j m) -> p b j m", j=QUARTERS)
                    e.tensor_copy(dst, src).then_inc(turn_saved_v, 1)
                for g in range(4):
                    half, pair = g // 2, g % 2
                    e.wait_ge(inverted, g + 1)
                    src = banks[g][:, 0:4 * C].rearrange("p (b c) -> p b c", b=4)
                    dst = spatial[:].rearrange("p (b s) c -> p s b c", s=HALVES)[:, half, 4 * pair:4 * pair + 4, :]
                    e.tensor_copy(dst, src).then_inc(xs_ready, 1)
                e.wait_ge(xs_ready, 4)
                e.tensor_tensor(residual[:], spatial[:], stream[:], ALU.add).then_inc(stream_s, 1)
                e.wait_ge(stream_s, 1)

            @block.scalar
            def _(e):
                e.wait_ge(w_loaded, 48)
                raw = w_raw[:].rearrange("p (f o r) -> p f o r", o=BLOCK, r=2)
                pair = [w[:, :, 0:COMPLEX].rearrange("p f (o r) -> p f o r", r=2) for w in w_for]
                e.activation(w_for[0][:, :, 0:COMPLEX], w_raw[:].rearrange("p (f m) -> p f m", m=COMPLEX),
                             ACT.Copy).then_inc(w_ready, 1)
                e.activation(pair[1][:, :, :, 1], raw[:, :, :, 0], ACT.Copy).then_inc(w_ready, 1)
                e.activation(pair[1][:, :, :, 0], raw[:, :, :, 1], ACT.Copy, scale=-1.0).then_inc(w_ready, 1)
                e.wait_ge(loaded, 48)
                for b in range(BATCH):
                    e.wait_ge(transformed, b + 1)
                    e.activation(spectrum[:, :, b], banks[b][0:C, 0:2 * FREQS], ACT.Copy, scale=affine[:, 0:1])\
                        .then_inc(evacuated, 1)
                e.wait_ge(shifted, 1)
                for n in range(1, BLOCKS, 2):
                    e.activation(spread[:, :, n, :], spectrum[:], ACT.Copy, scale=mask[:, n:n + 1])\
                        .then_inc(spread_ready, 1)
                e.wait_ge(biased, PRODUCT_BANKS)
                for n in range(BLOCKS):
                    part = mixed[:, n * BATCH:(n + 1) * BATCH, :]
                    e.activation(part, part, ACT.Relu).then_inc(relu_done, 1)
                for m in range(1, 16, 2):
                    e.wait_ge(turned, m + 1)
                    n, b0 = m // 2, 4 * (m % 2)
                    src = banks[m % 8][0:FQ, :].rearrange("p (b j m) -> p b j m", b=4, j=QUARTERS)[:, :, :, 0:COMPLEX]
                    dst = by_freq[:, b0:b0 + 4, n, :].rearrange("p b (j m) -> p b j m", j=QUARTERS)
                    e.activation(dst, src, ACT.Copy).then_inc(turn_saved_s, 1)

            @block.tensor
            def _(e):
                e.wait_ge(loaded, 48)
                for b in range(BATCH):
                    for half in range(HALVES):
                        tile = HALVES * b + half
                        e.wait_ge(norm.rows_ready, tile + 1)
                        last = e.matmul(banks[b][0:C, 0:2 * FREQS], rows[:, tile, :], dft[:, half, :],
                                        start=(half == 0), stop=(half == HALVES - 1))
                    last.then_inc(transformed, 1)
                e.wait_ge(w_ready, 5)
                e.wait_ge(spread_ready, BLOCKS)
                for f in range(FQ):
                    k, f8 = divmod(f, 8)
                    for part in range(2):
                        for j in range(QUARTERS):
                            freq = j * FQ + f
                            last = e.matmul(banks[k][32 * j:32 * j + 32, f8 * 64:(f8 + 1) * 64],
                                            w_for[part][:, freq, :], flat(spread[:, 2 * freq + part, :, :]),
                                            start=(part == 0), stop=(part == 1), skip_group_check=True)
                    if f8 == 7 or f == FQ - 1:
                        last.then_inc(products, 1)
                for m in range(16):
                    n, b0 = m // 2, 4 * (m % 2)
                    e.wait_ge(relu_done, n + 1)
                    if m >= 8:
                        e.wait_ge(turn_saved_v if m % 2 == 0 else turn_saved_s, (m - 8) // 2 + 1)
                    for b in range(4):
                        last = e.transpose(banks[m % 8][0:FQ, b * P:(b + 1) * P], mixed[:, n * BATCH + b0 + b, :], ident[:])
                    last.then_inc(turned, 1)
                e.wait_ge(turn_saved_v, 8)
                e.wait_ge(turn_saved_s, 8)
                for g in range(4):
                    half, pair = g // 2, g % 2
                    out = banks[g][:, 0:4 * C].rearrange("p (b n o) -> p b n o", b=4, n=BLOCKS)
                    for k in range(2 * QUARTERS):
                        j, part = divmod(k, 2)
                        rhs = by_freq[:, 4 * pair:4 * pair + 4, :, j * COMPLEX + part:(j + 1) * COMPLEX:2]
                        last = e.matmul(out, idft[:, k * HALVES + half, :], rhs, start=(k == 0), stop=(k == 2 * QUARTERS - 1))
                    last.then_inc(inverted, 1)

        mlp(nc, d, stream, spatial, residual, rows, banks, ident)


def mlp(nc, d, stream, spatial, residual, rows, banks, ident):
    with ExitStack() as ctx:
        sb = lambda n, shape, dt=F32: ctx.enter_context(nc.sbuf_tensor("mlp_" + n, shape, dt))
        sem = lambda n: ctx.enter_context(nc.semaphore("mlp_" + n))
        KH = HIDDEN // P
        NB = TOKENS // BANK
        w1, w2 = sb("w1", [C, HIDDEN]), sb("w2", [P, KH, C])
        b1, b2, affine = sb("b1", [P, KH]), sb("b2", [P, C]), sb("affine", [C, 2])
        xT = sb("xT", [C, TOKENS])
        hidden = sb("hidden", [P, 2, KH, BANK])
        loaded, turned, scaled = sem("loaded"), sem("turned"), sem("scaled")
        up, activated, down, added, base = sem("up"), sem("activated"), sem("down"), sem("added"), sem("base")
        norm = Norm(nc, ctx, "mlpn", spatial, rows, 1e-5)
        with nc.Block() as block:

            @block.sync
            def _(e):
                for dst, name in ((w1, "L0_mlp_w1"), (w2, "L0_mlp_w2"), (b1, "L0_mlp_b1"), (b2, "L0_mlp_b2"), (affine, "L0_norm2")):
                    e.dma_start(dst[:], d[name]).then_inc(loaded, 16)

            @block.gpsimd
            def _(e):
                norm_gpsimd(e, norm)
                e.wait_ge(loaded, 80)
                e.tensor_tensor(residual[:], residual[:], b2[:].unsqueeze(1).to_broadcast([P, TILES, C]), ALU.add)\
                    .then_inc(base, 1)

            @block.vector
            def _(e):
                norm_vector(e, norm)
                e.wait_ge(base, 1)
                for k in range(NB):
                    e.wait_ge(down, k + 1)
                    e.tensor_tensor(stream[:, 4 * k:4 * k + 4, :], residual[:, 4 * k:4 * k + 4, :],
                                    banks[6 + k % 2][:, 0:4 * C].rearrange("p (t c) -> p t c", c=C), ALU.add)\
                        .then_inc(added, 1)

            @block.scalar
            def _(e):
                e.wait_ge(loaded, 80)
                for k in range(NB):
                    e.wait_ge(turned, 4 * k + 4)
                    e.activation(xT[:, k * BANK:(k + 1) * BANK], banks[k][0:C, :], ACT.Identity,
                                 scale=affine[:, 0:1], bias=affine[:, 1:2]).then_inc(scaled, 1)
                for k in range(NB):
                    if k >= 2:
                        e.wait_ge(down, k - 1)
                    for m in range(KH):
                        e.wait_ge(up, k * KH + m + 1)
                        e.activation(hidden[:, k % 2, m, :], banks[(k * KH + m) % 6][:], ACT.Gelu,
                                     bias=b1[:, m:m + 1]).then_inc(activated, 1)

            @block.tensor
            def _(e):
                transposes(e, norm, ident, banks, turned)
                e.wait_ge(scaled, NB)
                for k in range(NB + 1):
                    if k < NB:
                        for m in range(KH):
                            n = k * KH + m
                            if n >= 6:
                                e.wait_ge(activated, n - 5)
                            e.matmul(banks[n % 6][:], w1[:, m * P:(m + 1) * P], xT[:, k * BANK:(k + 1) * BANK],
                                     start=True, stop=True).then_inc(up, 1)
                    if k >= 1:
                        q = k - 1
                        e.wait_ge(activated, KH * k)
                        if q >= 2:
                            e.wait_ge(added, q - 1)
                        for t in range(4):
                            for m in range(KH):
                                last = e.matmul(banks[6 + q % 2][:, t * C:(t + 1) * C],
                                                hidden[:, q % 2, m, t * P:(t + 1) * P], w2[:, m, :],
                                                start=(m == 0), stop=(m == KH - 1))
                        last.then_inc(down, 1)


def coefficients(nc, d, coef, ident, constants_loaded, constants_bytes):
    with ExitStack() as ctx:
        sb = lambda n, shape, dt=F32: ctx.enter_context(nc.sbuf_tensor("rpe_" + n, shape, dt))
        sem = lambda n: ctx.enter_context(nc.semaphore("rpe_" + n))
        pos = sb("pos", [1, LAGS])
        ones = sb("ones", [1, LAGS])
        rows = sb("rows", [1, 2, 2 + DEPTH, RPE])
        lw = sb("lw", [RPE, 2, DEPTH * RPE])
        ow = sb("ow", [RPE, 2, D1])
        ob = sb("ob", [C, 2, CHUNKS])
        x = sb("x", [LAGS, 2, RPE])
        stats = sb("stats", [LAGS, 2, 6])
        moments = sb("moments", [LAGS, 2, 2])
        power, guess, work, exponent = (sb("power", [LAGS, 2]), sb("guess", [LAGS, 2]), sb("work", [LAGS, 2]),
                                        sb("exponent", [LAGS, 2]))
        y = sb("y", [LAGS, 2, RPE])
        y_turned = sb("y_turned", [RPE, 2, LAGS])
        layer_bank = ctx.enter_context(nc.psum_tensor("rpe_layer", [LAGS, 2, RPE], F32))
        turn_bank = ctx.enter_context(nc.psum_tensor("rpe_turn", [RPE, 2, LAGS], F32))
        out_bank = ctx.enter_context(nc.psum_tensor("rpe_out", [C, CHUNKS, 2, LAGS], F32))
        loaded, chained, product = sem("loaded"), sem("chained"), sem("product")
        power_ready, guessed, y_ready, turned, y_saved = (sem("power_ready"), sem("guessed"), sem("y_ready"),
                                                          sem("turned"), sem("y_saved"))
        with nc.Block() as block:

            @block.sync
            def _(e):
                for dst, name in ((pos, "pos"), (rows, "rpe_rows"), (lw, "rpe_lw"), (ow, "rpe_ow"), (ob, "rpe_ob")):
                    e.dma_start(dst[:], d[name]).then_inc(loaded, 16)

            @block.tensor
            def _(e):
                e.wait_ge(loaded, 80)
                e.wait_ge(constants_loaded, constants_bytes)
                e.wait_ge(chained, 1)
                for i in range(DEPTH + 1):
                    for a in range(2):
                        if i == 0:
                            e.matmul(layer_bank[:, a, :], pos[:], rows[:, a, 0, :], start=True, stop=False)
                        else:
                            e.matmul(layer_bank[:, a, :], y_turned[:, a, :], lw[:, a, (i - 1) * RPE:i * RPE],
                                     start=True, stop=False)
                        e.matmul(layer_bank[:, a, :], ones[:], rows[:, a, 1 + i, :], start=False, stop=True)\
                            .then_inc(product, 1)
                    e.wait_ge(y_ready, 2 * i + 2)
                    for a in range(2):
                        e.transpose(turn_bank[:, a, :], y[:, a, :], ident[0:LAGS, 0:LAGS]).then_inc(turned, 1)
                    e.wait_ge(y_saved, i + 1)
                for a in range(2):
                    for m in range(CHUNKS):
                        e.matmul(out_bank[:, m, a, :], ow[:, a, m * C:(m + 1) * C], y_turned[:, a, :],
                                 start=True, stop=True).then_inc(product, 1)

            @block.gpsimd
            def _(e):
                for i in range(DEPTH + 1):
                    e.wait_ge(power_ready, i + 2)
                    e.tensor_tensor(guess[:], power[:], exponent[:], ALU.pow).then_inc(guessed, 1)

            @block.vector
            def _(e):
                count = 0

                def link(ins):
                    nonlocal count
                    count += 1
                    ins.then_inc(chained, 1)
                    e.wait_ge(chained, count)

                link(e.memset(ones[:], 1.0))
                e.memset(exponent[:], -0.5).then_inc(power_ready, 1)
                for i in range(DEPTH + 1):
                    e.wait_ge(product, 2 * i + 2)
                    if i == 0:
                        link(e.tensor_scalar(x[:], layer_bank[:], 0.0, None, ALU.max))
                    else:
                        link(e.tensor_copy(x[:], layer_bank[:]))
                    for a in range(2):
                        last = e.bn_stats(stats[:, a, :], x[:, a, :])
                    link(last)
                    for a in range(2):
                        last = e.bn_aggr(moments[:, a, :], stats[:, a, :])
                    link(last)
                    link(e.tensor_tensor(work[:], moments[:, :, 0], moments[:, :, 0], ALU.mult))
                    e.scalar_tensor_tensor(out=power[:], in0=moments[:, :, 1], scalar=1e-6, in1=work[:],
                                           op0=ALU.add, op1=ALU.add).then_inc(power_ready, 1)
                    e.wait_ge(guessed, i + 1)
                    link(e.tensor_tensor(work[:], guess[:], guess[:], ALU.mult))
                    link(e.tensor_tensor(work[:], work[:], power[:], ALU.mult))
                    link(e.tensor_scalar(work[:], work[:], -0.5, 1.5, ALU.mult, ALU.add))
                    link(e.tensor_tensor(work[:], work[:], guess[:], ALU.mult))
                    for a in range(2):
                        e.tensor_scalar(y[:, a, :], x[:, a, :], 0.0, work[:, a:a + 1], ALU.max, ALU.mult).then_inc(y_ready, 1)
                    e.wait_ge(turned, 2 * i + 2)
                    e.tensor_copy(y_turned[:], turn_bank[:]).then_inc(y_saved, 1)
                e.wait_ge(product, 2 * DEPTH + 2 + 2 * CHUNKS)
                e.tensor_tensor(coef[:], out_bank[:], ob[:].rearrange("p a m -> p m a").unsqueeze(3)
                                .to_broadcast([C, CHUNKS, 2, LAGS]), ALU.add)


PE_LAGS = [(axis, lag) for axis, lags in ((0, range(-3, 4)), (1, range(-3, 4))) for lag in lags]
PE_LAGS.sort(key=lambda al: al != (0, 0))
DVE_LAGS = [(axis, lag) for axis in range(2) for lag in sorted(range(1 - SIDE, SIDE), key=abs) if (axis, lag) not in PE_LAGS]


def shifted(v, axis, lag):
    n = SIDE - abs(lag)
    to, of = (slice(lag, SIDE), slice(0, n)) if lag >= 0 else (slice(0, n), slice(-lag, SIDE))
    return to, of


def toeplitz(nc, d, stream, ident, coef, weights):
    with ExitStack() as ctx:
        sb = lambda n, shape, dt=F32: ctx.enter_context(nc.sbuf_tensor("l1_" + n, shape, dt))
        sem = lambda n: ctx.enter_context(nc.semaphore("l1_" + n))
        NB = TOKENS // BANK
        NDIAG = 4
        rows = sb("rows", [P, TILES, C])
        xT = sb("xT", [C, TOKENS])
        w_uv, b_uv = sb("w_uv", [C, 2, D1]), sb("b_uv", [C, 2, CHUNKS])
        w_o, b_o = sb("w_o", [C, CHUNKS, C]), sb("b_o", [P, C])
        u, v = sb("u", [C, CHUNKS, TOKENS]), sb("v", [C, CHUNKS, TOKENS])
        acc = sb("acc", [C, CHUNKS, TOKENS])
        diag = sb("diag", [C, NDIAG, C])
        base = sb("base", [P, TILES, C])
        loaded, turned, copied = sem("loaded"), sem("turned"), sem("copied")
        uv_done, v_ready, u_ready = sem("uv_done"), sem("v_ready"), sem("u_ready")
        diag_ready, diag_used, conv_done = sem("diag_ready"), sem("diag_used"), sem("conv_done")
        acc_step, summed, gated, projected, added, based = (sem("acc_step"), sem("summed"), sem("gated"),
                                                            sem("projected"), sem("added"), sem("based"))
        norm = Norm(nc, ctx, "l1n", stream, rows, 1e-6, centred=False)
        splits = [WeightSplit(nc, ctx, w) for w in weights]
        banks = [ctx.enter_context(nc.psum_tensor(f"l1_bank{i}", [P, BANK], F32)) for i in range(8)]

        def bank_of(uv, m, k):
            return 4 + (4 * (2 * uv + m) + k) % 4

        with nc.Block() as block:

            @block.sync
            def _(e):
                for dst, name in ((w_uv, "L1_w_uv"), (b_uv, "L1_b_uv"), (w_o, "L1_w_o"), (b_o, "L1_b_o")):
                    e.dma_start(dst[:], d[name]).then_inc(loaded, 16)
                for split in splits:
                    split.load(e, d)

            @block.gpsimd
            def _(e):
                norm_gpsimd(e, norm)
                e.wait_ge(loaded, 64)
                e.tensor_tensor(base[:], stream[:], b_o[:].unsqueeze(1).to_broadcast([P, TILES, C]), ALU.add)\
                    .then_inc(based, 1)
                for m in range(CHUNKS):
                    for i, (axis, lag) in enumerate(PE_LAGS):
                        n = m * len(PE_LAGS) + i
                        if n >= NDIAG:
                            e.wait_ge(diag_used, n - NDIAG + 1)
                        at = lag + SIDE - 1
                        e.tensor_scalar(diag[:, n % NDIAG, :], ident[0:C, 0:C], coef[:, m, axis, at:at + 1], None,
                                        ALU.mult).then_inc(diag_ready, 1)
                for split in splits:
                    split.lo(e)

            @block.vector
            def _(e):
                norm_vector(e, norm)
                steps = 0
                for m in range(CHUNKS):
                    e.wait_ge(v_ready, NB * (m + 1))
                    for i, (axis, lag) in enumerate(DVE_LAGS):
                        at = lag + SIDE - 1
                        a = coef[:, m, axis, at:at + 1]
                        if i == 0:
                            e.memset(acc[:, m, :], 0.0).then_inc(acc_step, 1)
                            steps += 1
                        to, of = shifted(v, axis, lag)
                        if axis == 0:
                            row = lambda s, t: t[:, m, :].rearrange("p (b r) -> p b r", b=BATCH)[:, :, s.start * SIDE:s.stop * SIDE]
                        else:
                            row = lambda s, t: t[:, m, :].rearrange("p (b r) -> p b r", r=SIDE)[:, :, s]
                        e.wait_ge(acc_step, steps)
                        e.scalar_tensor_tensor(out=row(to, acc), in0=row(of, v), scalar=a, in1=row(to, acc),
                                               op0=ALU.mult, op1=ALU.add).then_inc(acc_step, 1)
                        steps += 1
                    e.wait_ge(acc_step, steps)
                    for k in range(NB):
                        cols = slice(k * BANK, (k + 1) * BANK)
                        e.wait_ge(conv_done, m + 1)
                        e.tensor_tensor(acc[:, m, cols], acc[:, m, cols], banks[4 * m + k][0:C, :], ALU.add)\
                            .then_inc(summed, 1)
                    e.wait_ge(summed, NB * (m + 1))
                    e.wait_ge(u_ready, NB * (m + 1))
                    e.tensor_tensor(v[:, m, :], acc[:, m, :], u[:, m, :], ALU.mult).then_inc(gated, 1)
                e.wait_ge(based, 1)
                for k in range(NB):
                    e.wait_ge(projected, k + 1)
                    e.tensor_tensor(stream[:, 4 * k:4 * k + 4, :], base[:, 4 * k:4 * k + 4, :],
                                    banks[k][:, 0:4 * C].rearrange("p (t c) -> p t c", c=C), ALU.add)\
                        .then_inc(added, 1)

            @block.scalar
            def _(e):
                for k in range(NB):
                    e.wait_ge(turned, 4 * k + 4)
                    e.activation(xT[:, k * BANK:(k + 1) * BANK], banks[k][0:C, :], ACT.Copy).then_inc(copied, 1)
                e.wait_ge(loaded, 64)
                n = 0
                for uv in (1, 0):
                    for m in range(CHUNKS):
                        for k in range(NB):
                            n += 1
                            e.wait_ge(uv_done, n)
                            out = (u if uv == 0 else v)[:, m, k * BANK:(k + 1) * BANK]
                            e.activation(out, banks[4 + (n - 1) % 4][0:C, :], ACT.Silu, bias=b_uv[:, uv, m:m + 1])\
                                .then_inc(u_ready if uv == 0 else v_ready, 1)
                for split in splits:
                    split.hi(e)

            @block.tensor
            def _(e):
                transposes(e, norm, ident, banks, turned)
                e.wait_ge(loaded, 64)
                e.wait_ge(copied, NB)
                n = 0
                for uv in (1, 0):
                    for m in range(CHUNKS):
                        for k in range(NB):
                            if n >= 4:
                                done = n - 3
                                e.wait_ge(v_ready, min(done, CHUNKS * NB))
                                if done > CHUNKS * NB:
                                    e.wait_ge(u_ready, done - CHUNKS * NB)
                            e.matmul(banks[4 + n % 4][0:C, :], w_uv[:, uv, m * C:(m + 1) * C],
                                     xT[:, k * BANK:(k + 1) * BANK], start=True, stop=True).then_inc(uv_done, 1)
                            n += 1
                e.wait_ge(v_ready, CHUNKS * NB)
                e.wait_ge(u_ready, CHUNKS * NB)
                for m in range(CHUNKS):
                    for i, (axis, lag) in enumerate(PE_LAGS):
                        e.wait_ge(diag_ready, m * len(PE_LAGS) + i + 1)
                        to, of = shifted(v, axis, lag)
                        for k in range(NB):
                            src = v[:, m, k * BANK:(k + 1) * BANK]
                            dst = banks[4 * m + k][0:C, :]
                            if axis == 0:
                                row = lambda s, t: t.rearrange("p (b r) -> p b r", b=2)[:, :, s.start * SIDE:s.stop * SIDE]
                            else:
                                row = lambda s, t: t.rearrange("p (b r) -> p b r", r=SIDE)[:, :, s]
                            last = e.matmul(row(to, dst), diag[:, (m * len(PE_LAGS) + i) % NDIAG, :], row(of, src),
                                            start=(i == 0), stop=(i == len(PE_LAGS) - 1))
                        last.then_inc(diag_used, 1)
                    e.wait_ge(diag_used, (m + 1) * len(PE_LAGS))
                    e.sem_inc(conv_done, 1)
                e.wait_ge(gated, CHUNKS)
                for k in range(NB):
                    for t in range(4):
                        tile = 4 * k + t
                        for m in range(CHUNKS):
                            last = e.matmul(banks[k][:, t * C:(t + 1) * C], v[:, m, tile * P:(tile + 1) * P], w_o[:, m, :],
                                            start=(m == 0), stop=(m == CHUNKS - 1))
                    last.then_inc(projected, 1)


class GruWeights:

    def __init__(self, nc, ctx, layer):
        n = len(GRUS) * GATES
        self.layer = layer
        self.hidden = ctx.enter_context(nc.sbuf_tensor(f"{layer}_w_hidden", [C + 1, 2, n, P], F16))
        self.input = ctx.enter_context(nc.sbuf_tensor(f"{layer}_w_input", [C + 1, 2, CHUNKS, n, P], F16))


class WeightSplit:

    def __init__(self, nc, ctx, weights):
        n = len(GRUS) * GATES
        layer = weights.layer
        hidden_raw = ctx.enter_context(nc.sbuf_tensor(f"{layer}_w_hidden_raw", [C + 1, n, P], F32))
        input_raw = ctx.enter_context(nc.sbuf_tensor(f"{layer}_w_input_raw", [C + 1, CHUNKS, n, P], F32))
        self.raw = ((hidden_raw, f"{layer}_whh", weights.hidden), (input_raw, f"{layer}_wih", weights.input))
        self.loaded = ctx.enter_context(nc.semaphore(f"{layer}_w_raw_loaded"))
        self.hi_ready = ctx.enter_context(nc.semaphore(f"{layer}_w_hi_ready"))
        self.lo_ready = ctx.enter_context(nc.semaphore(f"{layer}_w_lo_ready"))

    def load(self, e, d):
        for raw, name, _ in self.raw:
            e.dma_start(raw[:], d[name]).then_inc(self.loaded, 16)

    def hi(self, e):
        e.wait_ge(self.loaded, 32)
        for raw, _, parts in self.raw:
            e.activation(parts[:, 0], raw[:], ACT.Copy).then_inc(self.hi_ready, 1)

    def lo(self, e):
        for i, (raw, _, parts) in enumerate(self.raw):
            e.wait_ge(self.hi_ready, i + 1)
            e.tensor_tensor(parts[:, 1], raw[:], parts[:, 0], ALU.subtract).then_inc(self.lo_ready, 1)


def gru_layer(nc, d, layer, stream, ident, weights, out_dram=None):
    with ExitStack() as outer:
        sbo = lambda n, shape, dt=F32: outer.enter_context(nc.sbuf_tensor(f"{layer}_{n}", shape, dt))
        gate = sbo("gate", [C, CHUNKS, TOKENS])
        history = sbo("history", [C, SEQ, GROUPS, PER])
        w_out = sbo("w_out", [C, CHUNKS, C])
        w_loaded = outer.enter_context(nc.semaphore(f"{layer}_w_loaded"))
        with ExitStack() as ctx:
            sb = lambda n, shape, dt=F32: ctx.enter_context(nc.sbuf_tensor(f"{layer}_{n}", shape, dt))
            forward = sb("forward", [C + 1, 2, CHUNKS, SEQ + STEPS, BATCH], F16)
            backward = sb("backward", [C + 1, 2, CHUNKS, SEQ + STEPS, BATCH], F16)
            gru_input(nc, d, layer, stream, ident, forward, backward, gate, w_out, w_loaded)
            gru_steps(nc, layer, weights, forward, backward, history)
        gru_output(nc, layer, stream, gate, history, w_out, w_loaded, out_dram)


def gru_input(nc, d, layer, stream, ident, forward, backward, gate, w_out, w_loaded):
    with ExitStack() as ctx:
        sb = lambda n, shape, dt=F32: ctx.enter_context(nc.sbuf_tensor(f"{layer}i_{n}", shape, dt))
        sem = lambda n: ctx.enter_context(nc.semaphore(f"{layer}i_{n}"))
        NB = TOKENS // BANK
        TB = BANK // BATCH
        rows = sb("rows", [P, TILES, C])
        xT = sb("xT", [C, SEQ, BATCH])
        w_in = sb("w_in", [C, 2 * D1])
        affine = sb("affine", [C, 2])
        loaded, turned, scaled, projected = sem("loaded"), sem("turned"), sem("scaled"), sem("projected")
        hi_ready, lo_ready, gate_ready, filled, reversed_ = (sem("hi_ready"), sem("lo_ready"), sem("gate_ready"),
                                                                    sem("filled"), sem("reversed"))
        norm = Norm(nc, ctx, f"{layer}n", stream, rows, 1e-5)
        banks = [ctx.enter_context(nc.psum_tensor(f"{layer}i_bank{i}", [P, BANK], F32)) for i in range(8)]
        order = [(m, k) for m in range(CHUNKS) for k in range(NB)] + [(CHUNKS + m, k) for m in range(CHUNKS) for k in range(NB)]
        INNER = CHUNKS * NB
        with nc.Block() as block:

            @block.sync
            def _(e):
                e.dma_start(w_in[:], d[f"{layer}_w_in"]).then_inc(loaded, 16)
                e.dma_start(affine[:], d[f"{layer}_ln"]).then_inc(loaded, 16)
                e.dma_start(w_out[:], d[f"{layer}_w_out"]).then_inc(w_loaded, 16)

            @block.gpsimd
            def _(e):
                norm_gpsimd(e, norm)
                e.wait_ge(norm.guess_ready, 1)
                for i, x in enumerate((forward, backward)):
                    for part in range(2):
                        e.memset(x[0:C, part, :, SEQ:, :], 0.0).then_inc(filled, 1)
                        e.wait_ge(filled, 4 * i + 2 * part + 1)
                        e.memset(x[C:C + 1, part, 1, :, :], 1.0 - part).then_inc(filled, 1)
                        e.wait_ge(filled, 4 * i + 2 * part + 2)

            @block.vector
            def _(e):
                norm_vector(e, norm)
                for i, (m, k) in enumerate(order[:INNER]):
                    cols = slice(k * TB, (k + 1) * TB)
                    e.wait_ge(hi_ready, i + 1)
                    e.tensor_tensor(forward[0:C, 1, m, cols, :], banks[4 + i % 4][0:C, :].rearrange("p (t b) -> p t b", b=BATCH),
                                    forward[0:C, 0, m, cols, :], ALU.subtract).then_inc(lo_ready, 1)
                e.wait_ge(lo_ready, INNER)
                for part in range(2):
                    for m in range(CHUNKS):
                        e.tensor_copy(backward[0:C, part, m, 0:SEQ, :], forward[0:C, part, m, SEQ - 1::-1, :]).then_inc(reversed_, 1)

            @block.scalar
            def _(e):
                e.wait_ge(loaded, 32)
                for k in range(NB):
                    e.wait_ge(turned, 4 * k + 4)
                    e.activation(xT[:].rearrange("p t b -> p b t")[:, 2 * k:2 * k + 2, :],
                                 banks[k][0:C, :].rearrange("p (b t) -> p b t", b=2), ACT.Identity,
                                 scale=affine[:, 0:1], bias=affine[:, 1:2]).then_inc(scaled, 1)
                for i, (m, k) in enumerate(order):
                    e.wait_ge(projected, i + 1)
                    src = banks[4 + i % 4][0:C, :]
                    if m < CHUNKS:
                        e.activation(forward[0:C, 0, m, k * TB:(k + 1) * TB, :], src.rearrange("p (t b) -> p t b", b=BATCH),
                                     ACT.Copy).then_inc(hi_ready, 1)
                    else:
                        e.activation(gate[:, m - CHUNKS, k * BANK:(k + 1) * BANK], src, ACT.Silu).then_inc(gate_ready, 1)

            @block.tensor
            def _(e):
                transposes(e, norm, ident, banks, turned)
                e.wait_ge(loaded, 32)
                e.wait_ge(scaled, NB)
                x_all = flat(xT[:])
                for i, (m, k) in enumerate(order):
                    if i >= 4:
                        done = i - 3
                        e.wait_ge(lo_ready, min(done, INNER))
                        if done > INNER:
                            e.wait_ge(gate_ready, done - INNER)
                    e.matmul(banks[4 + i % 4][0:C, :], w_in[:, m * C:(m + 1) * C], x_all[:, k * BANK:(k + 1) * BANK],
                             start=True, stop=True).then_inc(projected, 1)


def gru_steps(nc, layer, weights, forward, backward, history):
    with ExitStack() as ctx:
        sb = lambda n, shape, dt=F32: ctx.enter_context(nc.sbuf_tensor(f"{layer}s_{n}", shape, dt))
        sem = lambda n: ctx.enter_context(nc.semaphore(f"{layer}s_{n}"))
        pairs = lambda n, shape, dt=F32: [sb(f"{n}{g}", shape, dt) for g in range(GROUPS)]
        each = lambda n: [sem(f"{n}{g}") for g in range(GROUPS)]
        reset = pairs("reset", [C, 2, PER, 2])
        cand = pairs("cand", [C, 2, PER, 2])
        update = pairs("update", [C, 2, PER, 3])
        WIDE = 3 * PER
        terms = pairs("terms", [C, RING, WIDE + 2])
        h_hi = pairs("h_hi", [C + 1, 2, PER, 3], F16)
        h_lo = pairs("h_lo", [C, 2, PER], F16)
        rz = [[ctx.enter_context(nc.psum_tensor(f"{layer}s_rz{g}{p}", [P, STEPS, 2, PER], F32)) for p in range(2)] for g in range(GROUPS)]
        nn = [[ctx.enter_context(nc.psum_tensor(f"{layer}s_nn{g}{p}", [P, STEPS, PER, 2], F32)) for p in range(2)] for g in range(GROUPS)]
        warm = sb("warm", [C, 1])
        prepared = sem("prepared")
        gates_summed, reset_ready = each("gates_summed"), each("reset_ready")
        cand_ready, tanh_ready = each("cand_ready"), each("tanh_ready")
        hi_ready, state_ready, lo_ready = each("hi_ready"), each("state_ready"), each("lo_ready")
        chunk_done, chunk_saved, ring_free = sem("chunk_done"), sem("chunk_saved"), sem("ring_free")
        PREPARED = 1 + 6 * GROUPS + 2 * GROUPS
        TURNS = SEQ // RING
        ring_of = lambda g, q: terms[g][:, q % RING, :]

        with nc.Block() as block:

            @block.vector
            def _(e):
                done = 0

                def prepare(ins):
                    nonlocal done
                    done += 1
                    ins.then_inc(prepared, 1)
                    e.wait_ge(prepared, done)

                prepare(e.memset(warm[:], 0.0))
                for g in range(GROUPS):
                    for buffer in (reset[g], update[g], terms[g], h_hi[g], h_lo[g]):
                        prepare(e.memset(buffer[:], 0.0))
                    prepare(e.memset(h_hi[g][C:C + 1], 1.0))
                for g in range(GROUPS):
                    for x in range(2):
                        prepare(e.memset(update[g][:, x, :, 1], -1.0))
                for s in (state_ready[1], hi_ready[0], hi_ready[1], lo_ready[0]):
                    e.sem_inc(s, 1)

                def candidate(g, q):
                    p, s = divmod(q, STEPS)
                    x = q % 2
                    e.wait_ge(reset_ready[g], q + 1)
                    e.tensor_tensor_scan(flat(cand[g][:, x]), flat(reset[g][:, x]), flat(nn[g][p][0:C, s]), 0.0,
                                         ALU.mult, ALU.add).then_inc(cand_ready[g], 1)

                def new_state(g, q):
                    x = q % 2
                    e.wait_ge(tanh_ready[g], q + 1)
                    e.tensor_tensor_scan(flat(h_hi[g][0:C, x]), flat(update[g][:, x]), ring_of(g, q)[:, 1:1 + WIDE], 0.0,
                                         ALU.mult, ALU.add).then_inc(hi_ready[g], 1)
                    e.tensor_tensor_scan(ring_of(g, q + 1)[:, 0:WIDE], flat(update[g][:, x]), ring_of(g, q)[:, 1:1 + WIDE], 0.0,
                                         ALU.mult, ALU.add).then_inc(state_ready[g], 1)

                def rest(g, q, count):
                    e.wait_ge(state_ready[g], count)
                    e.tensor_tensor(h_lo[g][:, q % 2], ring_of(g, q + 1)[:, 2:2 + WIDE:3], h_hi[g][0:C, q % 2, :, 2],
                                    ALU.subtract).then_inc(lo_ready[g], 1)

                with e.Fori(0, TURNS):
                    for q in range(RING):
                        if q % STEPS == 0:
                            e.wait_ge(ring_free, q // STEPS + 1)
                        candidate(0, q)
                        rest(1, q - 1, q + 1)
                        if q % STEPS == 0:
                            e.sem_inc(chunk_done, 1)
                        new_state(0, q)
                        rest(0, q, q + 1)
                        candidate(1, q)
                        new_state(1, q)
                    for s in (*reset_ready, *tanh_ready, *state_ready):
                        e.sem_inc(s, -RING)
                    e.sem_inc(ring_free, -2)
                rest(1, -1, 1)
                e.sem_inc(chunk_done, 1)

            @block.scalar
            def _(e):
                e.wait_ge(prepared, 1)
                e.activation(warm[:], warm[:], ACT.Sigmoid)
                e.wait_ge(prepared, PREPARED)
                with e.Fori(0, TURNS):
                    for q in range(RING):
                        p, s = divmod(q, STEPS)
                        x = q % 2
                        for g in range(GROUPS):
                            e.wait_ge(gates_summed[g], q + 1)
                            e.activation(reset[g][:, x, :, 1], rz[g][p][0:C, s, 0], ACT.Sigmoid).then_inc(reset_ready[g], 1)
                            e.activation(update[g][:, x, :, 2], rz[g][p][0:C, s, 1], ACT.Sigmoid)
                            e.wait_ge(cand_ready[g], q + 1)
                            places = ring_of(g, q)[:, 1:1 + WIDE].rearrange("p (a b) -> p a b", b=3)[:, :, 0::2]
                            e.activation(places, cand[g][:, x, :, 1:2].to_broadcast([C, PER, 2]), ACT.Tanh)\
                                .then_inc(tanh_ready[g], 1)
                    for s in (*gates_summed, *cand_ready):
                        e.sem_inc(s, -RING)

            @block.gpsimd
            def _(e):
                e.sem_inc(ring_free, 2)
                with e.Fori(0, TURNS) as turn:
                    for p in range(2):
                        chunk = turn * 2 + p
                        first = chunk * STEPS
                        e.wait_ge(chunk_done, chunk + 2)
                        for g in range(GROUPS):
                            e.tensor_copy(history[:, bass.ds(first, STEPS - 1), g, :],
                                          terms[g][:, p * STEPS + 1:(p + 1) * STEPS, 2:2 + WIDE:3])
                            last = e.tensor_copy(history[:, bass.ds(first + STEPS - 1, 1), g, :],
                                                 terms[g][:, (p + 1) * STEPS % RING, None, 2:2 + WIDE:3])
                        last.then_inc(chunk_saved, 1)
                        e.wait_ge(chunk_saved, chunk + 1)
                        e.sem_inc(ring_free, 1)

            @block.tensor
            def _(e):
                def inputs(p, chunk):
                    out = []
                    cols = bass.ds(chunk * (STEPS * BATCH), STEPS * BATCH)
                    for gru in range(len(GRUS)):
                        g, j = divmod(gru, 2)
                        source = forward if gru < 2 else backward
                        mine = slice(j * BATCH, (j + 1) * BATCH)

                        def share(dst, gate, first):
                            for m in range(CHUNKS):
                                rows = C + 1 if m else C
                                for wp, xp in ((0, 0), (1, 0), (0, 1)):
                                    lhsT = weights.input[0:rows, wp, m, GATES * gru + gate, :]
                                    rhs = source[0:rows, xp, m].rearrange("p t b -> p (t b)")[:, cols]
                                    start = first and m == 0 and (wp, xp) == (0, 0)
                                    out.append((dst, lhsT, rhs, start))

                        share(rz[g][p][:, :, 0, mine], 0, j == 0)
                        share(rz[g][p][:, :, 1, mine], 1, False)
                        share(nn[g][p][:, :, mine, 1], 2, j == 0)
                    return out

                def run(product):
                    dst, lhsT, rhs, start = product
                    return e.matmul(dst, lhsT, rhs, start=start, stop=False, skip_group_check=True)

                e.wait_ge(prepared, PREPARED)
                for product in inputs(0, 0):
                    run(product)
                with e.Fori(0, TURNS) as turn:
                    for q in range(RING):
                        p, s = divmod(q, STEPS)
                        x = (q + 1) % 2
                        if s == 0:
                            ahead = inputs(1 - p, turn * 2 + (p + 1))
                            sent = 0
                        for g in range(GROUPS):
                            def add(gate, wp, xp, j):
                                mine = slice(j * BATCH, (j + 1) * BATCH)
                                rows = C if xp else C + 1
                                rhs = h_lo[g][:, x, mine] if xp else h_hi[g][:, x, mine, 2]
                                dst = nn[g][p][:, s, mine, 0] if gate == 2 else rz[g][p][:, s, gate, mine]
                                return e.matmul(dst, weights.hidden[0:rows, wp, GATES * (2 * g + j) + gate, :], rhs,
                                                start=False, stop=False, skip_group_check=True)

                            e.wait_ge(hi_ready[g], q + 1)
                            for gate in range(GATES):
                                for j in range(2):
                                    add(gate, 0, 0, j)
                                    add(gate, 1, 0, j)
                            e.wait_ge(lo_ready[g], q + 1)
                            for gate in (2, 0, 1):
                                for j in range(2):
                                    last = add(gate, 0, 1, j)
                            last.then_inc(gates_summed[g], 1)
                            due = round((s + (AFTER_0 if g == 0 else 1)) * len(ahead) / STEPS)
                            for product in ahead[sent:due]:
                                run(product)
                            sent = due
                    for s in (*hi_ready, *lo_ready):
                        e.sem_inc(s, -RING)


def gru_output(nc, layer, stream, gate, history, w_out, w_loaded, out_dram):
    with ExitStack() as ctx:
        sb = lambda n, shape, dt=F32: ctx.enter_context(nc.sbuf_tensor(f"{layer}o_{n}", shape, dt))
        sem = lambda n: ctx.enter_context(nc.semaphore(f"{layer}o_{n}"))
        NB = TOKENS // BANK
        y = sb("y", [C, CHUNKS, SEQ, BATCH])
        s_tok = sb("s_tok", [C, CHUNKS, BATCH, SEQ])
        summed, silu_done, gated, projected, added, stored = (sem("summed"), sem("silu_done"), sem("gated"),
                                                             sem("projected"), sem("added"), sem("stored"))
        banks = [ctx.enter_context(nc.psum_tensor(f"{layer}o_bank{i}", [P, BANK], F32)) for i in range(NB)]
        hist = history[:].rearrange("p t g (j b) -> p t g j b", b=BATCH)
        mates = [((0, 0), (1, 1)), ((0, 1), (1, 0))]
        with nc.Block() as block:

            @block.vector
            def _(e):
                for m in range(CHUNKS):
                    (g0, j0), (g1, j1) = mates[m]
                    e.tensor_tensor(y[:, m], hist[:, :, g0, j0, :], hist[:, SEQ - 1::-1, g1, j1, :], ALU.add).then_inc(summed, 1)
                for m in range(CHUNKS):
                    for h in range(2):
                        t = slice(h * P, (h + 1) * P)
                        e.wait_ge(silu_done, 2 * m + h + 1)
                        e.tensor_tensor(s_tok[:, m].rearrange("p b t -> p t b")[:, t, :], y[:, m, t, :],
                                        gate[:, m, h * P * BATCH:(h + 1) * P * BATCH].rearrange("p (t b) -> p t b", b=BATCH),
                                        ALU.mult).then_inc(gated, 1)
                for k in range(NB):
                    e.wait_ge(projected, k + 1)
                    e.tensor_tensor(stream[:, 4 * k:4 * k + 4, :], stream[:, 4 * k:4 * k + 4, :],
                                    banks[k][:, 0:4 * C].rearrange("p (t c) -> p t c", c=C), ALU.add).then_inc(added, 1)

            @block.scalar
            def _(e):
                for m in range(CHUNKS):
                    e.wait_ge(summed, m + 1)
                    for h in range(2):
                        part = y[:, m, h * P:(h + 1) * P, :]
                        e.activation(part, part, ACT.Silu).then_inc(silu_done, 1)

            @block.tensor
            def _(e):
                e.wait_ge(w_loaded, 16)
                e.wait_ge(gated, 2 * CHUNKS)
                for k in range(NB):
                    for t in range(4):
                        b, half = divmod(4 * k + t, HALVES)
                        for m in range(CHUNKS):
                            last = e.matmul(banks[k][:, t * C:(t + 1) * C], s_tok[:, m, b, half * P:(half + 1) * P], w_out[:, m, :],
                                            start=(m == 0), stop=(m == CHUNKS - 1))
                    last.then_inc(projected, 1)

            if out_dram is not None:
                @block.sync
                def _(e):
                    for k in range(NB):
                        e.wait_ge(added, k + 1)
                        e.dma_start(out_dram[:, 4 * k:4 * k + 4, :], stream[:, 4 * k:4 * k + 4, :]).then_inc(stored, 16)
                    e.wait_ge(stored, 16 * NB)


def build(nc, d, out):
    with ExitStack() as ctx:
        stream = ctx.enter_context(nc.sbuf_tensor("stream", [P, TILES, C], F32))
        ident = ctx.enter_context(nc.sbuf_tensor("ident", [P, P], F32))
        coef = ctx.enter_context(nc.sbuf_tensor("coef", [C, CHUNKS, 2, LAGS], F32))
        loaded_x = ctx.enter_context(nc.semaphore("loaded_x"))
        with nc.Block() as block:

            @block.sync
            def _(e):
                e.dma_start(ident[:], d["ident"]).then_inc(loaded_x, 16)
                e.dma_start(stream[:], d["x"].rearrange("(t p) c -> p t c", p=P)).then_inc(loaded_x, 16)

        coefficients(nc, d, coef, ident, loaded_x, 32)
        fourier(nc, d, stream, ident, loaded_x, 32)
        weights = [GruWeights(nc, ctx, layer) for layer in ("L2", "L3")]
        toeplitz(nc, d, stream, ident, coef, weights)
        gru_layer(nc, d, "L2", stream, ident, weights[0])
        gru_layer(nc, d, "L3", stream, ident, weights[1], out.rearrange("(t p) c -> p t c", p=P))


def constants():
    h, w = np.divmod(np.arange(SEQ), SIDE)
    kh, kw = np.divmod(np.arange(FREQS), KW)
    turns = ((np.outer(h, kh) + np.outer(w, kw)) % SIDE) * (2 * np.pi / SIDE)
    dft = np.stack([np.cos(turns), -np.sin(turns)], axis=2) / SIDE
    dft = dft.reshape(HALVES, P, 2 * FREQS).transpose(1, 0, 2)
    twice = np.where((kw == 0) | (kw == SIDE // 2), 1.0, 2.0)
    idft = np.stack([np.cos(turns) * twice, -np.sin(turns) * twice], axis=2) / SIDE
    idft = idft.reshape(HALVES, P, QUARTERS, FQ, 2).transpose(3, 2, 4, 0, 1)
    mask = np.kron(np.eye(BLOCKS), np.ones((BLOCK, 1)))
    pos = np.arange(1 - SIDE, SIDE).reshape(1, LAGS)
    return {
        "dft": dft, "idft": idft.reshape(FQ, QUARTERS * 2 * HALVES, P), "mask": mask, "pos": pos,
        "ident": np.eye(P),
    }


def layouts(i):
    f = lambda n: np.asarray(i[n])
    by_part = lambda v: v.reshape(-1, C).T
    d = {"x": f("x").reshape(TOKENS, C)}
    d["L0_w1"] = f("L0_conv_w1").transpose(2, 3, 0, 1, 4, 5).reshape(C, FREQS * COMPLEX)
    b1 = f("L0_conv_b1").reshape(QUARTERS, FQ, BLOCKS, COMPLEX).transpose(0, 3, 1, 2)
    bias = np.zeros((QUARTERS, 32, FQ, BLOCKS), b1.dtype)
    bias[:, :COMPLEX] = b1
    d["L0_b1"] = bias.reshape(P, FQ * BLOCKS)
    d["L0_norm1"] = np.stack([f("L0_conv_norm1_w"), f("L0_conv_norm1_b")], axis=1)
    d["L0_norm2"] = np.stack([f("L0_conv_norm2_w"), f("L0_conv_norm2_b")], axis=1)
    d["L0_mlp_w1"] = f("L0_conv_mlp_w1")
    d["L0_mlp_b1"] = f("L0_conv_mlp_b1").reshape(-1, P).T
    d["L0_mlp_w2"] = f("L0_conv_mlp_w2").reshape(-1, P, C).transpose(1, 0, 2)
    d["L0_mlp_b2"] = np.broadcast_to(f("L0_conv_mlp_b2"), (P, C))
    d["L1_w_uv"] = np.stack([f("L1_conv_Wu"), f("L1_conv_Wv")], axis=1)
    d["L1_b_uv"] = np.stack([by_part(f("L1_conv_bu")), by_part(f("L1_conv_bv"))], axis=1)
    d["L1_w_o"] = f("L1_conv_Wo").reshape(CHUNKS, C, C).transpose(1, 0, 2)
    d["L1_b_o"] = np.broadcast_to(f("L1_conv_bo"), (P, C))
    nets = ("r2", "r1")
    g = lambda r, n: f(f"L1_conv_{r}_{n}")
    d["rpe_rows"] = np.stack([np.concatenate([g(r, "pw"), g(r, "pb")[None], g(r, "lb")]) for r in nets])[None]
    d["rpe_lw"] = np.stack([g(r, "lw").transpose(1, 0, 2).reshape(RPE, -1) for r in nets], axis=1)
    d["rpe_ow"] = np.stack([g(r, "ow") for r in nets], axis=1)
    d["rpe_ob"] = np.stack([by_part(g(r, "ob")) for r in nets], axis=1)
    for layer in ("L2", "L3"):
        w = lambda gru, n: f(f"{layer}_conv_" + gru % n)
        n = len(GRUS)
        whh = np.zeros((C + 1, n, GATES, P), np.float32)
        wih = np.zeros((C + 1, CHUNKS, n, GATES, P), np.float32)
        for k, gru in enumerate(GRUS):
            whh[:C, k, :, :C] = w(gru, "whh").reshape(GATES, C, C).transpose(2, 0, 1)
            whh[C, k, :, :C] = w(gru, "bhh").reshape(GATES, C)
            wih[:C, :, k, :, :C] = w(gru, "wih").reshape(GATES, C, CHUNKS, C).transpose(3, 2, 0, 1)
            wih[C, 1, k, :, :C] = w(gru, "bih").reshape(GATES, C)
        d[f"{layer}_whh"] = whh.reshape(C + 1, n * GATES, P)
        d[f"{layer}_wih"] = wih.reshape(C + 1, CHUNKS, n * GATES, P)
        d[f"{layer}_w_in"] = f(f"{layer}_conv_w_in").T
        d[f"{layer}_w_out"] = f(f"{layer}_conv_w_out").reshape(C, CHUNKS, C).transpose(2, 1, 0)
        d[f"{layer}_ln"] = np.stack([f(f"{layer}_conv_ln_g"), f(f"{layer}_conv_ln_b")], axis=1)
    return d


def kernel(**inputs):
    import concourse.bacc as bacc
    from concourse.bass_utils import run_bass_kernel_spmd

    nc = bacc.Bacc("TRN2", target_bir_lowering=False, num_devices=1)
    arrays = {n: np.ascontiguousarray(a) for n, a in layouts(inputs).items()}
    arrays |= {n: np.ascontiguousarray(a, np.float32) for n, a in constants().items()}
    dram = {n: nc.dram_tensor(f"in_{n}", list(a.shape), F32, kind="ExternalInput").ap() for n, a in arrays.items()}
    out = nc.dram_tensor("out", [TOKENS, C], F32, kind="ExternalOutput").ap()
    build(nc, dram, out)
    r = run_bass_kernel_spmd(nc, [{f"in_{n}": a for n, a in arrays.items()}], core_ids=[0])
    return r.results[0]["out"].reshape(BATCH, SIDE, SIDE, C)
```

```python
from contextlib import ExitStack

import numpy as np

import concourse.bass as bass
from concourse import mybir

F32 = mybir.dt.float32
F16 = mybir.dt.float16
ALU = mybir.AluOpType
ACT = mybir.ActivationFunctionType

P = 128
BATCH, SIDE, C = 8, 16, 96
SEQ = SIDE * SIDE
TOKENS = BATCH * SEQ
TILES = TOKENS // P
X_PARTS = 2
HALVES = SEQ // P
BANK = 512

KW = SIDE // 2 + 1
FREQS = SIDE * KW
BLOCKS = 8
BLOCK = C // BLOCKS
QUARTERS = 4
FQ = FREQS // QUARTERS
STACKED = 64 + FQ
COMPLEX = 2 * BLOCK
HIDDEN = 4 * C

CHUNKS = 2
D1 = CHUNKS * C
LAGS = 2 * SIDE - 1
RPE = 128
DEPTH = 3

GRUS = ("f_%s_fw", "b_%s_rv", "f_%s_rv", "b_%s_fw")
GATES = 3
STEPS = 8
SAVE = 16
RING = 32
GROUPS = 2
AFTER_0 = 0.7
PER = 2 * BATCH


def flat(ap):
    return ap.rearrange("p a b -> p (a b)")


def split_tokens(ap):
    return ap.rearrange("p (b t) -> p b t", b=BATCH)


class Norm:

    def __init__(self, nc, ctx, name, stream, out, eps, stats, centred=True):
        sb = lambda n, shape: ctx.enter_context(nc.sbuf_tensor(f"{name}_{n}", shape, F32))
        sem = lambda n: ctx.enter_context(nc.semaphore(f"{name}_{n}"))
        self.stream, self.out, self.eps, self.centred = stream, out, eps, centred
        self.stats = stats
        self.moments = sb("moments", [P, TILES, 2])
        self.power = sb("power", [P, TILES])
        self.root = sb("root", [P, TILES])
        self.warm = sb("warm", [P, 1])
        self.guess = sb("guess", [P, TILES])
        self.work = sb("work", [P, TILES])
        self.rstd = sb("rstd", [P, TILES])
        self.chained = sem("chained")
        self.power_ready = sem("power_ready")
        self.root_ready = sem("root_ready")
        self.rows_ready = sem("rows_ready")


def norm_vector(e, n):
    count = 0

    def link(ins):
        nonlocal count
        count += 1
        ins.then_inc(n.chained, 1)
        e.wait_ge(n.chained, count)

    e.memset(n.warm[:], 1.0).then_inc(n.power_ready, 1)
    for i in range(TILES):
        last = e.bn_aggr(n.moments[:, i, :], n.stats[:, i, :])
    link(last)
    if n.centred:
        e.tensor_scalar(n.power[:], n.moments[:, :, 1], n.eps, None, ALU.add).then_inc(n.power_ready, 1)
    else:
        link(e.tensor_tensor(n.work[:], n.moments[:, :, 0], n.moments[:, :, 0], ALU.mult))
        e.scalar_tensor_tensor(out=n.power[:], in0=n.moments[:, :, 1], scalar=n.eps, in1=n.work[:],
                               op0=ALU.add, op1=ALU.add).then_inc(n.power_ready, 1)
    e.wait_ge(n.root_ready, 1)
    link(e.reciprocal(n.guess[:], n.root[:]))
    link(e.tensor_tensor(n.work[:], n.guess[:], n.guess[:], ALU.mult))
    link(e.scalar_tensor_tensor(out=n.work[:], in0=n.work[:], scalar=-0.5, in1=n.power[:], op0=ALU.mult, op1=ALU.mult))
    link(e.scalar_tensor_tensor(out=n.rstd[:], in0=n.work[:], scalar=1.5, in1=n.guess[:], op0=ALU.add, op1=ALU.mult))
    for i in range(TILES):
        row = n.stream[:, i, :]
        if n.centred:
            ins = e.tensor_scalar(n.out[:, i, :], row, n.moments[:, i, 0:1], n.rstd[:, i:i + 1],
                                  ALU.subtract, ALU.mult)
        else:
            ins = e.tensor_scalar(n.out[:, i, :], row, n.rstd[:, i:i + 1], None, ALU.mult)
        ins.then_inc(n.rows_ready, 1)


def early_stats(e, stats, rows, tiles, written, count):
    e.wait_ge(written, count)
    for i in tiles:
        last = e.bn_stats(stats[:, i, :], rows[:, i, :])
    return last


def norm_scalar(e, n):
    e.wait_ge(n.power_ready, 1)
    e.activation(n.warm[:], n.warm[:], ACT.Sqrt)
    e.wait_ge(n.power_ready, 2)
    e.activation(n.root[:], n.power[:], ACT.Sqrt).then_inc(n.root_ready, 1)


def transposes(e, n, ident, banks, turned):
    for i in range(TILES):
        e.wait_ge(n.rows_ready, i + 1)
        e.transpose(banks[i // 4][0:C, (i % 4) * P:(i % 4 + 1) * P], n.out[:, i, :], ident[:]).then_inc(turned, 1)


def fourier(nc, d, stream, ident, coef, loaded_x, ident_loaded, stats):
    with ExitStack() as ctx:
        rows, spatial, residual = (ctx.enter_context(nc.sbuf_tensor("l0_" + n, [P, TILES, C], F32))
                                   for n in ("rows", "spatial", "residual"))
        banks = [ctx.enter_context(nc.psum_tensor(f"l0_bank{i}", [P, BANK], F32)) for i in range(8)]
        mix_frequencies(nc, d, stream, ident, coef, loaded_x, ident_loaded, rows, spatial, residual, banks, stats)
        mlp(nc, d, stream, spatial, residual, rows, banks, ident, stats)


def mix_frequencies(nc, d, stream, ident, coef, loaded_x, ident_loaded, rows, spatial, residual, banks, stats):
    with ExitStack() as ctx:
        sb = lambda n, shape, dt=F32: ctx.enter_context(nc.sbuf_tensor("l0_" + n, shape, dt))
        sem = lambda n: ctx.enter_context(nc.semaphore("l0_" + n))
        w_raw = sb("w_raw", [C, FREQS * COMPLEX])
        w_for = [sb("w_for_re", [C, FREQS, 32]), sb("w_for_im", [C, FREQS, 32])]
        bias = sb("bias", [P, FQ * BLOCKS])
        dft = sb("dft", [P, HALVES, 2 * FREQS])
        idft = sb("idft", [STACKED, 2 * 2 * HALVES, P])
        mask = sb("mask", [C, BLOCKS])
        affine = sb("affine", [C, 2])
        spectrum = sb("spectrum", [C, 2 * FREQS, BATCH])
        spread = sb("spread", [C, 2 * FREQS, BLOCKS, BATCH])
        mixed = sb("mixed", [P, BLOCKS * BATCH, FQ])
        by_freq = sb("by_freq", [STACKED, BATCH, BLOCKS, 2 * COMPLEX])
        shift0 = sb("shift0", [C, 1])
        loaded = sem("loaded")
        w_loaded = sem("w_loaded")
        chained = sem("chained")
        w_ready = sem("w_ready")
        w_steps = sem("w_steps")
        transformed = sem("transformed")
        evacuated = sem("evacuated")
        shifted = sem("shifted")
        spread_ready = sem("spread_ready")
        spread_ready_s = sem("spread_ready_s")
        products = sem("products")
        biased = sem("biased")
        relu_done = sem("relu_done")
        turned = sem("turned")
        turn_saved_v = sem("turn_saved_v")
        turn_saved_s = sem("turn_saved_s")
        inverted = sem("inverted")
        residual_ready = sem("residual_ready")
        spatial_ready = sem("spatial_ready")
        stats_ready = sem("stats_ready")
        norm = Norm(nc, ctx, "l0n", stream, rows, 1e-5, stats)
        PRODUCT_BANKS = -(-FQ // 8)
        CUTS = (0, 8, 20, FQ)
        SPREADS = len(CUTS) - 1

        def share(buffer, part):
            dims = "n b" if buffer is spread else "b"
            return buffer[:].rearrange(f"p (j f) {dims} -> p j f {dims}", j=QUARTERS)[:, :, 2 * CUTS[part]:2 * CUTS[part + 1]]

        rpe = Coefficients(nc, ctx, coef, ident, banks[PRODUCT_BANKS:])
        with nc.Block() as block:

            @block.sync
            def _(e):
                e.dma_start(dft[:], d["dft"]).then_inc(loaded, 16)
                e.dma_start(mask[:], d["mask"]).then_inc(loaded, 16)
                e.dma_start(affine[:], d["L0_norm1"]).then_inc(loaded, 16)
                e.dma_start(w_raw[:], d["L0_w1"]).then_inc(w_loaded, 16)
                e.dma_start(bias[:], d["L0_b1"]).then_inc(w_loaded, 16)
                rpe.load(e, d)
                e.dma_start(idft[:], d["idft"]).then_inc(w_loaded, 16)

            @block.gpsimd
            def _(e):
                e.memset(by_freq[:], 0.0).then_inc(w_ready, 1)
                for w in w_for:
                    e.memset(w[:, :, COMPLEX:32], 0.0).then_inc(w_ready, 1)
                rpe.guesses(e)

            @block.vector
            def _(e):
                rpe.prepare(e)
                for h in range(X_PARTS):
                    last = early_stats(e, stats, stream, range(h * TILES // X_PARTS, (h + 1) * TILES // X_PARTS), loaded_x[h], 16)
                last.then_inc(stats_ready, 1)
                e.wait_ge(stats_ready, 1)
                norm_vector(e, norm)
                e.wait_ge(loaded, 48)
                e.tensor_scalar(shift0[:], affine[:, 1:2], float(SIDE), None, ALU.mult).then_inc(chained, 1)
                e.wait_ge(evacuated, BATCH)
                e.wait_ge(chained, 1)
                e.tensor_scalar(spectrum[:, 0, :], spectrum[:, 0, :], shift0[:], None, ALU.add).then_inc(shifted, 1)
                e.wait_ge(shifted, 1)
                for part in range(SPREADS):
                    for n in range(0, BLOCKS, 2):
                        e.tensor_scalar(share(spread, part)[:, :, :, n, :], share(spectrum, part), mask[:, n:n + 1], None,
                                        ALU.mult).then_inc(spread_ready, 1)
                bias_v = bias[:].rearrange("p (f n) -> p f n", n=BLOCKS)
                for k in range(PRODUCT_BANKS):
                    if k <= DEPTH:
                        rpe.normalise(e, k)
                        rpe.turned_copy(e, k)
                    f0, f1 = 8 * k, min(FQ, 8 * k + 8)
                    e.wait_ge(products, k + 1)
                    for f in range(f0, f1):
                        ins = e.tensor_tensor(
                            mixed[:, :, f].rearrange("p (n b) -> p n b", b=BATCH),
                            banks[k][:, (f - f0) * 64:(f - f0 + 1) * 64].rearrange("p (n b) -> p n b", b=BATCH),
                            bias_v[:, f, :].unsqueeze(2).to_broadcast([P, BLOCKS, BATCH]), ALU.add)
                    ins.then_inc(biased, 1)
                rpe.finish(e)
                for m in range(0, 16, 2):
                    e.wait_ge(turned, m + 1)
                    n, b0 = m // 2, 4 * (m % 2)
                    for pair in range(2):
                        src = banks[m % 8][0:FQ, :].rearrange("p (b j m) -> p b j m", b=4, j=QUARTERS)
                        dst = by_freq[64 * pair:64 * pair + FQ, b0:b0 + 4, n, :].rearrange("p b (j m) -> p b j m", j=2)
                        src = src[:, :, 2 * pair:2 * pair + 2, 0:COMPLEX]
                        e.tensor_copy(dst, src).then_inc(turn_saved_v, 1)
                for g in range(4):
                    half, pair = g // 2, g % 2
                    e.wait_ge(inverted, g + 1)
                    src = banks[g][:, 0:4 * C].rearrange("p (b c) -> p b c", b=4)
                    dst = spatial[:].rearrange("p (b s) c -> p s b c", s=HALVES)[:, half, 4 * pair:4 * pair + 4, :]
                    e.tensor_copy(dst, src).then_inc(spatial_ready, 1)
                    early_stats(e, stats, spatial, [HALVES * b + half for b in range(4 * pair, 4 * pair + 4)], spatial_ready, g + 1)
                e.tensor_tensor(residual[:], spatial[:], stream[:], ALU.add).then_inc(residual_ready, 1)
                e.wait_ge(residual_ready, 1)

            @block.scalar
            def _(e):
                norm_scalar(e, norm)
                e.wait_ge(w_loaded, 48)
                raw = w_raw[:].rearrange("p (f o r) -> p f o r", o=BLOCK, r=2)
                pair = [w[:, :, 0:COMPLEX].rearrange("p f (o r) -> p f o r", r=2) for w in w_for]
                e.activation(w_for[0][:, :, 0:COMPLEX], w_raw[:].rearrange("p (f m) -> p f m", m=COMPLEX),
                             ACT.Copy).then_inc(w_ready, 1)
                e.activation(pair[1][:, :, :, 1], raw[:, :, :, 0], ACT.Copy).then_inc(w_ready, 1)
                e.activation(pair[1][:, :, :, 0], raw[:, :, :, 1], ACT.Copy, scale=-1.0).then_inc(w_ready, 1)
                e.wait_ge(loaded, 48)
                for b in range(BATCH):
                    e.wait_ge(transformed, b + 1)
                    e.activation(spectrum[:, :, b], banks[b][0:C, 0:2 * FREQS], ACT.Copy, scale=affine[:, 0:1])\
                        .then_inc(evacuated, 1)
                e.wait_ge(shifted, 1)
                for part in range(SPREADS):
                    for n in range(1, BLOCKS, 2):
                        e.activation(share(spread, part)[:, :, :, n, :], share(spectrum, part), ACT.Copy, scale=mask[:, n:n + 1])\
                            .then_inc(spread_ready_s, 1)
                e.wait_ge(biased, PRODUCT_BANKS)
                for n in range(BLOCKS):
                    part = mixed[:, n * BATCH:(n + 1) * BATCH, :]
                    e.activation(part, part, ACT.Relu).then_inc(relu_done, 1)
                for m in range(1, 16, 2):
                    e.wait_ge(turned, m + 1)
                    n, b0 = m // 2, 4 * (m % 2)
                    for pair in range(2):
                        src = banks[m % 8][0:FQ, :].rearrange("p (b j m) -> p b j m", b=4, j=QUARTERS)
                        dst = by_freq[64 * pair:64 * pair + FQ, b0:b0 + 4, n, :].rearrange("p b (j m) -> p b j m", j=2)
                        src = src[:, :, 2 * pair:2 * pair + 2, 0:COMPLEX]
                        e.activation(dst, src, ACT.Copy).then_inc(turn_saved_s, 1)

            @block.tensor
            def _(e):
                e.wait_ge(loaded, 48)
                e.wait_ge(ident_loaded, 16)
                for b in range(BATCH):
                    for half in range(HALVES):
                        tile = HALVES * b + half
                        e.wait_ge(norm.rows_ready, tile + 1)
                        last = e.matmul(banks[b][0:C, 0:2 * FREQS], rows[:, tile, :], dft[:, half, :],
                                        start=(half == 0), stop=(half == HALVES - 1))
                    last.then_inc(transformed, 1)
                e.wait_ge(w_ready, 6)
                for f in range(FQ):
                    k, f8 = divmod(f, 8)
                    for part in range(SPREADS):
                        if f == CUTS[part]:
                            e.wait_ge(spread_ready, BLOCKS // 2 * (part + 1))
                            e.wait_ge(spread_ready_s, BLOCKS // 2 * (part + 1))
                    if f8 == 0 and k <= DEPTH:
                        rpe.layer(e, k)
                    if f8 == 5 and k <= DEPTH:
                        rpe.turn(e, k)
                    if f == FQ - 1:
                        rpe.output(e)
                    for part in range(2):
                        for j in range(QUARTERS):
                            freq = j * FQ + f
                            last = e.matmul(banks[k][32 * j:32 * j + 32, f8 * 64:(f8 + 1) * 64],
                                            w_for[part][:, freq, :], flat(spread[:, 2 * freq + part, :, :]),
                                            start=(part == 0), stop=(part == 1), skip_group_check=True)
                    if f8 == 7 or f == FQ - 1:
                        last.then_inc(products, 1)
                e.wait_ge(rpe.finished, 1)
                for m in range(16):
                    n, b0 = m // 2, 4 * (m % 2)
                    e.wait_ge(relu_done, n + 1)
                    if m >= 8:
                        e.wait_ge(turn_saved_v if m % 2 == 0 else turn_saved_s, 2 * ((m - 8) // 2 + 1))
                    for b in range(4):
                        last = e.transpose(banks[m % 8][0:FQ, b * P:(b + 1) * P], mixed[:, n * BATCH + b0 + b, :], ident[:])
                    last.then_inc(turned, 1)
                e.wait_ge(turn_saved_v, 16)
                e.wait_ge(turn_saved_s, 16)
                for g in range(4):
                    half, pair = g // 2, g % 2
                    out = banks[g][:, 0:4 * C].rearrange("p (b n o) -> p b n o", b=4, n=BLOCKS)
                    for k in range(4):
                        j, part = divmod(k, 2)
                        rhs = by_freq[:, 4 * pair:4 * pair + 4, :, j * COMPLEX + part:(j + 1) * COMPLEX:2]
                        last = e.matmul(out, idft[:, k * HALVES + half, :], rhs, start=(k == 0), stop=(k == 3))
                    last.then_inc(inverted, 1)


def mlp(nc, d, stream, spatial, residual, rows, banks, ident, stats):
    with ExitStack() as ctx:
        sb = lambda n, shape, dt=F32: ctx.enter_context(nc.sbuf_tensor("mlp_" + n, shape, dt))
        sem = lambda n: ctx.enter_context(nc.semaphore("mlp_" + n))
        KH = HIDDEN // P
        NB = TOKENS // BANK
        w1, w2 = sb("w1", [C, HIDDEN]), sb("w2", [P, KH, C])
        b1, b2, affine = sb("b1", [P, KH]), sb("b2", [P, C]), sb("affine", [C, 2])
        xT = sb("xT", [C, TOKENS])
        hidden = sb("hidden", [P, 2, KH, BANK])
        loaded, turned, scaled = sem("loaded"), sem("turned"), sem("scaled")
        up, activated, down, added, base = sem("up"), sem("activated"), sem("down"), sem("added"), sem("base")
        norm = Norm(nc, ctx, "mlpn", spatial, rows, 1e-5, stats)
        with nc.Block() as block:

            @block.sync
            def _(e):
                for dst, name in ((w1, "L0_mlp_w1"), (w2, "L0_mlp_w2"), (b1, "L0_mlp_b1"), (b2, "L0_mlp_b2"), (affine, "L0_norm2")):
                    e.dma_start(dst[:], d[name]).then_inc(loaded, 16)

            @block.gpsimd
            def _(e):
                e.wait_ge(loaded, 80)
                e.tensor_tensor(residual[:], residual[:], b2[:].unsqueeze(1).to_broadcast([P, TILES, C]), ALU.add)\
                    .then_inc(base, 1)

            @block.vector
            def _(e):
                norm_vector(e, norm)
                e.wait_ge(base, 1)
                for k in range(NB):
                    e.wait_ge(down, k + 1)
                    e.tensor_tensor(stream[:, 4 * k:4 * k + 4, :], residual[:, 4 * k:4 * k + 4, :],
                                    banks[6 + k % 2][:, 0:4 * C].rearrange("p (t c) -> p t c", c=C), ALU.add)\
                        .then_inc(added, 1)
                    early_stats(e, stats, stream, range(4 * k, 4 * k + 4), added, k + 1)

            @block.scalar
            def _(e):
                norm_scalar(e, norm)
                e.wait_ge(loaded, 80)
                for k in range(NB):
                    e.wait_ge(turned, 4 * k + 4)
                    e.activation(xT[:, k * BANK:(k + 1) * BANK], banks[k][0:C, :], ACT.Identity,
                                 scale=affine[:, 0:1], bias=affine[:, 1:2]).then_inc(scaled, 1)
                for k in range(NB):
                    if k >= 2:
                        e.wait_ge(down, k - 1)
                    for m in range(KH):
                        e.wait_ge(up, k * KH + m + 1)
                        e.activation(hidden[:, k % 2, m, :], banks[(k * KH + m) % 6][:], ACT.Gelu,
                                     bias=b1[:, m:m + 1]).then_inc(activated, 1)

            @block.tensor
            def _(e):
                transposes(e, norm, ident, banks, turned)
                e.wait_ge(scaled, NB)
                for k in range(NB + 1):
                    if k < NB:
                        for m in range(KH):
                            n = k * KH + m
                            if n >= 6:
                                e.wait_ge(activated, n - 5)
                            e.matmul(banks[n % 6][:], w1[:, m * P:(m + 1) * P], xT[:, k * BANK:(k + 1) * BANK],
                                     start=True, stop=True).then_inc(up, 1)
                    if k >= 1:
                        q = k - 1
                        e.wait_ge(activated, KH * k)
                        if q >= 2:
                            e.wait_ge(added, q - 1)
                        for t in range(4):
                            for m in range(KH):
                                last = e.matmul(banks[6 + q % 2][:, t * C:(t + 1) * C],
                                                hidden[:, q % 2, m, t * P:(t + 1) * P], w2[:, m, :],
                                                start=(m == 0), stop=(m == KH - 1))
                        last.then_inc(down, 1)


class Coefficients:

    def __init__(self, nc, ctx, coef, ident, banks):
        sb = lambda n, shape, dt=F32: ctx.enter_context(nc.sbuf_tensor("rpe_" + n, shape, dt))
        sem = lambda n: ctx.enter_context(nc.semaphore("rpe_" + n))
        self.coef, self.ident = coef, ident
        self.pos = sb("pos", [1, LAGS])
        self.ones = sb("ones", [1, LAGS])
        self.rows = sb("rows", [1, 2, 2 + DEPTH, RPE])
        self.lw = sb("lw", [RPE, 2, DEPTH * RPE])
        self.ow = sb("ow", [RPE, 2, D1])
        self.ob = sb("ob", [C, 2, CHUNKS])
        self.x = sb("x", [LAGS, 2, RPE])
        self.stats = sb("stats", [LAGS, 2, 6])
        self.moments = sb("moments", [LAGS, 2, 2])
        self.power, self.guess, self.work, self.exponent = (sb("power", [LAGS, 2]), sb("guess", [LAGS, 2]),
                                                            sb("work", [LAGS, 2]), sb("exponent", [LAGS, 2]))
        self.y = sb("y", [LAGS, 2, RPE])
        self.y_turned = sb("y_turned", [RPE, 2, LAGS])
        self.layer_bank = banks[0][0:LAGS, 0:2 * RPE].rearrange("p (a f) -> p a f", a=2)
        self.turn_bank = banks[1][0:RPE, 0:2 * LAGS].rearrange("p (a f) -> p a f", a=2)
        self.out_bank = banks[2][0:C, 0:CHUNKS * 2 * LAGS].rearrange("p (m a f) -> p m a f", m=CHUNKS, a=2)
        self.loaded, self.chained, self.product = sem("loaded"), sem("chained"), sem("product")
        self.power_ready, self.guessed, self.y_ready = sem("power_ready"), sem("guessed"), sem("y_ready")
        self.turned, self.y_saved = sem("turned"), sem("y_saved")
        self.finished = sem("finished")
        self.links = 0

    def load(self, e, d):
        for dst, name in ((self.pos, "pos"), (self.rows, "rpe_rows"), (self.lw, "rpe_lw"), (self.ow, "rpe_ow"), (self.ob, "rpe_ob")):
            e.dma_start(dst[:], d[name]).then_inc(self.loaded, 16)

    def layer(self, e, i):
        if i == 0:
            e.wait_ge(self.loaded, 80)
            e.wait_ge(self.chained, 1)
        else:
            e.wait_ge(self.y_saved, i)
        for a in range(2):
            if i == 0:
                e.matmul(self.layer_bank[:, a, :], self.pos[:], self.rows[:, a, 0, :], start=True, stop=False)
            else:
                e.matmul(self.layer_bank[:, a, :], self.y_turned[:, a, :], self.lw[:, a, (i - 1) * RPE:i * RPE],
                         start=True, stop=False)
            e.matmul(self.layer_bank[:, a, :], self.ones[:], self.rows[:, a, 1 + i, :], start=False, stop=True)\
                .then_inc(self.product, 1)

    def turn(self, e, i):
        e.wait_ge(self.y_ready, 2 * i + 2)
        for a in range(2):
            e.transpose(self.turn_bank[:, a, :], self.y[:, a, :], self.ident[0:LAGS, 0:LAGS]).then_inc(self.turned, 1)

    def output(self, e):
        e.wait_ge(self.y_saved, DEPTH + 1)
        for a in range(2):
            for m in range(CHUNKS):
                e.matmul(self.out_bank[:, m, a, :], self.ow[:, a, m * C:(m + 1) * C], self.y_turned[:, a, :],
                         start=True, stop=True).then_inc(self.product, 1)

    def guesses(self, e):
        for i in range(DEPTH + 1):
            e.wait_ge(self.power_ready, i + 2)
            e.tensor_tensor(self.guess[:], self.power[:], self.exponent[:], ALU.pow).then_inc(self.guessed, 1)

    def link(self, e, ins):
        self.links += 1
        ins.then_inc(self.chained, 1)
        e.wait_ge(self.chained, self.links)

    def prepare(self, e):
        self.link(e, e.memset(self.ones[:], 1.0))
        e.memset(self.exponent[:], -0.5).then_inc(self.power_ready, 1)

    def normalise(self, e, i):
        x, power, guess, work, moments = self.x, self.power, self.guess, self.work, self.moments
        e.wait_ge(self.product, 2 * i + 2)
        if i == 0:
            self.link(e, e.tensor_scalar(x[:], self.layer_bank, 0.0, None, ALU.max))
        else:
            self.link(e, e.tensor_copy(x[:], self.layer_bank))
        for a in range(2):
            last = e.bn_stats(self.stats[:, a, :], x[:, a, :])
        self.link(e, last)
        for a in range(2):
            last = e.bn_aggr(moments[:, a, :], self.stats[:, a, :])
        self.link(e, last)
        self.link(e, e.tensor_tensor(work[:], moments[:, :, 0], moments[:, :, 0], ALU.mult))
        e.scalar_tensor_tensor(out=power[:], in0=moments[:, :, 1], scalar=1e-6, in1=work[:],
                               op0=ALU.add, op1=ALU.add).then_inc(self.power_ready, 1)
        e.wait_ge(self.guessed, i + 1)
        self.link(e, e.tensor_tensor(work[:], guess[:], guess[:], ALU.mult))
        self.link(e, e.tensor_tensor(work[:], work[:], power[:], ALU.mult))
        self.link(e, e.tensor_scalar(work[:], work[:], -0.5, 1.5, ALU.mult, ALU.add))
        self.link(e, e.tensor_tensor(work[:], work[:], guess[:], ALU.mult))
        for a in range(2):
            e.tensor_scalar(self.y[:, a, :], x[:, a, :], 0.0, work[:, a:a + 1], ALU.max, ALU.mult).then_inc(self.y_ready, 1)

    def turned_copy(self, e, i):
        e.wait_ge(self.turned, 2 * i + 2)
        e.tensor_copy(self.y_turned[:], self.turn_bank).then_inc(self.y_saved, 1)

    def finish(self, e):
        e.wait_ge(self.product, 2 * DEPTH + 2 + 2 * CHUNKS)
        e.tensor_tensor(self.coef[:], self.out_bank, self.ob[:].rearrange("p a m -> p m a").unsqueeze(3)
                        .to_broadcast([C, CHUNKS, 2, LAGS]), ALU.add).then_inc(self.finished, 1)


PE_LAGS = [(axis, lag) for axis, lags in ((0, range(-5, 5)), (1, range(-4, 4))) for lag in lags]
PE_LAGS.sort(key=lambda al: al != (0, 0))
DVE_LAGS = [(axis, lag) for axis in range(2) for lag in sorted(range(1 - SIDE, SIDE), key=abs) if (axis, lag) not in PE_LAGS]


def shifted(v, axis, lag):
    n = SIDE - abs(lag)
    to, of = (slice(lag, SIDE), slice(0, n)) if lag >= 0 else (slice(0, n), slice(-lag, SIDE))
    return to, of


def toeplitz(nc, d, stream, ident, coef, weights, stats):
    with ExitStack() as ctx:
        sb = lambda n, shape, dt=F32: ctx.enter_context(nc.sbuf_tensor("l1_" + n, shape, dt))
        sem = lambda n: ctx.enter_context(nc.semaphore("l1_" + n))
        NB = TOKENS // BANK
        NDIAG = 4
        rows = sb("rows", [P, TILES, C])
        xT = sb("xT", [C, TOKENS])
        w_uv, b_uv = sb("w_uv", [C, 2, D1]), sb("b_uv", [C, 2, CHUNKS])
        w_o, b_o = sb("w_o", [C, CHUNKS, C]), sb("b_o", [P, C])
        u, v = sb("u", [C, CHUNKS, TOKENS]), sb("v", [C, CHUNKS, TOKENS])
        acc = sb("acc", [C, CHUNKS, TOKENS])
        v_hi, v_lo = sb("v_hi", [C, CHUNKS, TOKENS], F16), sb("v_lo", [C, CHUNKS, TOKENS], F16)
        diag = sb("diag", [C, NDIAG, 2, P], F16)
        coef_half = sb("coef_half", [C, CHUNKS, 2, LAGS], F16)
        coef_parts = sb("coef_parts", [C, 2, CHUNKS, 2, LAGS])
        v_hi_ready, v_lo_ready, coef_split = sem("v_hi_ready"), sem("v_lo_ready"), sem("coef_split")
        base = sb("base", [P, TILES, C])
        loaded, turned, copied = sem("loaded"), sem("turned"), sem("copied")
        uv_done, u_ready = sem("uv_done"), sem("u_ready")
        diag_ready, diag_used, conv_done = sem("diag_ready"), sem("diag_used"), sem("conv_done")
        acc_step = [sem(f"acc_step{m}") for m in range(CHUNKS)]
        summed, gated, projected, added, based = sem("summed"), sem("gated"), sem("projected"), sem("added"), sem("based")
        norm = Norm(nc, ctx, "l1n", stream, rows, 1e-6, stats, centred=False)
        splits = [WeightSplit(nc, ctx, w) for w in weights]
        banks = [ctx.enter_context(nc.psum_tensor(f"l1_bank{i}", [P, BANK], F32)) for i in range(8)]

        with nc.Block() as block:

            @block.sync
            def _(e):
                for dst, name in ((w_uv, "L1_w_uv"), (b_uv, "L1_b_uv"), (w_o, "L1_w_o"), (b_o, "L1_b_o")):
                    e.dma_start(dst[:], d[name]).then_inc(loaded, 16)
                for split in splits:
                    split.load(e, d)

            @block.gpsimd
            def _(e):
                e.wait_ge(loaded, 64)
                e.tensor_tensor(base[:], stream[:], b_o[:].unsqueeze(1).to_broadcast([P, TILES, C]), ALU.add)\
                    .then_inc(based, 1)
                e.tensor_copy(coef_half[:], coef[:]).then_inc(coef_split, 1)
                e.wait_ge(coef_split, 1)
                e.tensor_copy(coef_parts[:, 0], coef_half[:]).then_inc(coef_split, 1)
                e.wait_ge(coef_split, 2)
                e.tensor_tensor(coef_parts[:, 1], coef[:], coef_parts[:, 0], ALU.subtract).then_inc(coef_split, 1)
                e.wait_ge(coef_split, 3)
                for m in range(CHUNKS):
                    for i, (axis, lag) in enumerate(PE_LAGS):
                        n = m * len(PE_LAGS) + i
                        if n >= NDIAG:
                            e.wait_ge(diag_used, n - NDIAG + 1)
                        at = lag + SIDE - 1
                        for part in range(2):
                            e.tensor_scalar(diag[:, n % NDIAG, part, :], ident[0:C, :], coef_parts[:, part, m, axis, at:at + 1],
                                            None, ALU.mult).then_inc(diag_ready, 1)
                for split in splits:
                    split.lo(e)

            @block.vector
            def _(e):
                norm_vector(e, norm)
                def rest_of_v(m):
                    e.wait_ge(v_hi_ready, NB * (m + 1))
                    e.tensor_tensor(v_lo[:, m, :], v[:, m, :], v_hi[:, m, :], ALU.subtract).then_inc(v_lo_ready, 1)

                def add_lag(m, i):
                    axis, lag = DVE_LAGS[i]
                    at = lag + SIDE - 1
                    to, of = shifted(v, axis, lag)
                    if axis == 0:
                        row = lambda s, t: t[:, m, :].rearrange("p (b r) -> p b r", b=BATCH)[:, :, s.start * SIDE:s.stop * SIDE]
                    else:
                        row = lambda s, t: t[:, m, :].rearrange("p (b r) -> p b r", r=SIDE)[:, :, s]
                    e.wait_ge(acc_step[m], i + 1)
                    e.scalar_tensor_tensor(out=row(to, acc), in0=row(of, v), scalar=coef[:, m, axis, at:at + 1],
                                           in1=row(to, acc), op0=ALU.mult, op1=ALU.add).then_inc(acc_step[m], 1)

                for m in range(CHUNKS):
                    e.memset(acc[:, m, :], 0.0).then_inc(acc_step[m], 1)
                rest_of_v(0)
                LEAD, COUNT = 6, len(DVE_LAGS)
                for i in range(COUNT + LEAD):
                    if i < COUNT:
                        add_lag(0, i)
                    if i == LEAD - 1:
                        rest_of_v(1)
                    if i >= LEAD:
                        add_lag(1, i - LEAD)
                for m in range(CHUNKS):
                    e.wait_ge(acc_step[m], COUNT + 1)
                for k in range(NB):
                    cols = slice(k * BANK, (k + 1) * BANK)
                    for m in range(CHUNKS):
                        e.wait_ge(conv_done, m + 1)
                        e.tensor_tensor(acc[:, m, cols], acc[:, m, cols], banks[4 * m + k][0:C, :], ALU.add)\
                            .then_inc(summed, 1)
                    for m in range(CHUNKS):
                        e.wait_ge(summed, CHUNKS * k + m + 1)
                        e.wait_ge(u_ready, NB * m + k + 1)
                        e.tensor_tensor(v[:, m, cols], acc[:, m, cols], u[:, m, cols], ALU.mult).then_inc(gated, 1)
                e.wait_ge(based, 1)
                for k in range(NB):
                    e.wait_ge(projected, k + 1)
                    e.tensor_tensor(stream[:, 4 * k:4 * k + 4, :], base[:, 4 * k:4 * k + 4, :],
                                    banks[k][:, 0:4 * C].rearrange("p (t c) -> p t c", c=C), ALU.add)\
                        .then_inc(added, 1)
                    early_stats(e, stats, stream, range(4 * k, 4 * k + 4), added, k + 1)

            @block.scalar
            def _(e):
                norm_scalar(e, norm)
                for k in range(NB):
                    e.wait_ge(turned, 4 * k + 4)
                    e.activation(xT[:, k * BANK:(k + 1) * BANK], banks[k][0:C, :], ACT.Copy).then_inc(copied, 1)
                e.wait_ge(loaded, 64)
                n = 0
                for uv in (1, 0):
                    for m in range(CHUNKS):
                        for k in range(NB):
                            n += 1
                            e.wait_ge(uv_done, n)
                            src, cols = banks[4 + (n - 1) % 4][0:C, :], slice(k * BANK, (k + 1) * BANK)
                            bias = b_uv[:, uv, m:m + 1]
                            if uv == 0:
                                e.activation(u[:, m, cols], src, ACT.Silu, bias=bias).then_inc(u_ready, 1)
                            else:
                                e.activation(v[:, m, cols], src, ACT.Silu, bias=bias)
                                e.activation(v_hi[:, m, cols], src, ACT.Silu, bias=bias).then_inc(v_hi_ready, 1)
                for split in splits:
                    split.hi(e)

            @block.tensor
            def _(e):
                transposes(e, norm, ident, banks, turned)
                e.wait_ge(loaded, 64)
                e.wait_ge(copied, NB)
                n = 0
                for uv in (1, 0):
                    for m in range(CHUNKS):
                        for k in range(NB):
                            if n >= 4:
                                done = n - 3
                                e.wait_ge(v_hi_ready, min(done, CHUNKS * NB))
                                if done > CHUNKS * NB:
                                    e.wait_ge(u_ready, done - CHUNKS * NB)
                            e.matmul(banks[4 + n % 4][0:C, :], w_uv[:, uv, m * C:(m + 1) * C],
                                     xT[:, k * BANK:(k + 1) * BANK], start=True, stop=True).then_inc(uv_done, 1)
                            n += 1
                e.wait_ge(v_hi_ready, CHUNKS * NB)
                e.wait_ge(u_ready, CHUNKS * NB)
                for m in range(CHUNKS):
                    for i, (axis, lag) in enumerate(PE_LAGS):
                        to, of = shifted(v, axis, lag)
                        if axis == 0:
                            row = lambda s, t: t.rearrange("p (b r) -> p b r", b=2)[:, :, s.start * SIDE:s.stop * SIDE]
                        else:
                            row = lambda s, t: t.rearrange("p (b r) -> p b r", r=SIDE)[:, :, s]
                        for step, (part, source) in enumerate(((0, v_hi), (1, v_hi), (0, v_lo))):
                            e.wait_ge(diag_ready, 2 * (m * len(PE_LAGS) + i) + 1 + (step > 0))
                            if i == 0 and step == 2:
                                e.wait_ge(v_lo_ready, m + 1)
                            for k in range(NB):
                                src = source[:, m, k * BANK:(k + 1) * BANK]
                                last = e.matmul(row(to, banks[4 * m + k][:]), diag[:, (m * len(PE_LAGS) + i) % NDIAG, part, :],
                                                row(of, src), start=(i == 0 and step == 0),
                                                stop=(i == len(PE_LAGS) - 1 and step == 2))
                        last.then_inc(diag_used, 1)
                    e.wait_ge(diag_used, (m + 1) * len(PE_LAGS))
                    e.sem_inc(conv_done, 1)
                for k in range(NB):
                    e.wait_ge(gated, CHUNKS * (k + 1))
                    for t in range(4):
                        tile = 4 * k + t
                        for m in range(CHUNKS):
                            last = e.matmul(banks[k][:, t * C:(t + 1) * C], v[:, m, tile * P:(tile + 1) * P], w_o[:, m, :],
                                            start=(m == 0), stop=(m == CHUNKS - 1))
                    last.then_inc(projected, 1)


class GruWeights:

    def __init__(self, nc, ctx, layer):
        n = len(GRUS) * GATES
        self.layer = layer
        self.hidden = ctx.enter_context(nc.sbuf_tensor(f"{layer}_w_hidden", [C + 1, 2, n, P], F16))
        self.input = ctx.enter_context(nc.sbuf_tensor(f"{layer}_w_input", [C + 1, 2, CHUNKS, n, P], F16))


class WeightSplit:

    def __init__(self, nc, ctx, weights):
        n = len(GRUS) * GATES
        layer = weights.layer
        hidden_raw = ctx.enter_context(nc.sbuf_tensor(f"{layer}_w_hidden_raw", [C + 1, n, P], F32))
        input_raw = ctx.enter_context(nc.sbuf_tensor(f"{layer}_w_input_raw", [C + 1, CHUNKS, n, P], F32))
        self.raw = ((hidden_raw, f"{layer}_whh", weights.hidden), (input_raw, f"{layer}_wih", weights.input))
        self.loaded = ctx.enter_context(nc.semaphore(f"{layer}_w_raw_loaded"))
        self.hi_ready = ctx.enter_context(nc.semaphore(f"{layer}_w_hi_ready"))
        self.lo_ready = ctx.enter_context(nc.semaphore(f"{layer}_w_lo_ready"))

    def load(self, e, d):
        for raw, name, _ in self.raw:
            e.dma_start(raw[:], d[name]).then_inc(self.loaded, 16)

    def hi(self, e):
        e.wait_ge(self.loaded, 32)
        for raw, _, parts in self.raw:
            e.activation(parts[:, 0], raw[:], ACT.Copy).then_inc(self.hi_ready, 1)

    def lo(self, e):
        for i, (raw, _, parts) in enumerate(self.raw):
            e.wait_ge(self.hi_ready, i + 1)
            e.tensor_tensor(parts[:, 1], raw[:], parts[:, 0], ALU.subtract).then_inc(self.lo_ready, 1)


def gru_layer(nc, d, layer, stream, ident, weights, stats, out_dram=None):
    with ExitStack() as outer:
        sbo = lambda n, shape, dt=F32: outer.enter_context(nc.sbuf_tensor(f"{layer}_{n}", shape, dt))
        gate = sbo("gate", [C, CHUNKS, TOKENS])
        history = sbo("history", [C, SEQ, GROUPS, PER])
        w_out = sbo("w_out", [C, CHUNKS, C])
        w_loaded = outer.enter_context(nc.semaphore(f"{layer}_w_loaded"))
        with ExitStack() as ctx:
            sb = lambda n, shape, dt=F32: ctx.enter_context(nc.sbuf_tensor(f"{layer}_{n}", shape, dt))
            forward = sb("forward", [C + 1, 2, CHUNKS, SEQ + STEPS, BATCH], F16)
            backward = sb("backward", [C + 1, 2, CHUNKS, SEQ + STEPS, BATCH], F16)
            gru_input(nc, d, layer, stream, ident, forward, backward, gate, w_out, w_loaded, stats)
            gru_steps(nc, layer, weights, forward, backward, history)
        gru_output(nc, layer, stream, gate, history, w_out, w_loaded, stats, out_dram)


def gru_input(nc, d, layer, stream, ident, forward, backward, gate, w_out, w_loaded, stats):
    with ExitStack() as ctx:
        sb = lambda n, shape, dt=F32: ctx.enter_context(nc.sbuf_tensor(f"{layer}i_{n}", shape, dt))
        sem = lambda n: ctx.enter_context(nc.semaphore(f"{layer}i_{n}"))
        NB = TOKENS // BANK
        TB = BANK // BATCH
        rows = sb("rows", [P, TILES, C])
        xT = sb("xT", [C, SEQ, BATCH])
        w_in = sb("w_in", [C, 2 * D1])
        affine = sb("affine", [C, 2])
        loaded, turned, scaled, projected = sem("loaded"), sem("turned"), sem("scaled"), sem("projected")
        hi_ready, lo_ready, gate_ready, filled, reversed_ = (sem("hi_ready"), sem("lo_ready"), sem("gate_ready"),
                                                                    sem("filled"), sem("reversed"))
        norm = Norm(nc, ctx, f"{layer}n", stream, rows, 1e-5, stats)
        banks = [ctx.enter_context(nc.psum_tensor(f"{layer}i_bank{i}", [P, BANK], F32)) for i in range(8)]
        order = [(m, k) for m in range(CHUNKS) for k in range(NB)] + [(CHUNKS + m, k) for m in range(CHUNKS) for k in range(NB)]
        INNER = CHUNKS * NB
        with nc.Block() as block:

            @block.sync
            def _(e):
                e.dma_start(w_in[:], d[f"{layer}_w_in"]).then_inc(loaded, 16)
                e.dma_start(affine[:], d[f"{layer}_ln"]).then_inc(loaded, 16)
                e.dma_start(w_out[:], d[f"{layer}_w_out"]).then_inc(w_loaded, 16)

            @block.gpsimd
            def _(e):
                for i, x in enumerate((forward, backward)):
                    for part in range(2):
                        e.memset(x[0:C, part, :, SEQ:, :], 0.0).then_inc(filled, 1)
                        e.wait_ge(filled, 4 * i + 2 * part + 1)
                        e.memset(x[C:C + 1, part, 1, :, :], 1.0 - part).then_inc(filled, 1)
                        e.wait_ge(filled, 4 * i + 2 * part + 2)

            @block.vector
            def _(e):
                norm_vector(e, norm)
                for i, (m, k) in enumerate(order[:INNER]):
                    cols = slice(k * TB, (k + 1) * TB)
                    e.wait_ge(hi_ready, i + 1)
                    e.tensor_tensor(forward[0:C, 1, m, cols, :], banks[4 + i % 4][0:C, :].rearrange("p (t b) -> p t b", b=BATCH),
                                    forward[0:C, 0, m, cols, :], ALU.subtract).then_inc(lo_ready, 1)
                e.wait_ge(lo_ready, INNER)
                for part in range(2):
                    for m in range(CHUNKS):
                        e.tensor_copy(backward[0:C, part, m, 0:SEQ, :], forward[0:C, part, m, SEQ - 1::-1, :]).then_inc(reversed_, 1)

            @block.scalar
            def _(e):
                norm_scalar(e, norm)
                e.wait_ge(loaded, 32)
                for k in range(NB):
                    e.wait_ge(turned, 4 * k + 4)
                    e.activation(xT[:].rearrange("p t b -> p b t")[:, 2 * k:2 * k + 2, :],
                                 banks[k][0:C, :].rearrange("p (b t) -> p b t", b=2), ACT.Identity,
                                 scale=affine[:, 0:1], bias=affine[:, 1:2]).then_inc(scaled, 1)
                for i, (m, k) in enumerate(order):
                    e.wait_ge(projected, i + 1)
                    src = banks[4 + i % 4][0:C, :]
                    if m < CHUNKS:
                        e.activation(forward[0:C, 0, m, k * TB:(k + 1) * TB, :], src.rearrange("p (t b) -> p t b", b=BATCH),
                                     ACT.Copy).then_inc(hi_ready, 1)
                    else:
                        e.activation(gate[:, m - CHUNKS, k * BANK:(k + 1) * BANK], src, ACT.Silu).then_inc(gate_ready, 1)

            @block.tensor
            def _(e):
                transposes(e, norm, ident, banks, turned)
                e.wait_ge(loaded, 32)
                e.wait_ge(scaled, NB)
                x_all = flat(xT[:])
                for i, (m, k) in enumerate(order):
                    if i >= 4:
                        done = i - 3
                        e.wait_ge(lo_ready, min(done, INNER))
                        if done > INNER:
                            e.wait_ge(gate_ready, done - INNER)
                    e.matmul(banks[4 + i % 4][0:C, :], w_in[:, m * C:(m + 1) * C], x_all[:, k * BANK:(k + 1) * BANK],
                             start=True, stop=True).then_inc(projected, 1)


def gru_steps(nc, layer, weights, forward, backward, history):
    with ExitStack() as ctx:
        sb = lambda n, shape, dt=F32: ctx.enter_context(nc.sbuf_tensor(f"{layer}s_{n}", shape, dt))
        sem = lambda n: ctx.enter_context(nc.semaphore(f"{layer}s_{n}"))
        pairs = lambda n, shape, dt=F32: [sb(f"{n}{g}", shape, dt) for g in range(GROUPS)]
        each = lambda n: [sem(f"{n}{g}") for g in range(GROUPS)]
        reset = pairs("reset", [C, 2, PER, 2])
        cand = pairs("cand", [C, 2, PER, 2])
        keep = pairs("keep", [C, 2, PER])
        renew = pairs("renew", [C, 2, PER, 2])
        terms = pairs("terms", [C, 2, PER, 2])
        states = pairs("states", [C, RING, PER, 2])
        h_hi = pairs("h_hi", [C + 1, 2, PER, 2], F16)
        h_lo = pairs("h_lo", [C, 2, PER], F16)
        early = [[ctx.enter_context(nc.psum_tensor(f"{layer}s_early{g}{p}", [P, 4, STEPS, PER], F32)) for p in range(2)] for g in range(GROUPS)]
        late = [[ctx.enter_context(nc.psum_tensor(f"{layer}s_late{g}{p}", [P, 4, STEPS, PER], F32)) for p in range(2)] for g in range(GROUPS)]
        reset_sum = lambda g, p: early[g][p][:, 0]
        cand_sum = lambda g, p: early[g][p][:, 1:3].rearrange("p a s c -> p (a s c)").rearrange("p (s c k) -> p s c k", c=PER, k=2)
        keep_sum = lambda g, p: late[g][p][:, 0]
        warm = sb("warm", [C, 1])
        prepared = sem("prepared")
        reset_summed, keep_summed = each("reset_summed"), each("keep_summed")
        activated, cand_ready = each("activated"), each("cand_ready")
        updated, hi_ready, lo_ready = each("updated"), each("hi_ready"), each("lo_ready")
        chunk_done, chunk_saved, ring_free = sem("chunk_done"), sem("chunk_saved"), sem("ring_free")
        PREPARED = 1 + 7 * GROUPS
        TURNS = SEQ // RING
        PARTS = RING // SAVE

        with nc.Block() as block:

            @block.vector
            def _(e):
                e.memset(warm[:], 0.0).then_inc(prepared, 1)
                for g in range(GROUPS):
                    for buffer in (reset[g], renew[g], terms[g], h_lo[g]):
                        e.memset(buffer[:], 0.0).then_inc(prepared, 1)
                    e.memset(states[g][:, RING - 1], 0.0).then_inc(prepared, 1)
                    e.memset(h_hi[g][0:C], 0.0).then_inc(prepared, 1)
                    e.memset(h_hi[g][C:C + 1], 1.0).then_inc(prepared, 1)
                e.wait_ge(prepared, PREPARED)
                for s, n in ((updated[1], 2), (hi_ready[0], 1), (hi_ready[1], 1), (lo_ready[0], 1)):
                    e.sem_inc(s, n)
                BEFORE = (0, 2)

                def candidate(g, q):
                    p, s = q // STEPS % 2, q % STEPS
                    x = q % 2
                    e.wait_ge(activated[g], 3 * q + 1)
                    e.tensor_tensor_scan(flat(cand[g][:, x]), flat(reset[g][:, x]), flat(cand_sum(g, p)[0:C, s]), 0.0,
                                         ALU.mult, ALU.add).then_inc(cand_ready[g], 1)

                def kept_part(g, q):
                    x = q % 2
                    e.wait_ge(activated[g], 3 * q + 2)
                    e.tensor_tensor(terms[g][:, x, :, 1], keep[g][:, x], states[g][:, (q - 1) % RING, :, 1], ALU.mult)\
                        .then_inc(updated[g], 1)

                def new_state(g, q):
                    x = q % 2
                    e.wait_ge(activated[g], 3 * q + 3)
                    e.wait_ge(updated[g], 2 * q + 1 + BEFORE[g])
                    e.tensor_tensor_scan(flat(h_hi[g][0:C, x]), flat(renew[g][:, x]), flat(terms[g][:, x]), 0.0,
                                         ALU.mult, ALU.add).then_inc(hi_ready[g], 1)
                    e.tensor_tensor_scan(flat(states[g][:, q % RING]), flat(renew[g][:, x]), flat(terms[g][:, x]), 0.0,
                                         ALU.mult, ALU.add).then_inc(updated[g], 1)
                    if q == RING - 1:
                        e.sem_inc(activated[g], -3 * RING)

                def rest(g, q):
                    e.wait_ge(updated[g], 2 * q + 2 + BEFORE[g])
                    e.tensor_tensor(h_lo[g][:, q % 2], states[g][:, q % RING, :, 1], h_hi[g][0:C, q % 2, :, 1],
                                    ALU.subtract).then_inc(lo_ready[g], 1)

                with e.Fori(0, TURNS):
                    for q in range(RING):
                        if q % SAVE == 0:
                            e.wait_ge(ring_free, q // SAVE + 1)
                        if q == RING - SAVE:
                            e.sem_inc(ring_free, -PARTS)
                        candidate(0, q)
                        rest(1, q - 1)
                        kept_part(0, q)
                        if q % SAVE == 0:
                            e.sem_inc(chunk_done, 1)
                        new_state(0, q)
                        rest(0, q)
                        candidate(1, q)
                        kept_part(1, q)
                        new_state(1, q)
                        if q == RING - 1:
                            for g in range(GROUPS):
                                e.sem_inc(updated[g], -2 * RING)
                e.wait_ge(updated[1], BEFORE[1])
                for g in range(GROUPS):
                    e.tensor_copy(history[:, SEQ - SAVE:, g, :], states[g][:, RING - SAVE:, :, 1])

            @block.scalar
            def _(e):
                e.wait_ge(prepared, 1)
                e.activation(warm[:], warm[:], ACT.Sigmoid)
                e.wait_ge(prepared, PREPARED)
                with e.Fori(0, TURNS):
                    for q in range(RING):
                        p, s = q // STEPS % 2, q % STEPS
                        x = q % 2
                        for g in range(GROUPS):
                            e.wait_ge(reset_summed[g], q + 1)
                            e.activation(reset[g][:, x, :, 1], reset_sum(g, p)[0:C, s], ACT.Sigmoid).then_inc(activated[g], 1)
                            e.wait_ge(keep_summed[g], q + 1)
                            e.activation(keep[g][:, x], keep_sum(g, p)[0:C, s], ACT.Sigmoid).then_inc(activated[g], 1)
                            e.activation(renew[g][:, x, :, 1], keep_sum(g, p)[0:C, s], ACT.Sigmoid, scale=-1.0)
                            if q == RING - 1:
                                e.sem_inc(reset_summed[g], -RING)
                                e.sem_inc(keep_summed[g], -RING)
                            e.wait_ge(cand_ready[g], q + 1)
                            e.activation(terms[g][:, x, :, 0], cand[g][:, x, :, 1], ACT.Tanh).then_inc(activated[g], 1)
                            if q == RING - 1:
                                e.sem_inc(cand_ready[g], -RING)

            @block.gpsimd
            def _(e):
                def save(chunk, part, to):
                    e.wait_ge(chunk_done, chunk + 2)
                    for g in range(GROUPS):
                        last = e.tensor_copy(history[:, to, g, :], states[g][:, part * SAVE:(part + 1) * SAVE, :, 1])
                    last.then_inc(chunk_saved, 1)
                    e.wait_ge(chunk_saved, chunk + 1)
                    e.sem_inc(ring_free, 1)

                e.sem_inc(ring_free, PARTS)
                save(0, 0, slice(0, SAVE))
                with e.Fori(0, TURNS - 1) as turn:
                    for p in range(PARTS):
                        chunk = turn * PARTS + (p + 1)
                        save(chunk, (p + 1) % PARTS, bass.ds(chunk * SAVE, SAVE))
                for p in range(1, PARTS - 1):
                    chunk = (TURNS - 1) * PARTS + p
                    save(chunk, p, slice(chunk * SAVE, (chunk + 1) * SAVE))

            @block.tensor
            def _(e):
                def inputs(p, chunk):
                    out = []
                    cols = bass.ds(chunk * (STEPS * BATCH), STEPS * BATCH)
                    for gru in range(len(GRUS)):
                        g, j = divmod(gru, 2)
                        source = forward if gru < 2 else backward
                        mine = slice(j * BATCH, (j + 1) * BATCH)

                        def share(dst, gate, first):
                            for m in range(CHUNKS):
                                rows = C + 1 if m else C
                                for wp, xp in ((0, 0), (1, 0), (0, 1)):
                                    lhsT = weights.input[0:rows, wp, m, GATES * gru + gate, :]
                                    rhs = source[0:rows, xp, m].rearrange("p t b -> p (t b)")[:, cols]
                                    start = first and m == 0 and (wp, xp) == (0, 0)
                                    out.append((dst, lhsT, rhs, start))

                        share(reset_sum(g, p)[:, :, mine], 0, j == 0)
                        share(cand_sum(g, p)[:, :, mine, 1], 2, False)
                        share(keep_sum(g, p)[:, :, mine], 1, j == 0)
                    return out

                def run(product):
                    dst, lhsT, rhs, start = product
                    return e.matmul(dst, lhsT, rhs, start=start, stop=False, skip_group_check=True)

                for product in inputs(0, 0):
                    run(product)
                e.wait_ge(prepared, PREPARED)
                with e.Fori(0, TURNS) as turn:
                    for q in range(RING):
                        p, s = q // STEPS % 2, q % STEPS
                        x = (q + 1) % 2
                        if s == 0:
                            ahead = inputs(1 - p, turn * (RING // STEPS) + (q // STEPS + 1))
                            sent = 0
                        for g in range(GROUPS):
                            def add(gate, wp, xp, j):
                                mine = slice(j * BATCH, (j + 1) * BATCH)
                                rows = C if xp else C + 1
                                rhs = h_lo[g][:, x, mine] if xp else h_hi[g][:, x, mine, 1]
                                dst = (reset_sum(g, p)[:, s, mine], keep_sum(g, p)[:, s, mine], cand_sum(g, p)[:, s, mine, 0])[gate]
                                return e.matmul(dst, weights.hidden[0:rows, wp, GATES * (2 * g + j) + gate, :], rhs,
                                                start=False, stop=False, skip_group_check=True)

                            e.wait_ge(hi_ready[g], q + 1)
                            for gate in (2, 0, 1):
                                for j in range(2):
                                    add(gate, 0, 0, j)
                                    add(gate, 1, 0, j)
                            e.wait_ge(lo_ready[g], q + 1)
                            for gate in (2, 0, 1):
                                for j in range(2):
                                    last = add(gate, 0, 1, j)
                                if gate == 0:
                                    last.then_inc(reset_summed[g], 1)
                            last.then_inc(keep_summed[g], 1)
                            if q == RING - 1:
                                e.sem_inc(hi_ready[g], -RING)
                                e.sem_inc(lo_ready[g], -RING)
                            due = round((s + (AFTER_0 if g == 0 else 1)) * len(ahead) / STEPS)
                            for product in ahead[sent:due]:
                                run(product)
                            sent = due


def gru_output(nc, layer, stream, gate, history, w_out, w_loaded, stats, out_dram):
    with ExitStack() as ctx:
        sb = lambda n, shape, dt=F32: ctx.enter_context(nc.sbuf_tensor(f"{layer}o_{n}", shape, dt))
        sem = lambda n: ctx.enter_context(nc.semaphore(f"{layer}o_{n}"))
        NB = TOKENS // BANK
        y = sb("y", [C, CHUNKS, SEQ, BATCH])
        s_tok = sb("s_tok", [C, CHUNKS, BATCH, SEQ])
        summed, silu_done, gated, projected, added, stored = (sem("summed"), sem("silu_done"), sem("gated"),
                                                             sem("projected"), sem("added"), sem("stored"))
        banks = [ctx.enter_context(nc.psum_tensor(f"{layer}o_bank{i}", [P, BANK], F32)) for i in range(NB)]
        hist = history[:].rearrange("p t g (j b) -> p t g j b", b=BATCH)
        mates = [((0, 0), (1, 1)), ((0, 1), (1, 0))]
        half_of = lambda h: slice(h * P, (h + 1) * P)

        def tiles_of(rows, k):
            first = 8 * (k % 2) + k // 2
            return rows[:, first:first + 2 * 4 - 1:2, :]

        with nc.Block() as block:

            @block.vector
            def _(e):
                def add_directions(h, m):
                    (g0, j0), (g1, j1) = mates[m]
                    mirrored = hist[:, SEQ - 1::-1, g1, j1, :]
                    e.tensor_tensor(y[:, m, half_of(h)], hist[:, half_of(h), g0, j0, :], mirrored[:, half_of(h)],
                                    ALU.add).then_inc(summed, 1)

                def apply_gate(h, m):
                    e.wait_ge(silu_done, 2 * h + m + 1)
                    e.tensor_tensor(s_tok[:, m].rearrange("p b t -> p t b")[:, half_of(h), :], y[:, m, half_of(h), :],
                                    gate[:, m, h * P * BATCH:(h + 1) * P * BATCH].rearrange("p (t b) -> p t b", b=BATCH),
                                    ALU.mult).then_inc(gated, 1)

                add_directions(0, 0)
                add_directions(0, 1)
                apply_gate(0, 0)
                apply_gate(0, 1)
                add_directions(1, 0)
                add_directions(1, 1)
                apply_gate(1, 0)
                apply_gate(1, 1)
                for k in range(NB):
                    e.wait_ge(projected, k + 1)
                    mine = tiles_of(stream, k)
                    e.tensor_tensor(mine, mine, banks[k][:, 0:4 * C].rearrange("p (t c) -> p t c", c=C), ALU.add).then_inc(added, 1)
                    if out_dram is None:
                        first = 8 * (k % 2) + k // 2
                        early_stats(e, stats, stream, range(first, first + 8, 2), added, k + 1)

            @block.scalar
            def _(e):
                for h in range(2):
                    for m in range(CHUNKS):
                        e.wait_ge(summed, 2 * h + m + 1)
                        part = y[:, m, half_of(h), :]
                        e.activation(part, part, ACT.Silu).then_inc(silu_done, 1)

            @block.tensor
            def _(e):
                e.wait_ge(w_loaded, 16)
                for k in range(NB):
                    h = k // 2
                    e.wait_ge(gated, CHUNKS * (h + 1))
                    for t in range(4):
                        for m in range(CHUNKS):
                            last = e.matmul(banks[k][:, t * C:(t + 1) * C], s_tok[:, m, 4 * (k % 2) + t, half_of(h)],
                                            w_out[:, m, :], start=(m == 0), stop=(m == CHUNKS - 1))
                    last.then_inc(projected, 1)

            if out_dram is not None:
                @block.sync
                def _(e):
                    for k in range(NB):
                        e.wait_ge(added, k + 1)
                        e.dma_start(tiles_of(out_dram, k), tiles_of(stream, k)).then_inc(stored, 16)
                    e.wait_ge(stored, 16 * NB)


def build(nc, d, out):
    with ExitStack() as ctx:
        stream = ctx.enter_context(nc.sbuf_tensor("stream", [P, TILES, C], F32))
        ident = ctx.enter_context(nc.sbuf_tensor("ident", [P, P], F32))
        coef = ctx.enter_context(nc.sbuf_tensor("coef", [C, CHUNKS, 2, LAGS], F32))
        loaded_x = [ctx.enter_context(nc.semaphore(f"loaded_x{h}")) for h in range(X_PARTS)]
        ident_loaded = ctx.enter_context(nc.semaphore("ident_loaded"))
        stats = ctx.enter_context(nc.sbuf_tensor("stats", [P, TILES, 6], F32))
        with nc.Block() as block:

            @block.sync
            def _(e):
                x = d["x"].rearrange("(t p) c -> p t c", p=P)
                for h in range(X_PARTS):
                    tiles = slice(h * TILES // X_PARTS, (h + 1) * TILES // X_PARTS)
                    e.dma_start(stream[:, tiles], x[:, tiles]).then_inc(loaded_x[h], 16)
                e.dma_start(ident[:], d["ident"]).then_inc(ident_loaded, 16)

        fourier(nc, d, stream, ident, coef, loaded_x, ident_loaded, stats)
        weights = [GruWeights(nc, ctx, layer) for layer in ("L2", "L3")]
        toeplitz(nc, d, stream, ident, coef, weights, stats)
        gru_layer(nc, d, "L2", stream, ident, weights[0], stats)
        gru_layer(nc, d, "L3", stream, ident, weights[1], stats, out.rearrange("(t p) c -> p t c", p=P))


def constants():
    h, w = np.divmod(np.arange(SEQ), SIDE)
    kh, kw = np.divmod(np.arange(FREQS), KW)
    turns = ((np.outer(h, kh) + np.outer(w, kw)) % SIDE) * (2 * np.pi / SIDE)
    dft = np.stack([np.cos(turns), -np.sin(turns)], axis=2) / SIDE
    dft = dft.reshape(HALVES, P, 2 * FREQS).transpose(1, 0, 2)
    twice = np.where((kw == 0) | (kw == SIDE // 2), 1.0, 2.0)
    idft = np.stack([np.cos(turns) * twice, -np.sin(turns) * twice], axis=2) / SIDE
    idft = idft.reshape(HALVES, P, 2, 2, FQ, 2).transpose(2, 4, 3, 5, 0, 1)
    stacked = np.zeros((STACKED, 2, 2, HALVES, P))
    stacked[:FQ], stacked[64:] = idft
    mask = np.kron(np.eye(BLOCKS), np.ones((BLOCK, 1)))
    pos = np.arange(1 - SIDE, SIDE).reshape(1, LAGS)
    return {
        "dft": dft, "idft": stacked.reshape(STACKED, 2 * 2 * HALVES, P), "mask": mask, "pos": pos,
        "ident": np.eye(P),
    }


def layouts(i):
    f = lambda n: np.asarray(i[n])
    by_part = lambda v: v.reshape(-1, C).T
    d = {"x": f("x").reshape(TOKENS, C)}
    d["L0_w1"] = f("L0_conv_w1").transpose(2, 3, 0, 1, 4, 5).reshape(C, FREQS * COMPLEX)
    b1 = f("L0_conv_b1").reshape(QUARTERS, FQ, BLOCKS, COMPLEX).transpose(0, 3, 1, 2)
    bias = np.zeros((QUARTERS, 32, FQ, BLOCKS), b1.dtype)
    bias[:, :COMPLEX] = b1
    d["L0_b1"] = bias.reshape(P, FQ * BLOCKS)
    d["L0_norm1"] = np.stack([f("L0_conv_norm1_w"), f("L0_conv_norm1_b")], axis=1)
    d["L0_norm2"] = np.stack([f("L0_conv_norm2_w"), f("L0_conv_norm2_b")], axis=1)
    d["L0_mlp_w1"] = f("L0_conv_mlp_w1")
    d["L0_mlp_b1"] = f("L0_conv_mlp_b1").reshape(-1, P).T
    d["L0_mlp_w2"] = f("L0_conv_mlp_w2").reshape(-1, P, C).transpose(1, 0, 2)
    d["L0_mlp_b2"] = np.broadcast_to(f("L0_conv_mlp_b2"), (P, C))
    d["L1_w_uv"] = np.stack([f("L1_conv_Wu"), f("L1_conv_Wv")], axis=1)
    d["L1_b_uv"] = np.stack([by_part(f("L1_conv_bu")), by_part(f("L1_conv_bv"))], axis=1)
    d["L1_w_o"] = f("L1_conv_Wo").reshape(CHUNKS, C, C).transpose(1, 0, 2)
    d["L1_b_o"] = np.broadcast_to(f("L1_conv_bo"), (P, C))
    nets = ("r2", "r1")
    g = lambda r, n: f(f"L1_conv_{r}_{n}")
    d["rpe_rows"] = np.stack([np.concatenate([g(r, "pw"), g(r, "pb")[None], g(r, "lb")]) for r in nets])[None]
    d["rpe_lw"] = np.stack([g(r, "lw").transpose(1, 0, 2).reshape(RPE, -1) for r in nets], axis=1)
    d["rpe_ow"] = np.stack([g(r, "ow") for r in nets], axis=1)
    d["rpe_ob"] = np.stack([by_part(g(r, "ob")) for r in nets], axis=1)
    for layer in ("L2", "L3"):
        w = lambda gru, n: f(f"{layer}_conv_" + gru % n)
        n = len(GRUS)
        whh = np.zeros((C + 1, n, GATES, P), np.float32)
        wih = np.zeros((C + 1, CHUNKS, n, GATES, P), np.float32)
        for k, gru in enumerate(GRUS):
            whh[:C, k, :, :C] = w(gru, "whh").reshape(GATES, C, C).transpose(2, 0, 1)
            whh[C, k, :, :C] = w(gru, "bhh").reshape(GATES, C)
            wih[:C, :, k, :, :C] = w(gru, "wih").reshape(GATES, C, CHUNKS, C).transpose(3, 2, 0, 1)
            wih[C, 1, k, :, :C] = w(gru, "bih").reshape(GATES, C)
        d[f"{layer}_whh"] = whh.reshape(C + 1, n * GATES, P)
        d[f"{layer}_wih"] = wih.reshape(C + 1, CHUNKS, n * GATES, P)
        d[f"{layer}_w_in"] = f(f"{layer}_conv_w_in").T
        d[f"{layer}_w_out"] = f(f"{layer}_conv_w_out").reshape(C, CHUNKS, C).transpose(2, 1, 0)
        d[f"{layer}_ln"] = np.stack([f(f"{layer}_conv_ln_g"), f(f"{layer}_conv_ln_b")], axis=1)
    return d


def kernel(**inputs):
    import concourse.bacc as bacc
    from concourse.bass_utils import run_bass_kernel_spmd

    nc = bacc.Bacc("TRN2", target_bir_lowering=False, num_devices=1)
    arrays = {n: np.ascontiguousarray(a) for n, a in layouts(inputs).items()}
    arrays |= {n: np.ascontiguousarray(a, np.float32) for n, a in constants().items()}
    dram = {n: nc.dram_tensor(f"in_{n}", list(a.shape), F32, kind="ExternalInput").ap() for n, a in arrays.items()}
    out = nc.dram_tensor("out", [TOKENS, C], F32, kind="ExternalOutput").ap()
    build(nc, dram, out)
    r = run_bass_kernel_spmd(nc, [{f"in_{n}": a for n, a in arrays.items()}], core_ids=[0])
    return r.results[0]["out"].reshape(BATCH, SIDE, SIDE, C)
```
